# Optimizing a Trainium2 kernel written in Bass

```python
import numpy as np
import jax
import jax.numpy as jnp

def _softmax(x, axis=-1):
    return jax.nn.softmax(x, axis=axis)

def _gelu(x):
    return jax.nn.gelu(x, approximate=True)

def _silu(x):
    return jax.nn.silu(x)

def _sigmoid(x):
    return jax.nn.sigmoid(x)

def _layernorm(x, axis=-1, eps=1e-05):
    m = jnp.mean(x, axis=axis, keepdims=True)
    v = jnp.var(x, axis=axis, keepdims=True)
    return (x - m) / jnp.sqrt(v + eps)

def _scatter_add(tgt, idx, src, axis=0):
    return tgt.at[idx].add(src)

def _segment_sum(src, seg, n):
    return jax.ops.segment_sum(src, seg, n)
kernel_name = 'mk_adaln_d1_jaxref_r4_ed4272'

def setup_inputs(seed: int=0):
    np.random.seed(seed)
    _w = jnp.asarray

    def _L0_attn_setup():
        import jax, jax.numpy as jnp
        import numpy as np
        from math import log2, ceil
        HEADS, DIM_HEAD, BLOCK, EPS = (16, 64, 16, 1e-08)
        key = jax.random.key(seed)
        k1, k2, k3, k4 = jax.random.split(key, 4)
        b, n, dim = (4, 1024, 256)
        inner = HEADS * DIM_HEAD
        return {'x': jax.random.normal(k1, (b, n, dim), jnp.float32), 'w_qkv': jax.random.normal(k2, (inner * 3, dim), jnp.float32) * 0.02, 'w_out': jax.random.normal(k3, (dim, inner), jnp.float32) * 0.02, 'b_out': jax.random.normal(k4, (dim,), jnp.float32) * 0.02}
    _L0_attn_in = _L0_attn_setup()

    def _L0_ffn_setup():
        import jax, jax.numpy as jnp
        import numpy as np
        D = 256
        F = 704
        E = 8
        TOP_K = 2
        key = jax.random.key(seed)
        ks = jax.random.split(key, 6)
        std = 0.02
        x = jax.random.normal(ks[0], (2, 512, D), dtype=jnp.float32)
        router_w = jax.random.normal(ks[1], (D, E), dtype=jnp.float32) * std
        w1 = jax.random.normal(ks[2], (E, D, F), dtype=jnp.float32) * std
        v1 = jax.random.normal(ks[3], (E, D, F), dtype=jnp.float32) * std
        w2 = jax.random.normal(ks[4], (E, F, D), dtype=jnp.float32) * std
        bias = jnp.zeros((D,), dtype=jnp.float32)
        return {'x': x, 'router_w': router_w, 'w1': w1, 'v1': v1, 'w2': w2, 'bias': bias}
    _L0_ffn_in = _L0_ffn_setup()
    _L0_c = _w((lambda *s: np.random.randn(*s).astype(np.float32) * 0.05)(8, 256))
    _L0_wmod = _w((lambda *s: np.random.randn(*s).astype(np.float32) * 0.05)(256, 6 * 256) * 256 ** (-0.5))
    _d = {'L0_attn_x': _L0_attn_in['x'], 'L0_attn_w_qkv': _L0_attn_in['w_qkv'], 'L0_attn_w_out': _L0_attn_in['w_out'], 'L0_attn_b_out': _L0_attn_in['b_out'], 'L0_ffn_router_w': _L0_ffn_in['router_w'], 'L0_ffn_w1': _L0_ffn_in['w1'], 'L0_ffn_v1': _L0_ffn_in['v1'], 'L0_ffn_w2': _L0_ffn_in['w2'], 'L0_ffn_bias': _L0_ffn_in['bias'], 'L0_c': _L0_c, 'L0_wmod': _L0_wmod}
    _x0 = _d['L0_attn_x']
    _d['L0_attn_x'] = jax.random.normal(jax.random.fold_in(jax.random.key(seed), 1), (8, 512, 256), dtype=_x0.dtype)
    del _x0
    return _d

def reference(L0_attn_x, L0_attn_w_qkv, L0_attn_w_out, L0_attn_b_out, L0_ffn_router_w, L0_ffn_w1, L0_ffn_v1, L0_ffn_w2, L0_ffn_bias, L0_c, L0_wmod):

    def _L0_attn_ref(x, w_qkv, w_out, b_out):
        import jax, jax.numpy as jnp
        import numpy as np
        from math import log2, ceil
        HEADS, DIM_HEAD, BLOCK, EPS = (16, 64, 16, 1e-08)
        b, n, dim = x.shape
        pad_to_len = 2 ** ceil(log2(n))
        if pad_to_len != n:
            x = jnp.pad(x, ((0, 0), (0, pad_to_len - n), (0, 0)))
        qkv = x @ w_qkv.T
        q, k, v = jnp.split(qkv, 3, axis=-1)

        def split_heads(t):
            return t.reshape(b, pad_to_len, HEADS, DIM_HEAD).transpose(0, 2, 1, 3).reshape(b * HEADS, pad_to_len, DIM_HEAD)
        q = split_heads(q) * DIM_HEAD ** (-0.5)
        k = split_heads(k)
        v = split_heads(v)
        num_levels = int(log2(pad_to_len // BLOCK)) - 1
        qkvs = [(q, k, v)]
        for _ in range(num_levels):
            q = q.reshape(q.shape[0], -1, 2, DIM_HEAD).mean(2)
            k = k.reshape(k.shape[0], -1, 2, DIM_HEAD).mean(2)
            v = v.reshape(v.shape[0], -1, 2, DIM_HEAD).sum(2)
            qkvs.append((q, k, v))
        neg_max = -jnp.finfo(x.dtype).max
        idx = jnp.arange(pad_to_len)
        Ysum = jnp.zeros((b * HEADS, pad_to_len, DIM_HEAD), x.dtype)
        Asum = jnp.zeros((b * HEADS, pad_to_len), x.dtype)
        for lvl, (ql, kl, vl) in enumerate(qkvs):
            B = ql.shape[0]
            nb = ql.shape[1] // BLOCK
            ql = ql.reshape(B, nb, BLOCK, DIM_HEAD)
            kl = kl.reshape(B, nb, BLOCK, DIM_HEAD)
            vl = vl.reshape(B, nb, BLOCK, DIM_HEAD)
            if lvl == 0:
                S = jnp.einsum('bnid,bnjd->bnij', ql, kl)
                S = jnp.where(jnp.triu(jnp.ones((BLOCK, BLOCK), bool), 1), neg_max, S)
                S = S - S.max(-1, keepdims=True)
                A = jnp.exp(S)
                y = jnp.einsum('bnij,bnjd->bnid', A, vl).reshape(B, pad_to_len, DIM_HEAD)
                Av = A.sum(-1).reshape(B, pad_to_len)
            else:
                q2 = ql.reshape(B, nb // 2, 2, BLOCK, DIM_HEAD)[:, :, 1]
                k1b = kl.reshape(B, nb // 2, 2, BLOCK, DIM_HEAD)[:, :, 0]
                v1b = vl.reshape(B, nb // 2, 2, BLOCK, DIM_HEAD)[:, :, 0]
                S = jnp.einsum('bnid,bnjd->bnij', q2, k1b)
                S = S - S.max(-1, keepdims=True)
                A = jnp.exp(S)
                y = jnp.einsum('bnij,bnjd->bnid', A, v1b)
                Av = A.sum(-1)
                y = jnp.pad(y[:, :, None], ((0, 0), (0, 0), (1, 0), (0, 0), (0, 0))).reshape(B, -1, DIM_HEAD)
                Av = jnp.pad(Av[:, :, None], ((0, 0), (0, 0), (1, 0), (0, 0))).reshape(B, -1)
                y = jnp.repeat(y, 2 ** lvl, axis=1)
                Av = jnp.repeat(Av, 2 ** lvl, axis=1)
            seq_key = (idx >> lvl << lvl) + (2 ** lvl - 1)
            keep = seq_key <= idx
            Ysum = Ysum + jnp.where(keep[None, :, None], y, 0.0)
            Asum = Asum + jnp.where(keep[None, :], Av, 0.0)
        out = Ysum / (Asum + EPS)[..., None]
        out = out.reshape(b, HEADS, pad_to_len, DIM_HEAD).transpose(0, 2, 1, 3).reshape(b, pad_to_len, HEADS * DIM_HEAD)
        out = out @ w_out.T + b_out
        return out[:, :n]

    def _L0_ffn_ref(x, router_w, w1, v1, w2, bias):
        import jax, jax.numpy as jnp
        import numpy as np
        D = 256
        F = 704
        E = 8
        TOP_K = 2
        B, S, d = x.shape
        xt = x.reshape(B * S, d)
        scores = jax.nn.softmax(xt @ router_w, axis=-1)
        expert_weights, expert_idx = jax.lax.top_k(scores, TOP_K)
        h = jax.nn.gelu(jnp.einsum('td,edf->tef', xt, w1), approximate=False) * jnp.einsum('td,edf->tef', xt, v1)
        y = jnp.einsum('tef,efd->ted', h, w2)
        yk = jnp.take_along_axis(y, expert_idx[:, :, None], axis=1)
        out = jnp.sum(expert_weights[:, :, None] * yk, axis=1) + bias
        return out.reshape(B, S, d)
    x = L0_attn_x
    mod = (_silu(L0_c) @ L0_wmod).reshape(L0_c.shape[0], 6, 1, -1)
    sa, ca, ga, sb, cb, gb = (mod[:, 0], mod[:, 1], mod[:, 2], mod[:, 3], mod[:, 4], mod[:, 5])
    ga = (2 * (ga >= 0) - 1) * jnp.maximum(jnp.abs(ga), 0.25)
    gb = (2 * (gb >= 0) - 1) * jnp.maximum(jnp.abs(gb), 0.25)
    h = _layernorm(x, axis=-1) * (1 + ca) + sa
    x = x + ga * _L0_attn_ref(h, L0_attn_w_qkv, L0_attn_w_out, L0_attn_b_out)
    h = _layernorm(x, axis=-1) * (1 + cb) + sb
    x = x + gb * _L0_ffn_ref(h, L0_ffn_router_w, L0_ffn_w1, L0_ffn_v1, L0_ffn_w2, L0_ffn_bias)
    return x

_drawn_inputs = setup_inputs


def setup_inputs(seed=0):
    import zlib

    import numpy as np

    out = dict(_drawn_inputs(seed))
    spreads = {'L0_ffn_bias': (0.0, 1.112)}
    factors = {'L0_attn_b_out': 8.0,
     'L0_ffn_router_w': 8.0,
     'L0_ffn_w1': 8.0,
     'L0_ffn_v1': 8.0,
     'L0_ffn_w2': 8.0}
    for name, (base, spread) in spreads.items():
        noise = np.random.default_rng([zlib.crc32(name.encode()), seed]).standard_normal(out[name].shape)
        drawn = base * np.exp(spread * noise) if base else spread * noise
        out[name] = jnp.asarray(drawn.astype(out[name].dtype))
    for name, factor in factors.items():
        out[name] = (out[name] * factor).astype(out[name].dtype)
    return out
```

```python
from contextlib import ExitStack

import concourse.bass as bass
from concourse import mybir

F32 = mybir.dt.float32
I32 = mybir.dt.int32
U32 = mybir.dt.uint32
ALU = mybir.AluOpType
ACT = mybir.ActivationFunctionType
AX = mybir.AxisListType

P = 128
BATCH, SEQ, D = 8, 512, 256
KD = D // P
TT = SEQ // P
TOKENS = BATCH * SEQ
HEADS, DH = 16, 64
INNER = HEADS * DH
GROUPS = 4
UNITS = TT + 2
EXPERTS, TOPK, FF = 8, 2, 704
FF2 = 2 * FF
FC = 6
FTAIL = FF - 5 * P
CAP = TOKENS + P
SLOTS = EXPERTS * CAP + P
TILES = 72
LN_EPS, SUM_EPS = 1e-5, 1e-8

C_ID, C_TRI = 0, P
C_M0, C_M1, C_M2 = 2 * P, 2 * P + 32, 2 * P + 64
C_SC2 = 2 * P + 96
C_E8 = C_SC2 + 1
C_CAP = C_E8 + 8
C_TILE = C_CAP + 8
C_PART = C_TILE + TILES
C_END = C_PART + 1

JOBS = 7 * GROUPS + KD


def some(count):
    return not (isinstance(count, int) and count <= 0)


def held(eng, count):
    return count if isinstance(count, int) else eng.to_reg(count)


def job_x(b, k):
    return b * JOBS + k


def job(b, g, i):
    return b * JOBS + (KD + 7 * g + i)


def build(nc, x, cT, wmod, wqkv, wout, b_out, router, w13, w2, ffn_bias, consts, sel, out):
    rows_dram = nc.dram_tensor("mod_rows", [BATCH, 6, D], F32, kind="Internal").ap()
    x2_dram = nc.dram_tensor("x_after_attention", [TOKENS, D], F32, kind="Internal").ap()
    xs_dram = nc.dram_tensor("dispatched_rows", [SLOTS, D], F32, kind="Internal").ap()
    ys_dram = nc.dram_tensor("expert_rows", [TILES * P, D], F32, kind="Internal").ap()

    ctx = ExitStack()
    with ctx:
        def sb(name, shape, dt=F32):
            return ctx.enter_context(nc.sbuf_tensor(name, shape, dt))

        def pb(name, shape):
            return ctx.enter_context(nc.psum_tensor(name, shape, F32))

        def sem(name):
            return ctx.enter_context(nc.semaphore(name))

        cst = sb("cst", [P, C_END])
        sel_sb = sb("sel_sb", [HEADS, 8, P])
        ones = sb("ones", [P, P])
        halfneg = sb("halfneg", [P, TT])
        wqkv_sb = sb("wqkv_sb", [P, KD, 3 * INNER])
        wout_sb = sb("wout_sb", [P, 8, D])
        rout_sb = sb("rout_sb", [P, KD, EXPERTS])
        cT_sb = sb("cT_sb", [P, KD, BATCH])
        sil = sb("sil", [P, KD, BATCH])
        siT = sb("siT", [P, KD, BATCH])
        modT = sb("modT", [P, 2 * KD, BATCH])
        ident = cst[:, C_ID:C_ID + P]
        x_sb = sb("x_sb", [P, TT, D])
        xn = sb("xn", [P, TT, D])
        bn1 = sb("bn1", [P, TT, 6])
        mv1 = sb("mv1", [P, TT, 2])
        rstd1 = sb("rstd1", [P, TT])
        hT = sb("hT", [P, KD, SEQ])
        hP = [sb(f"hP{n}", [P, KD, SEQ >> n]) for n in (1, 2, 3)]
        hC = sb("hC", [P, KD, 2 * P])
        qT = sb("qT", [P, 2, SEQ])
        kT = sb("kT", [P, 2, SEQ])
        qP = [sb(f"qP{n}", [P, 2, SEQ >> n]) for n in (1, 2, 3)]
        qC = sb("qC", [P, 2, 2 * P])
        kP = [sb(f"kP{n}", [P, 2, SEQ >> n]) for n in (1, 2, 3, 4)]
        V = sb("V", [P, 2, UNITS, 4 * DH])
        sm = sb("sm", [P, 2, UNITS * 2 * 32])
        mx = sb("mx", [P, 2, UNITS * 2])
        rs = sb("rs", [P, UNITS, HEADS])
        AT = sb("AT", [P, 2, 5 * 2, P])
        MG = sb("MG", [P, 2, 2, P + 64])
        YT = sb("YT", [P, 8, SEQ])
        YN = sb("YN", [P, 8, SEQ])
        mrow = YN[0:BATCH, 0:3, :].rearrange("p a (r d) -> p (a r) d", r=2)
        bo_row = YN[0:BATCH, 3, :].rearrange("p (r d) -> p r d", r=2)
        mtmp = YN[0:BATCH, 4, :].rearrange("p (r d) -> p r d", r=2)
        den = sb("den", [HEADS, SEQ])
        rden = sb("rden", [HEADS, SEQ])
        rows = sb("rows", [P, 4, D])
        xr = sb("xr", [P, TT, D])
        x2 = sb("x2", [P, TT, D])
        bn2 = sb("bn2", [P, TT, 6])
        mv2 = sb("mv2", [P, TT, 2])
        rstd2 = sb("rstd2", [P, TT])
        h2 = sb("h2", [P, TT, D])
        h2T = sb("h2T", [P, KD, SEQ])
        lg = sb("lg", [P, TT, EXPERTS])
        v8 = sb("v8", [P, TT, 8])
        i8 = sb("i8", [P, TT, 8], U32)
        if8 = sb("if8", [P, TT, TOPK])
        ex = sb("ex", [P, TT, EXPERTS + TOPK])
        sume = sb("sume", [P, TT])
        rsum = sb("rsum", [P, TT])
        oh = sb("oh", [P, TOPK, TT, EXPERTS])
        ohs = sb("ohs", [P, TT, EXPERTS])
        base = sb("base", [P, TT + 1, EXPERTS])
        posb = sb("posb", [P, TT, EXPERTS])
        posm = sb("posm", [P, TOPK, TT, EXPERTS])
        posf = sb("posf", [P, TOPK, TT])
        slot = sb("slot", [P, TOPK, TT], I32)
        slotf_all = sb("slotf_all", [P, BATCH, TOPK * TT])
        slot_all = sb("slot_all", [P, BATCH, TOPK * TT], I32)
        gate_all = sb("gate_all", [P, BATCH, TT * TOPK])
        tailf = sb("tailf", [P, EXPERTS])
        taili = sb("taili", [P, EXPERTS], I32)
        zrow = sb("zrow", [P, D])
        tb8 = sb("tb8", [P, 6, EXPERTS])
        nti = sb("nti", [P, EXPERTS], I32)
        past, pastw = (buf[:, 0, 0:512].rearrange("p (n e) -> p n e", e=EXPERTS) for buf in (h2T, YN))
        ind, indw = (buf[:, :, :].rearrange("p t n -> p (t n)")[:, 0:TILES * EXPERTS]
                     .rearrange("p (t e) -> p t e", e=EXPERTS) for buf in (xr, x_sb))
        tabf = sb("tabf", [P, 4, TILES])
        tabi = sb("tabi", [P, 4, TILES], I32)
        cumf = sb("cumf", [P, EXPERTS])
        cumi = sb("cumi", [P, EXPERTS], I32)
        w13_sb = sb("w13_sb", [P, 2, KD * FF2])
        w2_sb = sb("w2_sb", [P, 2, FC * D])
        bias_bc = sb("bias_bc", [P, D])

        xs = YT[:, 0:1, :].rearrange("p a (b n) -> p (a b) n", b=2)
        xT = YT[:, 1, 0:2 * P].rearrange("p (k n) -> p k n", k=KD)
        hh_flat = YT[:, 4:6, :].rearrange("p a n -> p (a n)")[:, 0:FF]
        gg = YT[:, 2:4, :].rearrange("p a n -> p (a n)")[:, 0:FF].rearrange("p (a n) -> p a n", a=2)
        hh = hh_flat.rearrange("p (a n) -> p a n", a=2)
        hTf = YN[:, 0:2, 0:3 * P].rearrange("p a (c n) -> p a c n", c=3)
        ysb = YN[:, 2, :].rearrange("p (b n) -> p b n", b=2)
        yg = YN[:, :, :].rearrange("p (a b) (c n) -> p a (b c) n", a=2, c=2)
        xf = YT[:, 0:4, :].rearrange("p (a b) (c n) -> p a (b c) n", a=2, c=2)
        of = YT[:, 4:8, :].rearrange("p (a b) (c n) -> p a (b c) n", a=2, c=2)
        gidx = sb("gidx", [P, 2, TOPK * TT], I32)
        frow = hT[:, :, :].rearrange("p n (r d) -> p n r d", r=2)

        pA = pb("pA", [P, 2, SEQ])
        pS = pb("pS", [P, 2, SEQ])
        pY = pb("pY", [P, 2, SEQ])
        pM = pb("pM", [P, 2, SEQ])
        p13 = [pA, pS]
        pH, pXY = pY, pM

        s_const = sem("s_const")
        s_b0 = sem("s_b0")
        s_silu = sem("s_silu")
        s_modp = sem("s_modp")
        s_mod = sem("s_mod")
        s_modst = sem("s_modst")
        s_xin = sem("s_xin")
        s_bn1, s_mv1, s_ve1, s_rs1, s_xn = (sem("s_" + n) for n in ("bn1", "mv1", "ve1", "rs1", "xn"))
        s_pj = sem("s_pj")
        s_pe = sem("s_pe")
        s_hp = sem("s_hp")
        s_qk = sem("s_qk")
        s_sc = sem("s_sc")
        s_mk, s_mx, s_sb_, s_ex = (sem("s_" + n) for n in ("mk", "mx", "sb", "ex"))
        s_rs = sem("s_rs")
        s_at = sem("s_at")
        s_y = sem("s_y")
        s_ye = sem("s_ye")
        s_rt, s_dn, s_rd, s_bc, s_yn = (sem("s_" + n) for n in ("rt", "dn", "rd", "bc", "yn"))
        s_rows, s_xres, s_xrb = sem("s_rows"), sem("s_xres"), sem("s_xrb")
        s_op, s_xg, s_x2, s_x2st = (sem("s_" + n) for n in ("op", "xg", "x2", "x2st"))
        s_bn2, s_mv2, s_ve2, s_rs2, s_xn2, s_hm, s_h2 = (
            sem("s_" + n) for n in ("bn2", "mv2", "ve2", "rs2", "xn2", "hm", "h2"))
        s_t2, s_t2e, s_lp, s_lg, s_v8, s_i8 = (sem("s_" + n) for n in ("t2", "t2e", "lp", "lg", "v8", "i8"))
        s_dx, s_ex8, s_su, s_rsu, s_gt, s_if, s_oh, s_ohs = (
            sem("s_" + n) for n in ("dx", "ex8", "su", "rsu", "gt", "if", "oh", "ohs"))
        s_px, s_ba, s_pb, s_pm, s_pf, s_sl, s_sla, s_disp = (
            sem("s_" + n) for n in ("px", "ba", "pb", "pm", "pf", "sl", "sla", "disp"))
        s_tab = sem("s_tab")
        s_zero = sem("s_zero")
        s_win = sem("s_win")
        s_tx, s_xT, s_m1, s_gl, s_mu, s_th, s_hT, s_m2, s_yv = (
            sem("s_" + n) for n in ("tx", "xT", "m1", "gl", "mu", "th", "hT", "m2", "yv"))
        s_xs, s_yst, s_yg, s_xf, s_out = ([sem(f"s_{n}{i}") for i in range(2)] for n in ("xs", "yst", "yg", "xf", "out"))
        s_ix, s_fa, s_fb, s_fc, s_fd, s_f = (
            sem("s_" + n) for n in ("ix", "fa", "fb", "fc", "fd", "f"))

        block = ctx.enter_context(nc.Block())

        NCONST = 12 * 16
        NMOD = 14
        NTAB = 23

        def x_rows(b):
            return x[bass.ds(b * SEQ, SEQ), :].rearrange("(t p) d -> p t d", p=P)

        def over_batches(eng, body):
            body(0)
            body(1)
            with eng.Fori(2, BATCH - 1) as b:
                body(b)
            body(BATCH - 1)
            body(BATCH)

        def head(b):
            return not (isinstance(b, int) and b == BATCH)

        def tail(b):
            return not (isinstance(b, int) and b == 0)

        def following(b):
            return not (isinstance(b, int) and b >= BATCH - 1)

        @block.sync
        def _(sp):
            for dst, src in ((cst[:, :], consts), (cT_sb[:, :, :], cT),
                             (sel_sb[:, :, :], sel),
                             (rout_sb[:, :, :], router),
                             (bo_row[:, 0, :], b_out.partition_broadcast(BATCH)),
                             (bo_row[:, 1, :], ffn_bias.partition_broadcast(BATCH)),
                             (bias_bc[:, :], ffn_bias.partition_broadcast(P)),
                             (YT[:, 0:6, :].rearrange("p (k a) n -> p k (a n)", k=KD), wmod)):
                sp.dma_start(dst, src).then_inc(s_const, 16)
            sp.dma_start(x_sb[:, :, :], x_rows(0)).then_inc(s_xin, 16)
            for k in range(KD):
                sp.dma_start(wqkv_sb[:, k, :], wqkv[:, k, :]).then_inc(s_const, 16)
            sp.dma_start(wout_sb[:, :, :], wout).then_inc(s_const, 16)
            sp.wait_ge(s_b0, 6)
            sp.dma_start(xs_dram[EXPERTS * CAP:SLOTS, :], zrow[:, :]).then_inc(s_const, 16)
            sp.wait_ge(s_mod, NMOD)
            sp.dma_start(rows_dram, mrow[:, :, :]).then_inc(s_modst, 16)
            sp.wait_ge(s_modst, 16)

            def weights(e, n):
                eng_src = w13[bass.ds(e, 1), :, :].rearrange("a p n -> (a p) n")
                sp.dma_start(w13_sb[:, n, :], eng_src).then_inc(s_win, 16)
                src = w2[bass.ds(e, 1), :, :].rearrange("a f n -> (a f) n")
                sp.dma_start(w2_sb[:, n, 0:5 * D].rearrange("p (c n) -> p c n", c=5),
                             src[0:5 * P, :].rearrange("(c p) n -> p c n", p=P)).then_inc(s_win, 16)
                sp.dma_start(w2_sb[0:FTAIL, n, 5 * D:6 * D], src[5 * P:FF, :]).then_inc(s_win, 16)

            def body(b):
                if following(b):
                    sp.wait_ge(s_xn, b + 1)
                    sp.dma_start(x_sb[:, :, :], x_rows(b + 1)).then_inc(s_xin, 16)
                if tail(b):
                    if some(b - 1):
                        sp.wait_ge(s_x2, b - 1)
                    sp.dma_start(xr[:, :, :], x_rows(b - 1)).then_inc(s_xres, 16)
                    if some(b - 1):
                        sp.wait_ge(s_h2, b - 1)
                    sp.dma_start(rows[:, :, :],
                                 rows_dram[bass.ds(b - 1, 1), 0:4, :].rearrange("a r n -> (a r) n")
                                 .partition_broadcast(P)).then_inc(s_rows, 16)
                    sp.wait_ge(s_x2, b)
                    sp.dma_start(x2_dram[bass.ds((b - 1) * SEQ, SEQ), :].rearrange("(t p) d -> p t d", p=P),
                                 x2[:, :, :]).then_inc(s_x2st, 16)
                else:
                    sp.wait_ge(s_win, 48)
                    weights(1, 1)

            weights(0, 0)
            over_batches(sp, body)
            sp.wait_ge(s_tab, NTAB)
            for e in range(2, EXPERTS):
                last_use = sp.value_load(cumi[0:1, e - 2:e - 1], min_val=1, max_val=TILES + 1)
                sp.wait_ge(s_m2, last_use)
                sp.wait_ge(s_win, 48 * e)
                weights(e, e % 2)
            for n in range(2):
                sp.wait_ge(s_yst[n], 8 * TILES)
            sp.wait_ge(s_x2st, 16 * BATCH)
            def load_last(b, n):
                sp.dma_start(xf[:, n, :, :],
                             x2_dram[bass.ds(b * SEQ, SEQ), :].rearrange("(t p) d -> p t d", p=P)).then_inc(s_xf[n], 16)
                sp.dma_start(frow[:, n, :, :],
                             rows_dram[bass.ds(b, 1), 4:6, :].rearrange("a r n -> (a r) n")
                             .partition_broadcast(P)).then_inc(s_xf[n], 16)

            def store_last(b, n):
                sp.wait_ge(s_f, b + 1)
                sp.dma_start(out[bass.ds(b * SEQ, SEQ), :].rearrange("(t p) d -> p t d", p=P),
                             of[:, n, :, :]).then_inc(s_out[n], 16)

            load_last(0, 0)
            load_last(1, 1)
            with sp.Fori(0, BATCH // 2 - 1) as pair:
                for n in range(2):
                    store_last(pair * 2 + n, n)
                    load_last(pair * 2 + (n + 2), n)
            for n in range(2):
                store_last(BATCH - 2 + n, n)
            for n in range(2):
                sp.wait_ge(s_out[n], 8 * BATCH)

        @block.gpsimd
        def _(pool):
            nc.gpsimd.memset(ones[:, :], 1.0).then_inc(s_b0, 1)
            nc.gpsimd.memset(halfneg[:, :], -0.5).then_inc(s_b0, 1)
            nc.gpsimd.memset(zrow[:, :], 0.0).then_inc(s_b0, 1)
            nc.gpsimd.memset(AT[:, :, :, :], 0.0).then_inc(s_b0, 1)
            nc.gpsimd.memset(MG[:, :, :, :], 0.0).then_inc(s_b0, 1)
            nc.gpsimd.memset(rs[:, :, :], 0.0).then_inc(s_b0, 1)
            pool.wait_ge(s_const, NCONST)

            def rstd(b, mv, r, s_mv, s_ve, s_rs_):
                needed = held(pool, TT * b + TT)
                pool.wait_ge(s_mv, 1)
                pool.wait_ge(s_mv, needed)
                nc.gpsimd.tensor_scalar(r[:, :], mv[:, :, 1], LN_EPS, None, ALU.add).then_inc(s_ve, 1)
                pool.wait_ge(s_ve, b + 1)
                nc.gpsimd.tensor_tensor(r[:, :], r[:, :], halfneg[:, :], ALU.pow).then_inc(s_rs_, 1)

            def halve(dst, src, s):
                nc.gpsimd.tensor_tensor(dst[:, :, :], src[:, :, 0::2], src[:, :, 1::2], ALU.add).then_inc(s, 1)

            def halve_part(dst, lo, n, src, block, s):
                pairs = src[:, :, 0:64 * n].rearrange("p k (n r s) -> p k n r s", r=32, s=2)[:, :, :, 16 * block:16 * block + 16, :]
                nc.gpsimd.tensor_tensor(dst[:, :, lo:lo + 16 * n].rearrange("p k (n r) -> p k n r", r=16),
                                        pairs[:, :, :, :, 0], pairs[:, :, :, :, 1], ALU.add).then_inc(s, 1)

            def pool_h(b):
                pool.wait_ge(s_pe, job_x(b, KD - 1) + 1)
                if tail(b):
                    pool.wait_ge(s_pj, job(b - 1, GROUPS - 1, 6) + 1)
                halve(hP[0], hT, s_hp)
                halve_part(hC, 0, 8, hT, 0, s_hp)
                pool.wait_ge(s_hp, 8 * b + 1)
                halve(hP[1], hP[0], s_hp)
                halve_part(hC, P, 4, hP[0], 0, s_hp)
                pool.wait_ge(s_hp, 8 * b + 3)
                halve(hP[2], hP[1], s_hp)
                halve_part(hC, P + 64, 2, hP[1], 0, s_hp)
                pool.wait_ge(s_hp, 8 * b + 5)
                halve_part(hC, P + 96, 1, hP[2], 0, s_hp)
                halve_part(hC, P + 112, 1, hP[2], 0, s_hp)

            def pool_qk(b, g):
                step = b * GROUPS + g
                pool.wait_ge(s_pe, job(b, g, 3) + 1)
                if some(2 * step):
                    pool.wait_ge(s_sc, 2 * step)
                done = 12 * step
                halve(qP[0], qT, s_qk)
                halve(kP[0], kT, s_qk)
                halve_part(qC, 0, 8, qT, 1, s_qk)
                pool.wait_ge(s_qk, done + 2)
                halve(qP[1], qP[0], s_qk)
                halve(kP[1], kP[0], s_qk)
                halve_part(qC, P, 4, qP[0], 1, s_qk)
                pool.wait_ge(s_qk, done + 5)
                halve(qP[2], qP[1], s_qk)
                halve(kP[2], kP[1], s_qk)
                halve_part(qC, P + 64, 2, qP[1], 1, s_qk)
                pool.wait_ge(s_qk, done + 8)
                halve(kP[3], kP[2], s_qk)
                halve_part(qC, P + 96, 1, qP[2], 1, s_qk)
                halve_part(qC, P + 112, 1, qP[2], 1, s_qk)

            def residual(b):
                pool.wait_ge(s_xres, 16 * (b + 1))
                pool.wait_ge(s_rows, 16 * (b + 1))
                nc.gpsimd.tensor_tensor(xr[:, :, :], xr[:, :, :],
                                        rows[:, 1:2, :].broadcast_to([P, TT, D]), ALU.add).then_inc(s_xrb, 1)

            def modulate2(b):
                pool.wait_ge(s_xn2, b + 1)
                nc.gpsimd.tensor_tensor(h2[:, :, :], h2[:, :, :],
                                        rows[:, 2:3, :].broadcast_to([P, TT, D]), ALU.mult).then_inc(s_hm, 1)
                pool.wait_ge(s_hm, b + 1)
                nc.gpsimd.tensor_tensor(h2[:, :, :], h2[:, :, :],
                                        rows[:, 3:4, :].broadcast_to([P, TT, D]), ALU.add).then_inc(s_h2, 1)

            def dispatch(b):
                needed = held(pool, b + 1)
                pool.wait_ge(s_sl, 1)
                pool.wait_ge(s_sl, needed)
                pool.wait_ge(s_h2, b + 1)
                for k in range(TOPK):
                    for t in range(TT):
                        nc.gpsimd.indirect_dma_start(
                            xs_dram, bass.IndirectOffsetOnAxis(ap=slot[:, k, t:t + 1], axis=0),
                            h2[:, t, :], None).then_inc(s_disp, 16)

            def body(b):
                if head(b):
                    if not tail(b):
                        rstd(0, mv1, rstd1, s_mv1, s_ve1, s_rs1)
                    pool_h(b)
                    pool_qk(b, 0)
                if tail(b):
                    residual(b - 1)
                if head(b):
                    pool_qk(b, 1)
                    if following(b):
                        rstd(b + 1, mv1, rstd1, s_mv1, s_ve1, s_rs1)
                    pool_qk(b, 2)
                if tail(b):
                    rstd(b - 1, mv2, rstd2, s_mv2, s_ve2, s_rs2)
                    modulate2(b - 1)
                if head(b):
                    pool_qk(b, 3)
                if tail(b):
                    dispatch(b - 1)

            over_batches(pool, body)
            pool.wait_ge(s_tab, 2)
            for e in range(EXPERTS):
                nc.gpsimd.indirect_dma_start(
                    xs_dram, bass.IndirectOffsetOnAxis(ap=taili[:, e:e + 1], axis=0),
                    zrow[:, :], None).then_inc(s_zero, 16)
            pool.wait_ge(s_disp, 16 * BATCH * TOPK * TT)
            pool.wait_ge(s_zero, 16 * EXPERTS)
            pool.wait_ge(s_const, NCONST)
            pool.wait_ge(s_tab, NTAB)
            pool.wait_ge(s_op, 2 * BATCH)

            def load_rows(j, n):
                row = pool.value_load(tabi[0:1, 0, bass.ds(j, 1)], min_val=0, max_val=EXPERTS * CAP)
                pool.dma_start(xs[:, n, :], xs_dram[bass.ds(row, P), :]).then_inc(s_xs[n], 16)

            def store_rows(j, n):
                pool.dma_start(ys_dram[bass.ds(j * P, P), :], ysb[:, n, :]).then_inc(s_yst[n], 16)

            load_rows(0, 0)
            load_rows(1, 1)

            def tile(pair, n, more):
                j = pair * 2 + n
                if more:
                    pool.wait_ge(s_tx, j + 1)
                    load_rows(j + 2, n)
                pool.wait_ge(s_yv, j + 1)
                store_rows(j, n)

            with pool.Fori(0, TILES // 2 - 1) as pair:
                tile(pair, 0, True)
                tile(pair, 1, True)
            tile(TILES // 2 - 1, 0, False)
            tile(TILES // 2 - 1, 1, False)
            for n in range(2):
                pool.wait_ge(s_yst[n], 8 * TILES)
            def gather(b, n):
                if some(TT * b - TT):
                    pool.wait_ge(s_fb, TT * b - TT)
                needed = held(pool, b + 1)
                pool.wait_ge(s_ix, 1)
                pool.wait_ge(s_ix, needed)
                for i in range(TOPK * TT):
                    nc.gpsimd.indirect_dma_start(
                        yg[:, n, i, :], None, ys_dram,
                        bass.IndirectOffsetOnAxis(ap=gidx[:, n, i:i + 1], axis=0)).then_inc(s_yg[n], 16)

            gather(0, 0)
            gather(1, 1)
            with pool.Fori(1, BATCH // 2) as pair:
                gather(pair * 2, 0)
                gather(pair * 2 + 1, 1)

        @block.scalar
        def _(act):
            act.wait_ge(s_const, NCONST)
            nc.scalar.activation(sil[:, :, :], cT_sb[:, :, :], ACT.Exp, scale=-1.0).then_inc(s_silu, 1)

            def evac(dst, src, src_job):
                act.wait_ge(s_pj, src_job + 1)
                nc.scalar.activation(dst, src, ACT.Copy).then_inc(s_pe, 1)

            def evac_x(b):
                for k in range(KD):
                    act.wait_ge(s_pj, job_x(b, k) + 1)
                    if k == 0 and tail(b):
                        act.wait_ge(s_hp, 8 * b)
                    nc.scalar.activation(hT[:, k, :], pA[:, k, :], ACT.Identity,
                                         bias=modT[:, k, bass.ds(b, 1)],
                                         scale=modT[:, KD + k, bass.ds(b, 1)]).then_inc(s_pe, 1)

            def exps(step):
                for e in range(2):
                    act.wait_ge(s_sb_, 2 * step + e + 1)
                    nc.scalar.activation(sm[:, e, :], sm[:, e, :], ACT.Exp).then_inc(s_ex, 1)

            def results(b, g):
                step = b * GROUPS + g
                for c in range(2):
                    act.wait_ge(s_y, 2 * step + c + 1)
                    act.wait_ge(s_yn, 8 * b + 2 * g + c + 1)
                    nc.scalar.activation(YT[:, 2 * g + c, :], pY[:, c, :], ACT.Copy).then_inc(s_ye, 1)

            act.wait_ge(s_mod, 2)
            evac_x(0)

            def body(b):
                for g in range(GROUPS):
                    step = b * GROUPS + g
                    if head(b):
                        if some(2 * step):
                            act.wait_ge(s_sc, 2 * step)
                        if some(12 * step):
                            act.wait_ge(s_qk, 12 * step)
                        for i in range(4):
                            dst = (qT if i < 2 else kT)[:, i % 2, :]
                            evac(dst, pA[:, (KD + 7 * g + i) % 2, :], job(b, g, i))
                        if some(2 * step - 2):
                            act.wait_ge(s_y, 2 * step - 2)
                        for i in range(3):
                            evac(V[:, g % 2, 2 * i:2 * i + 2, :].rearrange("p u n -> p (u n)"),
                                 pA[:, (KD + 7 * g + 4 + i) % 2, :], job(b, g, 4 + i))
                        if g == GROUPS - 1 and following(b):
                            evac_x(b + 1)
                    if g == 0:
                        if tail(b):
                            results(b - 1, GROUPS - 1)
                    elif head(b):
                        results(b, g - 1)
                    if head(b):
                        exps(step)
                    if g == 3 and tail(b):
                        for k in range(KD):
                            act.wait_ge(s_t2, (b - 1) * KD + k + 1)
                            nc.scalar.activation(h2T[:, k, :], pM[:, k, :], ACT.Copy).then_inc(s_t2e, 1)
                        act.wait_ge(s_dx, 2 * b)
                        nc.scalar.activation(ex[:, :, :], ex[:, :, :], ACT.Exp).then_inc(s_ex8, 1)

            over_batches(act, body)

            def tile(j):
                act.wait_ge(s_m1, j + 1)
                act.wait_ge(s_mu, j)
                nc.scalar.activation(gg[:, :, :], p13[0][:, :, 0:FF // 2], ACT.Gelu).then_inc(s_gl, 1)
                act.wait_ge(s_th, j + 1)
                act.wait_ge(s_m2, j + 1)
                nc.scalar.activation(hTf[:, :, :, :],
                                     pH[:, :, 0:3 * P].rearrange("p a (c n) -> p a c n", c=3),
                                     ACT.Copy).then_inc(s_hT, 1)

            tile(0)
            with act.Fori(1, TILES) as j:
                tile(j)

        @block.tensor
        def _(pe):
            mm = nc.tensor.matmul

            pe.wait_ge(s_silu, 4)
            wm = YT[:, 0:6, :].rearrange("p (k a) n -> p k (a n)", k=KD)
            for n in range(2 * KD):
                for k in range(KD):
                    mm(pM[:, 0, n * BATCH:(n + 1) * BATCH], wm[:, k, n * P:(n + 1) * P], siT[:, k, :],
                       start=(k == 0), stop=(k == KD - 1))
            for m in range(2):
                for k in range(KD):
                    last = mm(pA[0:BATCH, m, :], siT[:, k, :], wm[:, k, (m + 1) * SEQ:(m + 2) * SEQ],
                              start=(k == 0), stop=(k == KD - 1))
            last.then_inc(s_modp, 1)
            pe.wait_ge(s_mod, NMOD)

            def transposed_x(b):
                pe.wait_ge(s_xn, b + 1)
                for k in range(KD):
                    n = job_x(b, k)
                    if some(n - 1):
                        pe.wait_ge(s_pe, n - 1)
                    for t in range(TT):
                        last = nc.tensor.transpose(pA[:, k, t * P:(t + 1) * P],
                                                   xn[:, t, k * P:(k + 1) * P], ident)
                    last.then_inc(s_pj, 1)

            def heads_qk(b, g):
                for i in range(4):
                    n = job(b, g, i)
                    pe.wait_ge(s_pe, n - 1)
                    if i == 0 and g == 0:
                        pe.wait_ge(s_pe, n)
                    col = (i // 2) * INNER + (2 * g + i % 2) * P
                    for k in range(KD):
                        last = mm(pA[:, (KD + 7 * g + i) % 2, :], wqkv_sb[:, k, col:col + P], hT[:, k, :],
                                  start=(k == 0), stop=(k == KD - 1))
                    last.then_inc(s_pj, 1)

            def heads_v(b, g):
                for i in range(3):
                    n = job(b, g, 4 + i)
                    pe.wait_ge(s_pe, n - 1)
                    if i == 2 and g == 0:
                        pe.wait_ge(s_hp, 8 * b + 8)
                    col = 2 * INNER + g * 4 * DH
                    for u in (2 * i, 2 * i + 1):
                        for k in range(KD):
                            rows_u = hT[:, k, u * P:(u + 1) * P] if u < TT else hC[:, k, (u - TT) * P:(u - TT + 1) * P]
                            last = mm(pA[:, (KD + 7 * g + 4 + i) % 2, (u % 2) * 4 * DH:(u % 2 + 1) * 4 * DH],
                                      rows_u, wqkv_sb[:, k, col:col + 4 * DH],
                                      start=(k == 0), stop=(k == KD - 1))
                    last.then_inc(s_pj, 1)

            def scores(b, g):
                step = b * GROUPS + g
                pe.wait_ge(s_pe, job(b, g, 3) + 1)
                if some(6 * step):
                    needed = held(pe, 6 * step)
                    pe.wait_ge(s_mk, 1)
                    pe.wait_ge(s_mk, needed)
                for e in range(2):
                    lo, hi = e * DH, (e + 1) * DH

                    def block(u, c, quad, q, k):
                        return mm(pS[quad * 32:(quad + 1) * 32, e, (2 * u + c) * 32:(2 * u + c + 1) * 32],
                                  q, k, start=True, stop=True)

                    for u in range(TT):
                        for c in range(2):
                            for quad in range(4):
                                a = u * P + quad * 32
                                block(u, c, quad, qT[lo:hi, c, a:a + 32], kT[lo:hi, c, a:a + 32])
                    if e == 0:
                        needed = held(pe, 12 * step + 12)
                        pe.wait_ge(s_qk, 1)
                        pe.wait_ge(s_qk, needed)
                    for c in range(2):
                        for u in (4, 5):
                            for quad in range(4):
                                q = qC[lo:hi, c, (u - 4) * P + quad * 32:(u - 4) * P + (quad + 1) * 32]
                                n, a = (0, quad * 64) if u == 4 else ((1, quad * 64), (1, quad * 64), (2, 0), (3, 0))[quad]
                                if (u, quad) == (5, 3):
                                    k = kP[n][lo:hi, c:c + 1, 0:16].broadcast_to([DH, 2, 16])
                                else:
                                    k = kP[n][lo:hi, c, a:a + 64].rearrange("p (n r) -> p n r", r=32)[:, :, 0:16]
                                last = block(u, c, quad, q, k)
                    last.then_inc(s_sc, 1)

            def products(b, g):
                step = b * GROUPS + g
                pe.wait_ge(s_at, 16 * step + 16)
                pe.wait_ge(s_pe, job(b, g, 6) + 1)
                if some(2 * step):
                    pe.wait_ge(s_ye, 2 * step)
                for c in range(2):
                    for u in range(UNITS):
                        for e in range(2):
                            val = V[:, g % 2, u, (2 * c + e) * DH:(2 * c + e + 1) * DH]
                            row = pY[e * DH:(e + 1) * DH, c, :]
                            if u < TT:
                                dst, src = row[:, u * P:(u + 1) * P], AT[:, e, 2 * u + c, :]
                            elif u == TT:
                                dst = row.rearrange("p (n r s) -> p n r s", r=32, s=2)[:, :, 16:32, 1]
                                src = AT[:, e, 2 * u + c, :]
                            else:
                                dst, src = row.rearrange("p (n s) -> p n s", s=4)[:, :, 3], MG[:, e, c, 0:P]
                            last = mm(dst, val, src, start=(u == 0), stop=(u == UNITS - 1),
                                      skip_group_check=True)
                    last.then_inc(s_y, 1)

            def sums_transposed(b):
                pe.wait_ge(s_rs, 8 * b + 8)
                if some(b):
                    pe.wait_ge(s_lg, b)
                if some(b):
                    pe.wait_ge(s_pb, b)
                pe.wait_ge(s_ba, 5 * b + 1)
                for u in range(UNITS):
                    last = nc.tensor.transpose(pM[0:HEADS, u // 4, (u % 4) * P:(u % 4 + 1) * P],
                                               rs[:, u, :], ident)
                last.then_inc(s_rt, 1)

            def broadcast_sums(b):
                pe.wait_ge(s_rd, b + 1)
                for c in range(8):
                    pe.wait_ge(s_yn, 8 * b + c + 7)
                    mm(pM[:, c % 2, :], sel_sb[:, c, :], rden[:, :], start=True, stop=True).then_inc(s_bc, 1)

            def projection(b):
                pe.wait_ge(s_yn, 8 * b + 16)
                for t in range(TT):
                    for c in range(8):
                        last = mm(pM[:, t // 2, (t % 2) * D:(t % 2 + 1) * D],
                                  YN[:, c, t * P:(t + 1) * P], wout_sb[:, c, :],
                                  start=(c == 0), stop=(c == 7))
                    if t % 2:
                        last.then_inc(s_op, 1)

            def route(b):
                pe.wait_ge(s_h2, b + 1)
                pe.wait_ge(s_xg, 2 * b + 2)
                for k in range(KD):
                    for t in range(TT):
                        last = nc.tensor.transpose(pM[:, k, t * P:(t + 1) * P], h2[:, t, k * P:(k + 1) * P], ident)
                    last.then_inc(s_t2, 1)
                pe.wait_ge(s_t2e, KD * b + KD)
                for t in range(TT):
                    for k in range(KD):
                        last = mm(pM[:, 0, t * EXPERTS:(t + 1) * EXPERTS], h2T[:, k, t * P:(t + 1) * P],
                                  rout_sb[:, k, :], start=(k == 0), stop=(k == KD - 1))
                last.then_inc(s_lp, 1)

            def count(b):
                pe.wait_ge(s_ohs, b + 1)
                flat = ohs[:, :, :].rearrange("p t e -> p (t e)")
                mm(pM[:, 1, 0:TT * EXPERTS], cst[:, C_TRI:C_TRI + P], flat, start=True, stop=True)
                mm(pM[:, 1, TT * EXPERTS:2 * TT * EXPERTS], ones[:, :], flat,
                   start=True, stop=True).then_inc(s_px, 1)

            transposed_x(0)

            def body(b):
                for g in range(GROUPS):
                    if head(b):
                        heads_qk(b, g)
                    if g == 1 and tail(b):
                        broadcast_sums(b - 1)
                    if head(b):
                        heads_v(b, g)
                        if g == GROUPS - 1 and following(b):
                            transposed_x(b + 1)
                    if g == 0:
                        if tail(b):
                            products(b - 1, GROUPS - 1)
                            sums_transposed(b - 1)
                    elif head(b):
                        products(b, g - 1)
                    if head(b):
                        scores(b, g)
                    if g == 2 and tail(b):
                        projection(b - 1)
                    if g == 3 and tail(b):
                        route(b - 1)
                        count(b - 1)

            over_batches(pe, body)

            pe.wait_ge(s_tab, NTAB)

            def transposed_rows(j, n, pair):
                pe.wait_ge(s_xs[n], 16 * pair + 16)
                if some(j):
                    pe.wait_ge(s_xT, j)
                for k in range(KD):
                    last = nc.tensor.transpose(pXY[:, 0, k * P:(k + 1) * P], xs[:, n, k * P:(k + 1) * P], ident)
                last.then_inc(s_tx, 1)

            def up(j):
                arrived = pe.value_load(tabi[0:1, 2, bass.ds(j, 1)], min_val=48, max_val=48 * EXPERTS)
                at = pe.value_load(tabi[0:1, 3, bass.ds(j, 1)], min_val=0, max_val=1)
                pe.wait_ge(s_win, arrived)
                w = w13_sb[:, :, :].rearrange("p s n -> p (s n)")
                pe.wait_ge(s_xT, j + 1)
                if some(j):
                    pe.wait_ge(s_mu, j)
                if some(j):
                    pe.wait_ge(s_gl, j)
                for half in range(4):
                    for k in range(KD):
                        last = mm(p13[half // 2][:, half % 2, 0:FF // 2], xT[:, k, :],
                                  w[:, bass.ds(at * (KD * FF2) + (k * FF2 + half * (FF // 2)), FF // 2)],
                                  start=(k == 0), stop=(k == KD - 1))
                last.then_inc(s_m1, 1)

            def down(j):
                at = pe.value_load(tabi[0:1, 3, bass.ds(j, 1)], min_val=0, max_val=1)
                w = w2_sb[:, :, :].rearrange("p s n -> p (s n)")
                pe.wait_ge(s_hT, j + 1)
                pe.wait_ge(s_yv, j)
                for c in range(FC):
                    rows_c = P if c < FC - 1 else FTAIL
                    last = mm(pXY[:, 1, 0:D], hTf[0:rows_c, c // 3, c % 3, :],
                              w[0:rows_c, bass.ds(at * (FC * D) + c * D, D)], start=(c == 0), stop=(c == FC - 1))
                last.then_inc(s_m2, 1)

            def hidden_transposed(j):
                pe.wait_ge(s_mu, j + 1)
                if some(j):
                    pe.wait_ge(s_hT, j)
                for c in range(FC):
                    n = P if c < FC - 1 else FTAIL
                    last = nc.tensor.transpose(pH[0:n, c // 3, (c % 3) * P:(c % 3 + 1) * P],
                                               hh_flat[:, c * P:c * P + n], ident)
                last.then_inc(s_th, 1)

            transposed_rows(0, 0, 0)
            up(0)
            transposed_rows(1, 1, 0)
            hidden_transposed(0)

            def tile(j, n, pair):
                up(j)
                down(j - 1)
                transposed_rows(j + 1, n, pair)
                hidden_transposed(j)

            tile(1, 0, 1)
            tile(2, 1, 1)
            with pe.Fori(1, TILES // 2 - 1) as pair:
                tile(pair * 2 + 1, 0, pair + 1)
                tile(pair * 2 + 2, 1, pair + 1)
            up(TILES - 1)
            down(TILES - 2)
            hidden_transposed(TILES - 1)
            down(TILES - 1)

        @block.vector
        def _(dve):
            v = nc.vector
            dve.wait_ge(s_const, NCONST)
            v.tensor_copy(base[:, TT, :], cst[:, C_CAP:C_CAP + 8]).then_inc(s_ba, 1)
            v.memset(mx[:, :, :], 0.0).then_inc(s_yn, 8)
            dve.wait_ge(s_silu, 1)
            v.tensor_scalar(sil[:, :, :], sil[:, :, :], 1.0, None, ALU.add).then_inc(s_silu, 1)
            dve.wait_ge(s_silu, 2)
            v.reciprocal(sil[:, :, :], sil[:, :, :]).then_inc(s_silu, 1)
            dve.wait_ge(s_silu, 3)
            v.tensor_tensor(siT[:, :, :], cT_sb[:, :, :], sil[:, :, :], ALU.mult).then_inc(s_silu, 1)
            dve.wait_ge(s_modp, 1)
            cols = pM[:, 0, 0:2 * KD * BATCH].rearrange("p (n b) -> p n b", b=BATCH)
            v.tensor_copy(modT[:, 0:KD, :], cols[:, 0:KD, :]).then_inc(s_mod, 1)
            v.tensor_scalar(modT[:, KD:2 * KD, :], cols[:, KD:2 * KD, :], 1.0, None, ALU.add).then_inc(s_mod, 1)
            n = 2
            for g_psum, r, bias in ((pA[0:BATCH, 0, 0:D], 0, 0), (pA[0:BATCH, 1, D:2 * D], 4, 1)):
                v.tensor_scalar(mtmp[:, 0, :], g_psum, 0.0, 2.0, ALU.is_ge, ALU.mult).then_inc(s_mod, 1)
                dve.wait_ge(s_mod, n + 1)
                v.scalar_tensor_tensor(mtmp[:, 1, :], mtmp[:, 0, :], -1.0, g_psum, ALU.add, ALU.mult).then_inc(s_mod, 1)
                dve.wait_ge(s_mod, n + 2)
                v.tensor_scalar(mtmp[:, 1, :], mtmp[:, 1, :], 0.25, None, ALU.max).then_inc(s_mod, 1)
                dve.wait_ge(s_mod, n + 3)
                v.scalar_tensor_tensor(mrow[:, r, :], mtmp[:, 0, :], -1.0, mtmp[:, 1, :],
                                       ALU.add, ALU.mult).then_inc(s_mod, 1)
                dve.wait_ge(s_mod, n + 4)
                v.tensor_tensor(mrow[:, r + 1, :], mrow[:, r, :], bo_row[:, bias, :], ALU.mult).then_inc(s_mod, 1)
                n += 5
            v.tensor_copy(mrow[:, 3, :], pA[0:BATCH, 0, D:2 * D]).then_inc(s_mod, 1)
            v.tensor_scalar(mrow[:, 2, :], pA[0:BATCH, 1, 0:D], 1.0, None, ALU.add).then_inc(s_mod, 1)

            def stats(b, src, bn, mv, s_bn, s_mv):
                for t in range(TT):
                    v.bn_stats(bn[:, t, :], src[:, t, :]).then_inc(s_bn, 1)
                for t in range(TT):
                    needed = held(dve, TT * b + t + 1)
                    dve.wait_ge(s_bn, 1)
                    dve.wait_ge(s_bn, needed)
                    v.bn_aggr(mv[:, t, :], bn[:, t, :]).then_inc(s_mv, 1)

            def stats1(b):
                dve.wait_ge(s_xin, 16 * (b + 1))
                stats(b, x_sb, bn1, mv1, s_bn1, s_mv1)

            def normalise1(b):
                dve.wait_ge(s_rs1, b + 1)
                if tail(b):
                    dve.wait_ge(s_pj, job_x(b - 1, KD - 1) + 1)
                for t in range(TT):
                    last = v.tensor_scalar(xn[:, t, :], x_sb[:, t, :], mv1[:, t, 0:1], rstd1[:, t:t + 1],
                                           ALU.subtract, ALU.mult)
                last.then_inc(s_xn, 1)

            def softmax(b, g):
                step = b * GROUPS + g
                for e in range(2):
                    dve.wait_ge(s_sc, 2 * step + e + 1)
                    for lo, n, scale, mask in ((0, 2 * TT, DH ** -0.5, C_M0), (2 * TT, 2, DH ** -0.5 / 4, C_M1),
                                               (2 * TT + 2, 2, cst[:, C_SC2:C_SC2 + 1], C_M2)):
                        piece = slice(lo * 32, (lo + n) * 32)
                        v.scalar_tensor_tensor(
                            sm[:, e, piece].rearrange("p (n r) -> p n r", r=32),
                            pS[:, e, piece].rearrange("p (n r) -> p n r", r=32), scale,
                            cst[:, mask:mask + 32].unsqueeze(1).broadcast_to([P, n, 32]),
                            ALU.mult, ALU.add).then_inc(s_mk, 1)
                    dve.wait_ge(s_mk, 6 * step + 3 * e + 3)
                    tiles = sm[:, e, :].rearrange("p (n r) -> p n r", r=32)
                    v.tensor_reduce(mx[:, e, :], tiles, AX.X, ALU.max).then_inc(s_mx, 1)
                    dve.wait_ge(s_mx, 2 * step + e + 1)
                    v.tensor_tensor(tiles, tiles, mx[:, e, :].unsqueeze(2).broadcast_to([P, 2 * UNITS, 32]),
                                    ALU.subtract).then_inc(s_sb_, 1)
                if g == 0 and tail(b):
                    dve.wait_ge(s_rt, b)
                for e in range(2):
                    dve.wait_ge(s_ex, 2 * step + e + 1)
                    tiles = sm[:, e, :].rearrange("p (u c r) -> p u c r", c=2, r=32)
                    v.tensor_reduce(rs[:, :, 4 * g + e:4 * g + e + 3:2], tiles, AX.X, ALU.add).then_inc(s_rs, 1)
                    if some(2 * step):
                        dve.wait_ge(s_y, 2 * step)
                    for quad in range(4):
                        q = slice(quad * 32, (quad + 1) * 32)
                        flat = sm[q, e, :].rearrange("p (n r) -> p n r", r=32)
                        v.transpose(AT[q, e, :, quad * 32:(quad + 1) * 32],
                                    flat[:, 0:2 * TT + 2, :]).then_inc(s_at, 1)
                        if quad < 2:
                            dst = MG[q, e, :, quad * 64:(quad + 1) * 64].rearrange("p c (n r) -> p c n r", r=32)[:, :, :, 16:32]
                        elif quad == 2:
                            dst = MG[q, e, :, 0:P].rearrange("p c (n r s) -> p c n r s", r=32, s=2)[:, :, :, 16:32, 1]
                        else:
                            dst = MG[q, e, :, 64:64 + P].rearrange("p c (n r s) -> p c n r s", r=16, s=4)[:, :, :, :, 3]
                        v.transpose(dst, flat[:, 2 * TT + 2:, :]).then_inc(s_at, 1)

            def sums(b):
                dve.wait_ge(s_rt, b + 1)
                v.tensor_scalar(den[:, :], pM[0:HEADS, 0, :], SUM_EPS, None, ALU.add).then_inc(s_dn, 1)
                n = 5 * b + 1
                for s, lo, cnt in ((2, 0, 8), (4, P, 4), (8, P + 64, 2), (16, P + 96, 1)):
                    dve.wait_ge(s_dn, n)
                    to = den[:, :].rearrange("p (n r s) -> p n r s", r=32, s=s)[:, :, 16:32, s - 1]
                    v.tensor_tensor(to, to, pM[0:HEADS, 1, lo:lo + 16 * cnt].rearrange("p (n r) -> p n r", r=16),
                                    ALU.add).then_inc(s_dn, 1)
                    n += 1
                dve.wait_ge(s_dn, n)
                v.reciprocal(rden[:, :], den[:, :]).then_inc(s_rd, 1)

            def divide(b):
                dve.wait_ge(s_ye, 8 * b + 8)
                if some(2 * b):
                    dve.wait_ge(s_op, 2 * b)
                for c in range(8):
                    dve.wait_ge(s_bc, 8 * b + c + 1)
                    v.tensor_tensor(YN[:, c, :], pM[:, c % 2, :], YT[:, c, :], ALU.mult).then_inc(s_yn, 1)

            def residual(b):
                dve.wait_ge(s_xrb, b + 1)
                if some(16 * b):
                    dve.wait_ge(s_x2st, 16 * b)
                for half in range(2):
                    dve.wait_ge(s_op, 2 * b + half + 1)
                    v.tensor_tensor(x2[:, 2 * half:2 * half + 2, :],
                                    pM[:, half, :].rearrange("p (t n) -> p t n", n=D),
                                    rows[:, 0:1, :].broadcast_to([P, 2, D]), ALU.mult).then_inc(s_xg, 1)
                dve.wait_ge(s_xg, 2 * b + 2)
                v.tensor_tensor(x2[:, :, :], x2[:, :, :], xr[:, :, :], ALU.add).then_inc(s_x2, 1)
                dve.wait_ge(s_x2, b + 1)
                stats(b, x2, bn2, mv2, s_bn2, s_mv2)

            def normalise2(b):
                dve.wait_ge(s_rs2, b + 1)
                if some(16 * TOPK * TT * b):
                    dve.wait_ge(s_disp, 16 * TOPK * TT * b)
                for t in range(TT):
                    last = v.tensor_scalar(h2[:, t, :], x2[:, t, :], mv2[:, t, 0:1], rstd2[:, t:t + 1],
                                           ALU.subtract, ALU.mult)
                last.then_inc(s_xn2, 1)

            def choose(b):
                dve.wait_ge(s_lp, b + 1)
                v.tensor_copy(lg[:, :, :], pM[:, 0, 0:TT * EXPERTS].rearrange("p (t e) -> p t e", e=EXPERTS)).then_inc(s_lg, 1)
                needed = held(dve, b + 1)
                dve.wait_ge(s_lg, 1)
                dve.wait_ge(s_lg, needed)
                for t in range(TT):
                    v.max(v8[:, t, :], lg[:, t, :]).then_inc(s_v8, 1)
                for t in range(TT):
                    needed = held(dve, TT * b + t + 1)
                    dve.wait_ge(s_v8, 1)
                    dve.wait_ge(s_v8, needed)
                    v.max_index(i8[:, t, :], v8[:, t, :], lg[:, t, :]).then_inc(s_i8, 1)
                top = v8[:, :, 0:1]
                v.tensor_tensor(ex[:, :, 0:EXPERTS], lg[:, :, :], top.broadcast_to([P, TT, EXPERTS]),
                                ALU.subtract).then_inc(s_dx, 1)
                v.tensor_tensor(ex[:, :, EXPERTS:], v8[:, :, 0:TOPK], top.broadcast_to([P, TT, TOPK]),
                                ALU.subtract).then_inc(s_dx, 1)
                dve.wait_ge(s_i8, TT * b + TT)
                v.tensor_copy(if8[:, :, :], i8[:, :, 0:TOPK]).then_inc(s_if, 1)
                dve.wait_ge(s_if, b + 1)
                for k in range(TOPK):
                    v.tensor_tensor(oh[:, k, :, :],
                                    cst[:, C_E8:C_E8 + 8].unsqueeze(1).broadcast_to([P, TT, EXPERTS]),
                                    if8[:, :, k:k + 1].broadcast_to([P, TT, EXPERTS]), ALU.is_equal).then_inc(s_oh, 1)
                dve.wait_ge(s_oh, TOPK * (b + 1))
                v.tensor_tensor(ohs[:, :, :], oh[:, 0, :, :], oh[:, 1, :, :], ALU.add).then_inc(s_ohs, 1)
                dve.wait_ge(s_ex8, b + 1)
                v.tensor_reduce(sume[:, :], ex[:, :, 0:EXPERTS], AX.X, ALU.add).then_inc(s_su, 1)
                dve.wait_ge(s_su, b + 1)
                v.reciprocal(rsum[:, :], sume[:, :]).then_inc(s_rsu, 1)
                dve.wait_ge(s_rsu, b + 1)
                v.tensor_tensor(gate_all[:, bass.ds(b, 1), :].rearrange("p a (t k) -> p (a t) k", k=TOPK),
                                ex[:, :, EXPERTS:], rsum[:, :].unsqueeze(2).broadcast_to([P, TT, TOPK]),
                                ALU.mult).then_inc(s_gt, 1)
                dve.wait_ge(s_px, b + 1)
                v.tensor_copy(base[:, 0, :], base[:, TT, :]).then_inc(s_ba, 1)
                for t in range(TT):
                    dve.wait_ge(s_ba, 5 * b + 2 + t)
                    tot = pM[:, 1, (TT + t) * EXPERTS:(TT + t + 1) * EXPERTS]
                    v.tensor_tensor(base[:, t + 1, :], tot, base[:, t, :], ALU.add).then_inc(s_ba, 1)
                dve.wait_ge(s_ba, 5 * b + 1 + TT)
                v.tensor_tensor(posb[:, :, :], pM[:, 1, 0:TT * EXPERTS].rearrange("p (t e) -> p t e", e=EXPERTS),
                                base[:, 0:TT, :], ALU.add).then_inc(s_pb, 1)
                dve.wait_ge(s_pb, b + 1)
                v.tensor_tensor(posm[:, :, :, :].rearrange("p k t e -> p k (t e)"),
                                oh[:, :, :, :].rearrange("p k t e -> p k (t e)"),
                                posb[:, :, :].rearrange("p t e -> p (t e)").unsqueeze(1)
                                .broadcast_to([P, TOPK, TT * EXPERTS]), ALU.mult).then_inc(s_pm, 1)
                dve.wait_ge(s_pm, b + 1)
                v.tensor_reduce(posf[:, :, :].rearrange("p k t -> p (k t)"),
                                posm[:, :, :, :].rearrange("p k t e -> p (k t) e"), AX.X, ALU.add).then_inc(s_pf, 1)
                dve.wait_ge(s_pf, b + 1)
                v.tensor_copy(slot[:, :, :], posf[:, :, :]).then_inc(s_sl, 1)
                v.tensor_copy(slotf_all[:, bass.ds(b, 1), :],
                              posf[:, :, :].rearrange("p k t -> p (k t)").unsqueeze(1)).then_inc(s_sla, 1)

            dve.wait_ge(s_b0, 6)
            stats1(0)
            normalise1(0)

            def body(b):
                if tail(b):
                    sums(b - 1)
                if head(b):
                    softmax(b, 0)
                if tail(b):
                    divide(b - 1)
                if head(b):
                    softmax(b, 1)
                if following(b):
                    stats1(b + 1)
                if head(b):
                    softmax(b, 2)
                if following(b):
                    normalise1(b + 1)
                if tail(b):
                    residual(b - 1)
                    normalise2(b - 1)
                if head(b):
                    softmax(b, 3)
                if tail(b):
                    choose(b - 1)

            over_batches(dve, body)

            tab = [0]

            def did(op):
                tab[0] += 1
                op.then_inc(s_tab, 1)
                dve.wait_ge(s_tab, tab[0])

            dve.wait_ge(s_ba, 5 * BATCH + 1)
            dve.wait_ge(s_x2st, 16 * BATCH)
            dve.wait_ge(s_sla, BATCH)
            count, ntile, shift, cum = (tb8[:, i, :] for i in range(4))
            did(v.tensor_scalar(tailf[:, :], base[:, TT, :], cst[:, C_PART:C_PART + 1], None, ALU.add))
            did(v.tensor_copy(taili[:, :], tailf[:, :]))
            did(v.tensor_tensor(count, base[:, TT, :], cst[:, C_CAP:C_CAP + 8], ALU.subtract))
            did(v.tensor_scalar(nti[:, :], count, P / 2 - 0.5, 1.0 / P, ALU.add, ALU.mult))
            did(v.tensor_copy(ntile, nti[:, :]))
            did(v.tensor_tensor_scan(cumf[:, :], ones[:, 0:EXPERTS], ntile, 0.0, ALU.mult, ALU.add))
            did(v.tensor_scalar(cumi[:, :], cumf[:, :], 1.0, None, ALU.add))
            tile_no = cst[:, C_TILE:C_TILE + TILES]
            did(v.tensor_tensor(ind[:, :, :], tile_no.unsqueeze(2).broadcast_to([P, TILES, EXPERTS]),
                                cumf[:, :].unsqueeze(1).broadcast_to([P, TILES, EXPERTS]), ALU.is_ge))
            did(v.tensor_scalar(shift, ntile, -float(P), float(CAP), ALU.mult, ALU.add))
            did(v.tensor_tensor(indw[:, :, :], ind[:, :, :],
                                shift.unsqueeze(1).broadcast_to([P, TILES, EXPERTS]), ALU.mult))
            did(v.tensor_reduce(tabf[:, 0, :], indw[:, :, :], AX.X, ALU.add))
            did(v.tensor_reduce(tabf[:, 1, :], ind[:, :, :], AX.X, ALU.add))
            did(v.scalar_tensor_tensor(tabf[:, 2, :], tile_no, float(P), tabf[:, 0, :], ALU.mult, ALU.add))
            did(v.tensor_scalar(tabi[:, 0, :], tabf[:, 2, :], float(EXPERTS * CAP), None, ALU.min))
            did(v.tensor_scalar(tabf[:, 3, :], tabf[:, 1, :], EXPERTS - 1.0, None, ALU.min))
            did(v.tensor_copy(tabi[:, 1, :], tabf[:, 3, :]))
            did(v.tensor_scalar(tabi[:, 2, :], tabf[:, 3, :], 48.0, 48.0, ALU.mult, ALU.add))
            did(v.tensor_scalar(tabi[:, 3, :], tabi[:, 1, :], 1, None, ALU.bitwise_and))
            slots = slotf_all[:, :, :].rearrange("p b n -> p (b n)")
            N = BATCH * TOPK * TT
            did(v.tensor_scalar(tb8[:, 4, :], cst[:, C_CAP:C_CAP + 8], float(CAP), None, ALU.add))
            did(v.tensor_tensor(past, slots.unsqueeze(2).broadcast_to([P, N, EXPERTS]),
                                tb8[:, 4:5, :].broadcast_to([P, N, EXPERTS]), ALU.is_ge))
            did(v.tensor_tensor(pastw, past, shift.unsqueeze(1).broadcast_to([P, N, EXPERTS]), ALU.mult))
            lower = x2[:, 0, 0:N]
            did(v.tensor_reduce(lower, pastw, AX.X, ALU.add))
            did(v.tensor_tensor(slot_all[:, :, :].rearrange("p b n -> p (b n)"), slots, lower, ALU.subtract))
            v.memset(tb8[:, 5, :], 0.0).then_inc(s_m2, 1)

            def take_rows(j):
                dve.wait_ge(s_tx, j + 1)
                if some(j):
                    dve.wait_ge(s_m1, j)
                v.tensor_copy(xT[:, :, :], pXY[:, 0, 0:D].rearrange("p (k n) -> p k n", k=KD)).then_inc(s_xT, 1)

            def gated(j):
                dve.wait_ge(s_gl, j + 1)
                dve.wait_ge(s_m1, j + 1)
                if some(j):
                    dve.wait_ge(s_th, j)
                v.tensor_tensor(hh[:, :, :], p13[1][:, :, 0:FF // 2], gg[:, :, :], ALU.mult).then_inc(s_mu, 1)

            def result(j, n, pair):
                dve.wait_ge(s_m2, j + 2)
                if some(16 * pair):
                    dve.wait_ge(s_yst[n], 16 * pair)
                v.tensor_copy(ysb[:, n, :], pXY[:, 1, 0:D]).then_inc(s_yv, 1)

            take_rows(0)
            gated(0)
            take_rows(1)

            def tiles(pair):
                for i in range(2):
                    gated(pair * 2 + (i + 1))
                    result(pair * 2 + i, i, pair)
                    take_rows(pair * 2 + (i + 2))

            tiles(0)
            with dve.Fori(1, TILES // 2 - 1) as pair:
                tiles(pair)
            gated(TILES - 1)
            result(TILES - 2, 0, TILES // 2 - 1)
            result(TILES - 1, 1, TILES // 2 - 1)

            def indices(b, n, pair):
                if some(16 * TOPK * TT * pair):
                    dve.wait_ge(s_yg[n], 16 * TOPK * TT * pair)
                v.tensor_copy(gidx[:, n:n + 1, :], slot_all[:, bass.ds(b, 1), :]).then_inc(s_ix, 1)

            def finish(b, n, pair):
                dve.wait_ge(s_xf[n], 32 * (pair + 1))
                v.tensor_tensor(xf[:, n, :, :], xf[:, n, :, :],
                                frow[:, n, 1:2, :].broadcast_to([P, TT, D]), ALU.add).then_inc(s_fd, 1)
                dve.wait_ge(s_yg[n], 16 * TOPK * TT * (pair + 1))
                if some(16 * pair):
                    dve.wait_ge(s_out[n], 16 * pair)
                for t in range(TT):
                    v.tensor_scalar(of[:, n, t, :], yg[:, n, t, :],
                                    gate_all[:, bass.ds(b, 1), TOPK * t:TOPK * t + 1].rearrange("p a n -> p (a n)"),
                                    None, ALU.mult).then_inc(s_fa, 1)
                for t in range(TT):
                    dve.wait_ge(s_fa, TT * b + t + 1)
                    v.scalar_tensor_tensor(of[:, n, t, :], yg[:, n, TT + t, :],
                                           gate_all[:, bass.ds(b, 1), TOPK * t + 1:TOPK * t + 2].rearrange("p a n -> p (a n)"),
                                           of[:, n, t, :], ALU.mult, ALU.add).then_inc(s_fb, 1)
                dve.wait_ge(s_fb, TT * (b + 1))
                v.tensor_tensor(of[:, n, :, :], of[:, n, :, :],
                                frow[:, n, 0:1, :].broadcast_to([P, TT, D]), ALU.mult).then_inc(s_fc, 1)
                dve.wait_ge(s_fc, b + 1)
                v.tensor_tensor(of[:, n, :, :], of[:, n, :, :], xf[:, n, :, :], ALU.add).then_inc(s_f, 1)

            for n in range(2):
                dve.wait_ge(s_yst[n], 8 * TILES)
            for n in range(2):
                indices(n, n, 0)
            for n in range(2):
                finish(n, n, 0)
                indices(n + 2, n, 1)
            with dve.Fori(1, BATCH // 2 - 1) as pair:
                for n in range(2):
                    finish(pair * 2 + n, n, pair)
                    indices(pair * 2 + (n + 2), n, pair + 1)
            for n in range(2):
                finish(BATCH - 2 + n, n, BATCH // 2 - 1)


def constants():
    import numpy as np
    c = np.zeros((P, C_END), np.float32)
    r = np.arange(P)
    c[:, C_ID:C_ID + P] = np.eye(P)
    c[:, C_TRI:C_TRI + P] = r[:, None] < r[None, :]
    row, col = r[:, None] % 32, np.arange(32)[None, :]
    same = row // 16 == col // 16
    c[:, C_M0:C_M0 + 32] = np.where(same & (col <= row), 0.0, -1e30)
    c[:, C_M1:C_M1 + 32] = np.where(same, 0.0, -1e30)
    c[:, C_M2:C_M2 + 32] = np.where(np.where(r[:, None] < 96, same, col < 16), 0.0, -1e30)
    level = np.array([2, 2, 3, 4])[r // 32]
    c[:, C_SC2] = DH ** -0.5 / 4.0 ** level
    c[:, C_E8:C_E8 + 8] = np.arange(8)
    c[:, C_CAP:C_CAP + 8] = np.arange(8) * CAP
    c[:, C_TILE:C_TILE + TILES] = np.arange(TILES)
    c[:, C_PART] = r
    sel = np.zeros((HEADS, 8, P), np.float32)
    for h in range(HEADS):
        sel[h, h // 2, (h % 2) * DH:(h % 2 + 1) * DH] = 1.0
    return c, sel


def kernel(**inputs):
    import numpy as np
    import concourse.bacc as bacc
    from concourse.bass_utils import run_bass_kernel_spmd

    def chunks(w):
        k = w.shape[0] // P
        return np.ascontiguousarray(w.reshape(k, P, -1).transpose(1, 0, 2))

    a = {n: np.asarray(v) for n, v in inputs.items()}
    c, sel = constants()
    up = np.concatenate([a["L0_ffn_w1"], a["L0_ffn_v1"]], axis=2)
    arrays = {
        "x": np.ascontiguousarray(a["L0_attn_x"].reshape(TOKENS, D)),
        "cT": chunks(a["L0_c"].T),
        "wmod": chunks(a["L0_wmod"]),
        "wqkv": chunks(a["L0_attn_w_qkv"].T),
        "wout": chunks(a["L0_attn_w_out"].T),
        "b_out": a["L0_attn_b_out"],
        "router": chunks(a["L0_ffn_router_w"]),
        "w13": np.ascontiguousarray(up.reshape(EXPERTS, KD, P, FF2).transpose(0, 2, 1, 3).reshape(EXPERTS, P, KD * FF2)),
        "w2": np.ascontiguousarray(a["L0_ffn_w2"]),
        "ffn_bias": a["L0_ffn_bias"],
        "consts": c,
        "sel": sel,
    }
    nc = bacc.Bacc("TRN2", target_bir_lowering=False, num_devices=1)
    args = [nc.dram_tensor(n, v.shape, F32, kind="ExternalInput").ap() for n, v in arrays.items()]
    out = nc.dram_tensor("out", (TOKENS, D), F32, kind="ExternalOutput").ap()
    build(nc, *args, out)
    r = run_bass_kernel_spmd(nc, [arrays], core_ids=[0])
    return r.results[0]["out"].reshape(BATCH, SEQ, D)
```

```python
from contextlib import ExitStack

import concourse.bass as bass
from concourse import mybir

F32 = mybir.dt.float32
F32R = mybir.dt.float32r
I32 = mybir.dt.int32
U32 = mybir.dt.uint32
ALU = mybir.AluOpType
ACT = mybir.ActivationFunctionType
AX = mybir.AxisListType

P = 128
BATCH, SEQ, D = 8, 512, 256
KD = D // P
TT = SEQ // P
TOKENS = BATCH * SEQ
HEADS, DH = 16, 64
INNER = HEADS * DH
GROUPS = 4
UNITS = TT + 2
EXPERTS, TOPK, FF = 8, 2, 704
FF2 = 2 * FF
FC = 6
FTAIL = FF - 5 * P
CAP = TOKENS + P
SLOTS = EXPERTS * CAP + P
TILES = 72
LN_EPS, SUM_EPS = 1e-5, 1e-8

C_ID, C_TRI = 0, P
C_M0, C_M1, C_M2 = 2 * P, 2 * P + 32, 2 * P + 64
C_SC2 = 2 * P + 96
C_E8 = C_SC2 + 1
C_CAP = C_E8 + 8
C_TILE = C_CAP + 8
C_END = C_TILE + TILES

W13, W2 = KD * FF2, FC * D
SLOT = 2 * W13 + 2 * W2

JOBS = 7 * GROUPS + KD


def some(count):
    return not (isinstance(count, int) and count <= 0)


def held(eng, count):
    return count if isinstance(count, int) else eng.to_reg(count)


def f32(ap):
    return ap.bitcast(F32)


def parts(stationary, moving):
    return ((stationary[0], moving[0]), (stationary[0], moving[1]), (stationary[1], moving[0]))


def job_x(b, k):
    return b * JOBS + k


def job(b, g, i):
    return b * JOBS + (KD + 7 * g + i)


def build(nc, x, cT, wmod, wqkv, wout, b_out, router, w13, w2, ffn_bias, consts, sel, out):
    rows_dram = nc.dram_tensor("mod_rows", [BATCH, 6, D], F32, kind="Internal").ap()
    x2_dram = nc.dram_tensor("x_after_attention", [TOKENS, D], F32, kind="Internal").ap()
    xs_dram = nc.dram_tensor("dispatched_rows", [SLOTS, D], F32, kind="Internal").ap()
    ys_dram = nc.dram_tensor("expert_rows", [TILES * P, D], F32, kind="Internal").ap()

    ctx = ExitStack()
    with ctx:
        def sb(name, shape, dt=F32):
            return ctx.enter_context(nc.sbuf_tensor(name, shape, dt))

        def pb(name, shape):
            return ctx.enter_context(nc.psum_tensor(name, shape, F32))

        def sem(name):
            return ctx.enter_context(nc.semaphore(name))

        cst = sb("cst", [P, C_END])
        sel_sb = sb("sel_sb", [HEADS, 8, P])
        ones = sb("ones", [P, P])
        halfneg = sb("halfneg", [P, TT])
        big = sb("big", [P, 2 * SLOT], F32R)
        work = sb("work", [P, 2 * UNITS * 4 * DH + 4 * SEQ])
        WQ = KD * 3 * INNER
        wq_h, wq_l = (big[:, i * WQ:(i + 1) * WQ].rearrange("p (k n) -> p k n", k=KD) for i in range(2))
        assert WQ <= SLOT
        V = work[:, 0:2 * UNITS * 4 * DH].rearrange("p (s u n) -> p s u n", s=2, u=UNITS)
        at_q = 2 * UNITS * 4 * DH
        qT, kT = (work[:, at_q + i * 2 * SEQ:at_q + (i + 1) * 2 * SEQ].rearrange("p (c n) -> p c n", c=2)
                  for i in range(2))
        wout_sb = sb("wout_sb", [P, 8, D])
        rout_sb = sb("rout_sb", [P, KD, EXPERTS])
        cT_sb = sb("cT_sb", [P, KD, BATCH])
        sil = sb("sil", [P, KD, BATCH])
        siT = sb("siT", [P, KD, BATCH])
        modT = sb("modT", [P, 2 * KD, BATCH])
        ident = cst[:, C_ID:C_ID + P]
        x_sb = sb("x_sb", [P, TT, D])
        bn1 = sb("bn1", [P, TT, 6])
        mv1 = sb("mv1", [P, TT, 2])
        rstd1 = sb("rstd1", [P, TT])
        hT = sb("hT", [P, KD, SEQ])
        hP = [sb(f"hP{n}", [P, KD, SEQ >> n]) for n in (1, 2, 3)]
        hT_h, hT_l = sb("hT_h", [P, KD, SEQ], F32R), sb("hT_l", [P, KD, SEQ], F32R)
        hC = sb("hC", [P, KD, 2 * P])
        hC_l = sb("hC_l", [P, KD, 2 * P], F32R)
        hC_h = sb("hC_h", [P, KD, 2 * P], F32R)
        qP = [sb(f"qP{n}", [P, 2, SEQ >> n]) for n in (1, 2, 3)]
        qC = sb("qC", [P, 2, 2 * P])
        kP = [sb(f"kP{n}", [P, 2, SEQ >> n]) for n in (1, 2, 3, 4)]
        sm = sb("sm", [P, 2, UNITS * 2 * 32])
        mx = sb("mx", [P, 2, UNITS * 2])
        rs = sb("rs", [P, UNITS, HEADS])
        rs_done = sb("rs_done", [P, UNITS, HEADS])
        AT = sb("AT", [P, 2, 5 * 2, P])
        MG = sb("MG", [P, 2, 2, P + 64])
        YT = sb("YT", [P, 8, SEQ])
        YN = sb("YN", [P, 8, SEQ])
        den = sb("den", [HEADS, SEQ])
        rows = sb("rows", [P, 4, D])
        xr = sb("xr", [P, TT, D])
        x2 = sb("x2", [P, TT, D])
        bn2 = sb("bn2", [P, TT, 6])
        mv2 = sb("mv2", [P, TT, 2])
        rstd2 = sb("rstd2", [P, TT])
        h2 = sb("h2", [P, TT, D])
        mrow = [x2[0:BATCH, r, :] for r in range(4)] + [h2[0:BATCH, r, :] for r in range(2)]
        bo_row = h2[0:BATCH, 2:4, :]
        mtmp = xr[0:BATCH, 0:2, :]
        h2T = xr[:, :, :].rearrange("p t n -> p (t n)").rearrange("p (k n) -> p k n", k=KD)
        lg = sb("lg", [P, TT, EXPERTS])
        v8 = sb("v8", [P, TT, 8])
        i8 = sb("i8", [P, TT, 8], U32)
        if8 = sb("if8", [P, TT, TOPK])
        ex = sb("ex", [P, TT, EXPERTS + TOPK])
        sume = sb("sume", [P, TT])
        rsum = sb("rsum", [P, TT])
        oh = sb("oh", [P, TOPK, TT, EXPERTS])
        ohs = sb("ohs", [P, TT, EXPERTS])
        base = sb("base", [P, TT + 1, EXPERTS])
        posb = sb("posb", [P, TT, EXPERTS])
        posm = sb("posm", [P, TOPK, TT, EXPERTS])
        posf = sb("posf", [P, TOPK, TT])
        slot = sb("slot", [P, TOPK, TT], I32)
        slotf_all = sb("slotf_all", [P, BATCH, TOPK * TT])
        gate_all = sb("gate_all", [P, BATCH, TT * TOPK])
        zrow = sb("zrow", [P, D])
        tb8 = rows[:, 0, 2 * TILES:2 * TILES + 6 * EXPERTS].rearrange("p (i e) -> p i e", e=EXPERTS)
        past, pastw = (buf[:, 0, 0:512].rearrange("p (n e) -> p n e", e=EXPERTS) for buf in (h2T, YN))
        ind, indw = (buf[:, :, :].rearrange("p t n -> p (t n)")[:, 0:TILES * EXPERTS]
                     .rearrange("p (t e) -> p t e", e=EXPERTS) for buf in (xr, x_sb))
        tabf = rows[:, :, 0:TILES]
        tabi = rows[:, :, TILES:2 * TILES].bitcast(I32)
        cumf = rows[:, 2, 2 * TILES:2 * TILES + EXPERTS]

        wq_raw = [buf[:, at:at + 3, :].rearrange("p a n -> p (a n)").rearrange("p (k s n) -> p k s n", k=KD, s=3)
                  for buf, at in ((YN, 0), (YN, 3), (YT, 0), (YT, 3))]
        xs = YT[:, 0:1, :].rearrange("p a (b n) -> p (a b) n", b=2)
        xT_h, xT_l = (buf[:, :, :].rearrange("p k n -> p (k n)").rearrange("p (n k c) -> p n k c", n=2, k=KD)
                      for buf in (hC_h, hC_l))
        hh_flat = YT[:, 4:6, :].rearrange("p a n -> p (a n)")[:, 0:FC * P]
        gg = YT[:, 2:4, :].rearrange("p a n -> p (a n)")[:, 0:FF].rearrange("p (a n) -> p a n", a=2)
        ints = x2[:, 1, :].bitcast(I32)
        slot_all = ints[:, 0:BATCH * TOPK * TT].rearrange("p (b n) -> p b n", b=BATCH)
        gidx = ints[:, 64:64 + 2 * TOPK * TT].rearrange("p (b n) -> p b n", b=2)
        endi, nti, cumi = (rows[:, 3, 2 * TILES + i * EXPERTS:2 * TILES + (i + 1) * EXPERTS].bitcast(I32) for i in range(3))
        w13_raw, w2_raw = work[:, 0:W13], work[:, W13:W13 + W2]
        hh = hh_flat[:, 0:FF].rearrange("p (a n) -> p a n", a=2)
        hid_h, hid_l = (buf[:, :, 0:3 * P].rearrange("p a (c n) -> p a c n", c=3) for buf in (hT_h, hT_l))
        ysb = YN[:, 2, :].rearrange("p (b n) -> p b n", b=2)
        yg = YN[:, :, :].rearrange("p (a b) (c n) -> p a (b c) n", a=2, c=2)
        xf = YT[:, 0:4, :].rearrange("p (a b) (c n) -> p a (b c) n", a=2, c=2)
        of = YT[:, 4:8, :].rearrange("p (a b) (c n) -> p a (b c) n", a=2, c=2)
        frow = hT[:, :, :].rearrange("p n (r d) -> p n r d", r=2)

        pA = pb("pA", [P, 2, SEQ])
        pS = pb("pS", [P, 2, SEQ])
        pY = pb("pY", [P, 2, SEQ])
        pM = pb("pM", [P, 2, SEQ])
        p13 = [pA, pS]
        pH, pXY = pY, pM

        s_cm = sem("s_cm")
        s_cst = sem("s_cst")
        s_wq = [sem(f"s_wq{g}") for g in range(GROUPS)]
        s_late = sem("s_late")
        s_zeros = sem("s_zeros")
        s_wqh, s_wql = sem("s_wqh"), sem("s_wql")
        s_hh, s_hl, s_hch, s_hcl = (sem("s_" + n) for n in ("hh", "hl", "hch", "hcl"))
        s_wh, s_wl = sem("s_wh"), sem("s_wl")
        s_pad = sem("s_pad")
        s_b0 = sem("s_b0")
        s_silu = sem("s_silu")
        s_modp = sem("s_modp")
        s_mod = sem("s_mod")
        s_modst = sem("s_modst")
        s_xin = sem("s_xin")
        s_bn1, s_mv1, s_ve1, s_rs1, s_xn = (sem("s_" + n) for n in ("bn1", "mv1", "ve1", "rs1", "xn"))
        s_pj = sem("s_pj")
        s_pe = sem("s_pe")
        s_hp = sem("s_hp")
        s_qk = sem("s_qk")
        s_sc, s_mk, s_mx, s_sb_, s_ex = ([sem(f"s_{n}{i}") for i in range(2)] for n in ("sc", "mk", "mx", "sb", "ex"))
        s_rs, s_rsd = sem("s_rs"), sem("s_rsd")
        s_at = sem("s_at")
        s_y = sem("s_y")
        s_ye = sem("s_ye")
        s_rt, s_dn, s_rd, s_bc, s_yn = (sem("s_" + n) for n in ("rt", "dn", "rd", "bc", "yn"))
        s_rows, s_xres, s_xrb = sem("s_rows"), sem("s_xres"), sem("s_xrb")
        s_op, s_xg, s_x2, s_x2st = (sem("s_" + n) for n in ("op", "xg", "x2", "x2st"))
        s_bn2, s_mv2, s_ve2, s_rs2, s_xn2, s_hm, s_h2 = (
            sem("s_" + n) for n in ("bn2", "mv2", "ve2", "rs2", "xn2", "hm", "h2"))
        s_t2, s_t2e, s_lp, s_lg, s_v8, s_i8 = (sem("s_" + n) for n in ("t2", "t2e", "lp", "lg", "v8", "i8"))
        s_dx, s_ex8, s_su, s_rsu, s_gt, s_if, s_oh, s_ohs = (
            sem("s_" + n) for n in ("dx", "ex8", "su", "rsu", "gt", "if", "oh", "ohs"))
        s_px, s_ba, s_pb, s_pm, s_pf, s_sl, s_sla, s_disp = (
            sem("s_" + n) for n in ("px", "ba", "pb", "pm", "pf", "sl", "sla", "disp"))
        s_tab = sem("s_tab")
        s_zero = sem("s_zero")
        s_win, s_win2 = sem("s_win"), sem("s_win2")
        s_xh, s_hdh = sem("s_xh"), sem("s_hdh")
        s_tx, s_xT, s_m1, s_gl, s_mu, s_th, s_hT, s_m2, s_yv = (
            sem("s_" + n) for n in ("tx", "xT", "m1", "gl", "mu", "th", "hT", "m2", "yv"))
        s_xs, s_yst, s_yg, s_xf, s_out = ([sem(f"s_{n}{i}") for i in range(2)] for n in ("xs", "yst", "yg", "xf", "out"))
        s_ix, s_fa, s_fb, s_fc, s_fd, s_f = (
            sem("s_" + n) for n in ("ix", "fa", "fb", "fc", "fd", "f"))

        block = ctx.enter_context(nc.Block())

        NMOD = 14
        NTAB = 17

        def of_group(w, g):
            return w.rearrange("p k (s n) -> p k s n", s=3)[:, :, :, g * 4 * DH:(g + 1) * 4 * DH]

        def slot_parts(n):
            at = n * SLOT
            return (big[:, at:at + W13], big[:, at + W13:at + 2 * W13],
                    big[:, at + 2 * W13:at + 2 * W13 + W2], big[:, at + 2 * W13 + W2:at + SLOT])

        def load_weights(eng, e, arrived):
            eng.dma_start(w13_raw, w13[bass.ds(e, 1), :, :].rearrange("a p n -> (a p) n")).then_inc(arrived, 16)
            src = w2[bass.ds(e, 1), :, :].rearrange("a f n -> (a f) n")
            eng.dma_start(w2_raw[:, 0:5 * D].rearrange("p (c n) -> p c n", c=5),
                          src[0:5 * P, :].rearrange("(c p) n -> p c n", p=P)).then_inc(arrived, 16)
            eng.dma_start(w2_raw[0:FTAIL, 5 * D:6 * D], src[5 * P:FF, :]).then_inc(arrived, 16)

        PIECES = (slice(0, 2 * TT * 32), slice(2 * TT * 32, 2 * UNITS * 32))

        def x_rows(b):
            return x[bass.ds(b * SEQ, SEQ), :].rearrange("(t p) d -> p t d", p=P)

        def over_batches(eng, body):
            body(0)
            body(1)
            with eng.Fori(2, BATCH - 1) as b:
                body(b)
            body(BATCH - 1)
            body(BATCH)
            body(BATCH + 1)

        def head(b):
            return not (isinstance(b, int) and b >= BATCH)

        def tail(b):
            return not (isinstance(b, int) and not 1 <= b <= BATCH)

        def late(b):
            return not (isinstance(b, int) and b < 2)

        def following(b):
            return not (isinstance(b, int) and b >= BATCH - 1)

        @block.sync
        def _(sp):
            sp.dma_start(cT_sb[:, :, :], cT).then_inc(s_cm, 16)
            sp.dma_start(x_sb[:, :, :], x_rows(0)).then_inc(s_xin, 16)
            sp.dma_start(YT[:, 0:6, :].rearrange("p (k a) n -> p k (a n)", k=KD), wmod).then_inc(s_cm, 16)
            for dst, src in ((cst[:, :], consts),
                             (bo_row[:, 0, :], b_out.partition_broadcast(BATCH)),
                             (bo_row[:, 1, :], ffn_bias.partition_broadcast(BATCH))):
                sp.dma_start(dst, src).then_inc(s_cst, 16)
            for g in range(GROUPS):
                if g == 2:
                    sp.wait_ge(s_modp, 1)
                for k in range(KD):
                    sp.dma_start(wq_raw[g][:, k, :, :], of_group(wqkv, g)[:, k, :, :]).then_inc(s_wq[g], 16)
            for dst, src in ((sel_sb[:, :, :], sel), (rout_sb[:, :, :], router), (wout_sb[:, :, :], wout)):
                sp.dma_start(dst, src).then_inc(s_late, 16)
            sp.wait_ge(s_b0, 6)
            sp.dma_start(xs_dram[EXPERTS * CAP:SLOTS, :], zrow[:, :]).then_inc(s_zeros, 16)
            sp.wait_ge(s_mod, NMOD)
            sp.dma_start(rows_dram[:, 0:4, :], x2[0:BATCH, :, :]).then_inc(s_modst, 16)
            sp.dma_start(rows_dram[:, 4:6, :], h2[0:BATCH, 0:2, :]).then_inc(s_modst, 16)
            sp.wait_ge(s_modst, 32)

            def body(b):
                if following(b):
                    sp.wait_ge(s_pj, job_x(b, KD - 1) + 1)
                    sp.dma_start(x_sb[:, :, :], x_rows(b + 1)).then_inc(s_xin, 16)
                if tail(b):
                    if some(b - 1):
                        sp.wait_ge(s_lp, b - 1)
                    sp.dma_start(xr[:, :, :], x_rows(b - 1)).then_inc(s_xres, 16)
                    if some(b - 1):
                        sp.wait_ge(s_h2, b - 1)
                    sp.dma_start(rows[:, :, :],
                                 rows_dram[bass.ds(b - 1, 1), 0:4, :].rearrange("a r n -> (a r) n")
                                 .partition_broadcast(P)).then_inc(s_rows, 16)
                    if isinstance(b, int) and b == BATCH:
                        sp.wait_ge(s_pad, 1)
                        load_weights(sp, 0, s_win)
                    sp.wait_ge(s_x2, b)
                    sp.dma_start(x2_dram[bass.ds((b - 1) * SEQ, SEQ), :].rearrange("(t p) d -> p t d", p=P),
                                 x2[:, :, :]).then_inc(s_x2st, 16)

            over_batches(sp, body)
            sp.wait_ge(s_tab, 1)
            for e in range(EXPERTS):
                end = sp.value_load(endi[0:1, e:e + 1], min_val=e * CAP, max_val=e * CAP + TOKENS)
                sp.dma_start(xs_dram[bass.ds(end, P), :], zrow[:, :]).then_inc(s_zero, 16)
            sp.wait_ge(s_wl, 2)
            load_weights(sp, 1, s_win)
            sp.wait_ge(s_disp, 16 * BATCH * TOPK * TT)
            sp.wait_ge(s_zero, 16 * EXPERTS)
            sp.wait_ge(s_zeros, 16)
            sp.wait_ge(s_tab, NTAB)
            sp.wait_ge(s_op, 2 * BATCH)

            def load_rows(j, n):
                row = sp.value_load(tabi[0:1, 0, bass.ds(j, 1)], min_val=0, max_val=EXPERTS * CAP)
                sp.dma_start(xs[:, n, :], xs_dram[bass.ds(row, P), :]).then_inc(s_xs[n], 16)

            load_rows(0, 0)
            load_rows(1, 1)
            with sp.Fori(0, TILES // 2 - 1) as pair:
                for n in range(2):
                    sp.wait_ge(s_tx, pair * 2 + (n + 1))
                    load_rows(pair * 2 + (n + 2), n)
            for n in range(2):
                sp.wait_ge(s_yst[n], 8 * TILES)
            sp.wait_ge(s_x2st, 16 * BATCH)
            def load_last(b, n):
                sp.dma_start(xf[:, n, :, :],
                             x2_dram[bass.ds(b * SEQ, SEQ), :].rearrange("(t p) d -> p t d", p=P)).then_inc(s_xf[n], 16)
                sp.dma_start(frow[:, n, :, :],
                             rows_dram[bass.ds(b, 1), 4:6, :].rearrange("a r n -> (a r) n")
                             .partition_broadcast(P)).then_inc(s_xf[n], 16)

            def store_last(b, n):
                sp.wait_ge(s_f, b + 1)
                sp.dma_start(out[bass.ds(b * SEQ, SEQ), :].rearrange("(t p) d -> p t d", p=P),
                             of[:, n, :, :]).then_inc(s_out[n], 16)

            load_last(0, 0)
            load_last(1, 1)
            with sp.Fori(0, BATCH // 2 - 1) as pair:
                for n in range(2):
                    store_last(pair * 2 + n, n)
                    load_last(pair * 2 + (n + 2), n)
            for n in range(2):
                store_last(BATCH - 2 + n, n)
            for n in range(2):
                sp.wait_ge(s_out[n], 8 * BATCH)

        @block.gpsimd
        def _(pool):
            nc.gpsimd.memset(halfneg[:, :], -0.5).then_inc(s_b0, 1)

            def rstd(b, mv, r, s_mv, s_ve, s_rs_):
                needed = held(pool, TT * b + TT)
                pool.wait_ge(s_mv, 1)
                pool.wait_ge(s_mv, needed)
                nc.gpsimd.tensor_scalar(r[:, :], mv[:, :, 1], LN_EPS, None, ALU.add).then_inc(s_ve, 1)
                pool.wait_ge(s_ve, b + 1)
                nc.gpsimd.tensor_tensor(r[:, :], r[:, :], halfneg[:, :], ALU.pow).then_inc(s_rs_, 1)

            rstd(0, mv1, rstd1, s_mv1, s_ve1, s_rs1)
            nc.gpsimd.memset(zrow[:, :], 0.0).then_inc(s_b0, 1)
            nc.gpsimd.memset(AT[:, :, :, :], 0.0).then_inc(s_b0, 1)
            nc.gpsimd.memset(MG[:, :, :, :], 0.0).then_inc(s_b0, 1)
            nc.gpsimd.memset(rs[:, :, :], 0.0).then_inc(s_b0, 1)
            nc.gpsimd.memset(ones[:, :], 1.0).then_inc(s_b0, 1)

            def halve(dst, src, s):
                nc.gpsimd.tensor_tensor(dst[:, :, :], src[:, :, 0::2], src[:, :, 1::2], ALU.add).then_inc(s, 1)

            def halve_part(dst, lo, n, src, block, s):
                pairs = src[:, :, 0:64 * n].rearrange("p k (n r s) -> p k n r s", r=32, s=2)[:, :, :, 16 * block:16 * block + 16, :]
                nc.gpsimd.tensor_tensor(dst[:, :, lo:lo + 16 * n].rearrange("p k (n r) -> p k n r", r=16),
                                        pairs[:, :, :, :, 0], pairs[:, :, :, :, 1], ALU.add).then_inc(s, 1)

            def pool_h(b):
                pool.wait_ge(s_pe, job_x(b, KD - 1) + 1)
                if tail(b):
                    pool.wait_ge(s_pj, job(b - 1, GROUPS - 1, 6) + 1)
                halve(hP[0], hT, s_hp)
                halve_part(hC, 0, 8, hT, 0, s_hp)
                pool.wait_ge(s_hp, 8 * b + 1)
                halve(hP[1], hP[0], s_hp)
                halve_part(hC, P, 4, hP[0], 0, s_hp)
                pool.wait_ge(s_hp, 8 * b + 3)
                halve(hP[2], hP[1], s_hp)
                halve_part(hC, P + 64, 2, hP[1], 0, s_hp)
                pool.wait_ge(s_hp, 8 * b + 5)
                halve_part(hC, P + 96, 1, hP[2], 0, s_hp)
                halve_part(hC, P + 112, 1, hP[2], 0, s_hp)

            def pool_qk(b, g):
                step = b * GROUPS + g
                pool.wait_ge(s_pe, job(b, g, 3) + 1)
                if some(2 * step):
                    pool.wait_ge(s_sc[1], 2 * step)
                done = 12 * step
                halve(qP[0], qT, s_qk)
                halve(kP[0], kT, s_qk)
                halve_part(qC, 0, 8, qT, 1, s_qk)
                pool.wait_ge(s_qk, done + 2)
                halve(qP[1], qP[0], s_qk)
                halve(kP[1], kP[0], s_qk)
                halve_part(qC, P, 4, qP[0], 1, s_qk)
                pool.wait_ge(s_qk, done + 5)
                halve(qP[2], qP[1], s_qk)
                halve(kP[2], kP[1], s_qk)
                halve_part(qC, P + 64, 2, qP[1], 1, s_qk)
                pool.wait_ge(s_qk, done + 8)
                halve(kP[3], kP[2], s_qk)
                halve_part(qC, P + 96, 1, qP[2], 1, s_qk)
                halve_part(qC, P + 112, 1, qP[2], 1, s_qk)

            def residual(b):
                pool.wait_ge(s_xres, 16 * (b + 1))
                pool.wait_ge(s_rows, 16 * (b + 1))
                nc.gpsimd.tensor_tensor(xr[:, :, :], xr[:, :, :],
                                        rows[:, 1:2, :].broadcast_to([P, TT, D]), ALU.add).then_inc(s_xrb, 1)

            def modulate2(b):
                pool.wait_ge(s_xn2, b + 1)
                nc.gpsimd.tensor_tensor(h2[:, :, :], h2[:, :, :],
                                        rows[:, 2:3, :].broadcast_to([P, TT, D]), ALU.mult).then_inc(s_hm, 1)
                pool.wait_ge(s_hm, b + 1)
                nc.gpsimd.tensor_tensor(h2[:, :, :], h2[:, :, :],
                                        rows[:, 3:4, :].broadcast_to([P, TT, D]), ALU.add).then_inc(s_h2, 1)

            def dispatch(b):
                needed = held(pool, b + 1)
                pool.wait_ge(s_sl, 1)
                pool.wait_ge(s_sl, needed)
                pool.wait_ge(s_h2, b + 1)
                for k in range(TOPK):
                    for t in range(TT):
                        nc.gpsimd.indirect_dma_start(
                            xs_dram, bass.IndirectOffsetOnAxis(ap=slot[:, k, t:t + 1], axis=0),
                            h2[:, t, :], None).then_inc(s_disp, 16)

            def high(dst, raw, s):
                nc.gpsimd.tensor_tensor(dst, raw, zrow[:, 0:1].broadcast_to([P, dst.shape[-1]]),
                                        ALU.add).then_inc(s, 1)

            def low(dst, raw, high_, s):
                nc.gpsimd.tensor_tensor(dst, raw, f32(high_), ALU.subtract).then_inc(s, 1)

            def low_weights(e, n):
                w13_h, w13_l, w2_h, w2_l = slot_parts(n)
                pool.wait_ge(s_wh, 2 * e + 2)
                low(w13_l, w13_raw, w13_h, s_wl)
                low(w2_l, w2_raw, w2_h, s_wl)

            def body(b):
                if head(b):
                    if not tail(b):
                        pool_h(0)
                    pool_qk(b, 0)
                if late(b):
                    dispatch(b - 2)
                if tail(b):
                    residual(b - 1)
                if head(b):
                    pool_qk(b, 1)
                    if following(b):
                        rstd(b + 1, mv1, rstd1, s_mv1, s_ve1, s_rs1)
                    pool_qk(b, 2)
                elif tail(b):
                    pool.wait_ge(s_y, 2 * BATCH * GROUPS)
                    pool.wait_ge(s_qk, 12 * BATCH * GROUPS)
                    pool.wait_ge(s_xrb, BATCH)
                    nc.gpsimd.memset(w2_raw[FTAIL:P, 5 * D:6 * D], 0.0).then_inc(s_pad, 1)
                    pool.wait_ge(s_pad, 1)
                    low_weights(0, 0)
                if tail(b):
                    rstd(b - 1, mv2, rstd2, s_mv2, s_ve2, s_rs2)
                    modulate2(b - 1)
                if head(b):
                    pool_qk(b, 3)
                    if following(b):
                        pool_h(b + 1)

            over_batches(pool, body)
            low_weights(1, 1)

            pool.wait_ge(s_tab, NTAB)

            def weights(e, n):
                w13_h, w13_l, w2_h, w2_l = slot_parts(n)
                last_use = pool.value_load(cumi[0:1, bass.ds(e - 2, 1)], min_val=1, max_val=TILES + 1)
                pool.wait_ge(s_m2, last_use)
                load_weights(pool, e, s_win2)
                pool.wait_ge(s_win2, 48 * e - 48)
                high(w13_h, w13_raw, s_wh)
                high(w2_h, w2_raw, s_wh)
                low_weights(e, n)

            with pool.Fori(1, EXPERTS // 2) as pair:
                weights(pair * 2, 0)
                weights(pair * 2 + 1, 1)
            for n in range(2):
                pool.wait_ge(s_yst[n], 8 * TILES)
            def gather(b, n):
                if some(TT * b - TT):
                    pool.wait_ge(s_fb, TT * b - TT)
                needed = held(pool, b + 1)
                pool.wait_ge(s_ix, 1)
                pool.wait_ge(s_ix, needed)
                for i in range(TOPK * TT):
                    nc.gpsimd.indirect_dma_start(
                        yg[:, n, i, :], None, ys_dram,
                        bass.IndirectOffsetOnAxis(ap=gidx[:, n, i:i + 1], axis=0)).then_inc(s_yg[n], 16)

            gather(0, 0)
            gather(1, 1)
            with pool.Fori(1, BATCH // 2) as pair:
                gather(pair * 2, 0)
                gather(pair * 2 + 1, 1)

        @block.scalar
        def _(act):
            act.wait_ge(s_cm, 32)
            nc.scalar.activation(sil[:, :, :], cT_sb[:, :, :], ACT.Exp, scale=-1.0).then_inc(s_silu, 1)

            def evac(dst, src, src_job):
                act.wait_ge(s_pj, src_job + 1)
                nc.scalar.activation(dst, src, ACT.Copy).then_inc(s_pe, 1)

            def copy(dst, src, s):
                nc.scalar.activation(dst, src, ACT.Copy).then_inc(s, 1)

            def evac_x(b):
                for k in range(KD):
                    act.wait_ge(s_pj, job_x(b, k) + 1)
                    if k == 0 and tail(b):
                        act.wait_ge(s_hp, 8 * b)
                    for dst, done in ((hT_h, s_hh), (hT, s_pe)):
                        nc.scalar.activation(dst[:, k, :], pA[:, k, :], ACT.Identity,
                                             bias=modT[:, k, bass.ds(b, 1)],
                                             scale=modT[:, KD + k, bass.ds(b, 1)]).then_inc(done, 1)

            def exps(step, level, e):
                act.wait_ge(s_sb_[level], 2 * step + e + 1)
                piece = PIECES[level]
                nc.scalar.activation(sm[:, e, piece], sm[:, e, piece], ACT.Exp).then_inc(s_ex[level], 1)

            def results(b, g):
                step = b * GROUPS + g
                for c in range(2):
                    act.wait_ge(s_y, 2 * step + c + 1)
                    if isinstance(step, int) and step == 0:
                        act.wait_ge(s_wql, GROUPS)
                    act.wait_ge(s_yn, 8 * b + 2 * g + c + 1)
                    nc.scalar.activation(YT[:, 2 * g + c, :], pY[:, c, :], ACT.Copy).then_inc(s_ye, 1)

            act.wait_ge(s_mod, 2)
            evac_x(0)
            for g in range(GROUPS):
                act.wait_ge(s_wq[g], 16 * KD)
                copy(of_group(wq_h, g), wq_raw[g], s_wqh)

            def heads(b, g):
                step = b * GROUPS + g
                if some(2 * step):
                    act.wait_ge(s_sc[0], 2 * step)
                if some(12 * step):
                    act.wait_ge(s_qk, 12 * step)
                for i in range(4):
                    dst = (qT if i < 2 else kT)[:, i % 2, :]
                    evac(dst, pA[:, (KD + 7 * g + i) % 2, :], job(b, g, i))
                if some(step):
                    exps(step - 1, 1, 0)
                    exps(step - 1, 1, 1)
                if some(2 * step - 2):
                    act.wait_ge(s_y, 2 * step - 2)
                if g == 0:
                    act.wait_ge(s_hp, 8 * b + 8)
                    copy(hC_h[:, :, :], hC[:, :, :], s_hch)
                for i in range(3):
                    evac(V[:, g % 2, 2 * i:2 * i + 2, :].rearrange("p u n -> p (u n)"),
                         pA[:, (KD + 7 * g + 4 + i) % 2, :], job(b, g, 4 + i))
                    if i == 0:
                        exps(step, 0, 0)
                        exps(step, 0, 1)

            def body(b):
                for g in range(GROUPS):
                    if head(b):
                        heads(b, g)
                        if g == GROUPS - 1 and following(b):
                            evac_x(b + 1)
                    elif g == 0 and tail(b):
                        exps(BATCH * GROUPS - 1, 1, 0)
                        exps(BATCH * GROUPS - 1, 1, 1)
                    if g == 0:
                        if late(b):
                            act.wait_ge(s_dx, 2 * (b - 1))
                            nc.scalar.activation(ex[:, :, :], ex[:, :, :], ACT.Exp).then_inc(s_ex8, 1)
                        if tail(b):
                            results(b - 1, GROUPS - 1)
                        if not head(b) and tail(b):
                            act.wait_ge(s_win, 48)
                            high_weights(0)
                    elif head(b):
                        results(b, g - 1)
                    if g == GROUPS - 1 and tail(b):
                        for k in range(KD):
                            act.wait_ge(s_t2, (b - 1) * KD + k + 1)
                            nc.scalar.activation(h2T[:, k, :], pM[:, k, :], ACT.Copy).then_inc(s_t2e, 1)

            def high_weights(n):
                w13_h, _, w2_h, _ = slot_parts(n)
                copy(w13_h, w13_raw, s_wh)
                copy(w2_h, w2_raw, s_wh)

            over_batches(act, body)
            act.wait_ge(s_win, 96)
            high_weights(1)

            def rows_high(j, n):
                act.wait_ge(s_tx, j + 1)
                if some(j - 1):
                    act.wait_ge(s_m1, j - 1)
                copy(xT_h[:, n, :, :], pXY[:, 0, 0:D].rearrange("p (k n) -> p k n", k=KD), s_xh)

            def store_rows(j, n):
                act.wait_ge(s_yv, j + 1)
                act.dma_start(ys_dram[bass.ds(j * P, P), :], ysb[:, n, :]).then_inc(s_yst[n], 16)

            def tile(j, n, more):
                if more:
                    rows_high(j + 1, 1 - n)
                act.wait_ge(s_m1, j + 1)
                if some(j):
                    act.wait_ge(s_mu, j)
                nc.scalar.activation(gg[:, :, :], p13[0][:, :, 0:FF // 2], ACT.Gelu).then_inc(s_gl, 1)
                act.wait_ge(s_th, j + 1)
                act.wait_ge(s_m2, j + 1)
                copy(hid_h, pH[:, :, 0:3 * P].rearrange("p a (c n) -> p a c n", c=3), s_hdh)
                if some(j):
                    store_rows(j - 1, 1 - n)

            rows_high(0, 0)
            tile(0, 0, True)
            tile(1, 1, True)
            with act.Fori(1, TILES // 2 - 1) as pair:
                tile(pair * 2, 0, True)
                tile(pair * 2 + 1, 1, True)
            tile(TILES - 2, 0, True)
            tile(TILES - 1, 1, False)
            store_rows(TILES - 1, 1)

        @block.tensor
        def _(pe):
            mm = nc.tensor.matmul

            pe.wait_ge(s_cm, 32)
            pe.wait_ge(s_silu, 4)
            wm = YT[:, 0:6, :].rearrange("p (k a) n -> p k (a n)", k=KD)
            for n in range(2 * KD):
                for k in range(KD):
                    mm(pM[:, 0, n * BATCH:(n + 1) * BATCH], wm[:, k, n * P:(n + 1) * P], siT[:, k, :],
                       start=(k == 0), stop=(k == KD - 1))
            for m in range(2):
                for k in range(KD):
                    last = mm(pS[0:BATCH, m, :], siT[:, k, :], wm[:, k, (m + 1) * SEQ:(m + 2) * SEQ],
                              start=(k == 0), stop=(k == KD - 1))
            last.then_inc(s_modp, 1)
            pe.wait_ge(s_cst, 48)

            def transposed_x(b):
                pe.wait_ge(s_xn, b + 1)
                for k in range(KD):
                    n = job_x(b, k)
                    if some(n - 1):
                        pe.wait_ge(s_pe, n - 1)
                    for t in range(TT):
                        last = nc.tensor.transpose(pA[:, k, t * P:(t + 1) * P],
                                                   x_sb[:, t, k * P:(k + 1) * P], ident)
                    last.then_inc(s_pj, 1)

            def heads_qk(b, g):
                for i in range(4):
                    n = job(b, g, i)
                    pe.wait_ge(s_pe, n - 1)
                    if i == 0 and g == 0:
                        pe.wait_ge(s_hl, KD * b + KD)
                    if i == 0 and isinstance(b, int) and b == 0:
                        pe.wait_ge(s_wql, g + 1)
                    col = (i // 2) * INNER + (2 * g + i % 2) * P
                    for k in range(KD):
                        w = (wq_h[:, k, col:col + P], wq_l[:, k, col:col + P])
                        products_ = parts(w, (hT_h[:, k, :], hT_l[:, k, :]))
                        for m, (still, moving) in enumerate(products_):
                            last = mm(pA[:, (KD + 7 * g + i) % 2, :], still, moving,
                                      start=(k == 0 and m == 0), stop=(k == KD - 1 and m == 2))
                    last.then_inc(s_pj, 1)

            def heads_v(b, g, jobs):
                for i in jobs:
                    n = job(b, g, 4 + i)
                    pe.wait_ge(s_pe, n - 1)
                    if i == 2 and g == 0:
                        pe.wait_ge(s_hcl, b + 1)
                    col = 2 * INNER + g * 4 * DH
                    for u in (2 * i, 2 * i + 1):
                        at = u % TT * P
                        for k in range(KD):
                            rows_u = tuple(buf[:, k, at:at + P] for buf in ((hT_h, hT_l) if u < TT else (hC_h, hC_l)))
                            w = (wq_h[:, k, col:col + 4 * DH], wq_l[:, k, col:col + 4 * DH])
                            for m, (still, moving) in enumerate(parts(rows_u, w)):
                                last = mm(pA[:, (KD + 7 * g + 4 + i) % 2, (u % 2) * 4 * DH:(u % 2 + 1) * 4 * DH],
                                          still, moving, start=(k == 0 and m == 0), stop=(k == KD - 1 and m == 2))
                    last.then_inc(s_pj, 1)

            def block(e, u, c, quad, q, k):
                return mm(pS[quad * 32:(quad + 1) * 32, e, (2 * u + c) * 32:(2 * u + c + 1) * 32],
                          q, k, start=True, stop=True)

            def scores(b, g):
                step = b * GROUPS + g
                if isinstance(step, int) and step == 0:
                    pe.wait_ge(s_mod, NMOD)
                pe.wait_ge(s_pe, job(b, g, 3) + 1)
                if some(4 * step):
                    needed = held(pe, 4 * step)
                    pe.wait_ge(s_mk[1], 1)
                    pe.wait_ge(s_mk[1], needed)
                for e in range(2):
                    lo, hi = e * DH, (e + 1) * DH
                    for u in range(TT):
                        for c in range(2):
                            for quad in range(4):
                                a = u * P + quad * 32
                                last = block(e, u, c, quad, qT[lo:hi, c, a:a + 32], kT[lo:hi, c, a:a + 32])
                    last.then_inc(s_sc[0], 1)

            def pooled_scores(b, g):
                step = b * GROUPS + g
                pe.wait_ge(s_mk[0], 2 * step + 2)
                needed = held(pe, 12 * step + 12)
                pe.wait_ge(s_qk, 1)
                pe.wait_ge(s_qk, needed)
                for e in range(2):
                    lo, hi = e * DH, (e + 1) * DH
                    for c in range(2):
                        for u in (4, 5):
                            for quad in range(4):
                                q = qC[lo:hi, c, (u - 4) * P + quad * 32:(u - 4) * P + (quad + 1) * 32]
                                n, a = (0, quad * 64) if u == 4 else ((1, quad * 64), (1, quad * 64), (2, 0), (3, 0))[quad]
                                if (u, quad) == (5, 3):
                                    k = kP[n][lo:hi, c:c + 1, 0:16].broadcast_to([DH, 2, 16])
                                else:
                                    k = kP[n][lo:hi, c, a:a + 64].rearrange("p (n r) -> p n r", r=32)[:, :, 0:16]
                                last = block(e, u, c, quad, q, k)
                    last.then_inc(s_sc[1], 1)

            def products(b, g):
                step = b * GROUPS + g
                pe.wait_ge(s_at, 24 * step + 24)
                pe.wait_ge(s_pe, job(b, g, 6) + 1)
                if some(2 * step):
                    pe.wait_ge(s_ye, 2 * step)
                for c in range(2):
                    for u in range(UNITS):
                        for e in range(2):
                            val = V[:, g % 2, u, (2 * c + e) * DH:(2 * c + e + 1) * DH]
                            row = pY[e * DH:(e + 1) * DH, c, :]
                            if u < TT:
                                dst, src = row[:, u * P:(u + 1) * P], AT[:, e, 2 * u + c, :]
                            elif u == TT:
                                dst = row.rearrange("p (n r s) -> p n r s", r=32, s=2)[:, :, 16:32, 1]
                                src = AT[:, e, 2 * u + c, :]
                            else:
                                dst, src = row.rearrange("p (n s) -> p n s", s=4)[:, :, 3], MG[:, e, c, 0:P]
                            last = mm(dst, val, src, start=(u == 0), stop=(u == UNITS - 1),
                                      skip_group_check=True)
                    last.then_inc(s_y, 1)

            def sums_transposed(b):
                pe.wait_ge(s_rsd, b + 1)
                if some(b):
                    pe.wait_ge(s_lg, b)
                if some(b):
                    pe.wait_ge(s_pb, b)
                pe.wait_ge(s_ba, 5 * b + 1)
                for u in range(UNITS):
                    last = nc.tensor.transpose(pM[0:HEADS, u // 4, (u % 4) * P:(u % 4 + 1) * P],
                                               rs_done[:, u, :], ident)
                last.then_inc(s_rt, 1)

            def broadcast_sums(b):
                pe.wait_ge(s_rd, b + 1)
                if isinstance(b, int) and b == 0:
                    pe.wait_ge(s_late, 48)
                for c in range(8):
                    pe.wait_ge(s_yn, 8 * b + c + 7)
                    mm(pM[:, c % 2, :], sel_sb[:, c, :], den[:, :], start=True, stop=True).then_inc(s_bc, 1)

            def projection(b):
                pe.wait_ge(s_yn, 8 * b + 16)
                for t in range(TT):
                    for c in range(8):
                        last = mm(pM[:, t // 2, (t % 2) * D:(t % 2 + 1) * D],
                                  YN[:, c, t * P:(t + 1) * P], wout_sb[:, c, :],
                                  start=(c == 0), stop=(c == 7))
                    if t % 2:
                        last.then_inc(s_op, 1)

            def transposed_h2(b):
                pe.wait_ge(s_h2, b + 1)
                pe.wait_ge(s_xg, 2 * b + 2)
                for k in range(KD):
                    for t in range(TT):
                        last = nc.tensor.transpose(pM[:, k, t * P:(t + 1) * P], h2[:, t, k * P:(k + 1) * P], ident)
                    last.then_inc(s_t2, 1)

            def route(b):
                pe.wait_ge(s_t2e, KD * b + KD)
                for t in range(TT):
                    for k in range(KD):
                        last = mm(pM[:, 0, t * EXPERTS:(t + 1) * EXPERTS], h2T[:, k, t * P:(t + 1) * P],
                                  rout_sb[:, k, :], start=(k == 0), stop=(k == KD - 1))
                last.then_inc(s_lp, 1)

            def count(b):
                pe.wait_ge(s_ohs, b + 1)
                flat = ohs[:, :, :].rearrange("p t e -> p (t e)")
                mm(pM[:, 1, 0:TT * EXPERTS], cst[:, C_TRI:C_TRI + P], flat, start=True, stop=True)
                mm(pM[:, 1, TT * EXPERTS:2 * TT * EXPERTS], ones[:, :], flat,
                   start=True, stop=True).then_inc(s_px, 1)

            transposed_x(0)

            def body(b):
                for g in range(GROUPS):
                    if head(b):
                        heads_qk(b, g)
                    if g == 0 and late(b):
                        route(b - 2)
                    if g == 1 and tail(b):
                        sums_transposed(b - 1)
                    if head(b):
                        heads_v(b, g, (0,))
                        scores(b, g)
                        heads_v(b, g, (1, 2))
                    if g == GROUPS - 1 and following(b):
                        transposed_x(b + 1)
                    if g == 0:
                        if tail(b):
                            products(b - 1, GROUPS - 1)
                        if late(b):
                            count(b - 2)
                    elif head(b):
                        products(b, g - 1)
                    if tail(b):
                        if g == 1:
                            broadcast_sums(b - 1)
                        if g == 2:
                            projection(b - 1)
                        if g == 3:
                            transposed_h2(b - 1)
                    if head(b):
                        pooled_scores(b, g)

            over_batches(pe, body)

            pe.wait_ge(s_tab, NTAB)

            def transposed_rows(j, n, pair):
                pe.wait_ge(s_xs[n], 16 * pair + 16)
                if some(j):
                    pe.wait_ge(s_xT, j)
                for k in range(KD):
                    last = nc.tensor.transpose(pXY[:, 0, k * P:(k + 1) * P], xs[:, n, k * P:(k + 1) * P], ident)
                last.then_inc(s_tx, 1)

            def weights_of(j):
                return (pe.value_load(tabi[0:1, 2, bass.ds(j, 1)], min_val=2, max_val=2 * EXPERTS),
                        pe.value_load(tabi[0:1, 3, bass.ds(j, 1)], min_val=0, max_val=1))

            def up(j, n, arrived, at):
                pe.wait_ge(s_wl, arrived)
                pe.wait_ge(s_xT, j + 1)
                if some(j):
                    pe.wait_ge(s_mu, j)
                if some(j):
                    pe.wait_ge(s_gl, j)
                for half in range(4):
                    for k in range(KD):
                        w = tuple(big[:, bass.ds(at * SLOT + (part * W13 + k * FF2 + half * (FF // 2)), FF // 2)]
                                  for part in range(2))
                        for m, (still, moving) in enumerate(parts((xT_h[:, n, k, :], xT_l[:, n, k, :]), w)):
                            last = mm(p13[half // 2][:, half % 2, 0:FF // 2], still, moving,
                                      start=(k == 0 and m == 0), stop=(k == KD - 1 and m == 2))
                last.then_inc(s_m1, 1)

            def down(j):
                at = pe.value_load(tabi[0:1, 3, bass.ds(j, 1)], min_val=0, max_val=1)
                pe.wait_ge(s_hT, j + 1)
                if some(j):
                    pe.wait_ge(s_yv, j)
                for c in range(FC):
                    w = tuple(big[:, bass.ds(at * SLOT + (2 * W13 + part * W2 + c * D), D)] for part in range(2))
                    rows_c = (hid_h[:, c // 3, c % 3, :], hid_l[:, c // 3, c % 3, :])
                    for m, (still, moving) in enumerate(parts(rows_c, w)):
                        last = mm(pXY[:, 1, 0:D], still, moving,
                                  start=(c == 0 and m == 0), stop=(c == FC - 1 and m == 2))
                last.then_inc(s_m2, 1)

            pe.wait_ge(s_pad, 2)

            def hidden_transposed(j):
                pe.wait_ge(s_mu, j + 1)
                if some(j):
                    pe.wait_ge(s_hT, j)
                for c in range(FC):
                    last = nc.tensor.transpose(pH[:, c // 3, (c % 3) * P:(c % 3 + 1) * P],
                                               hh_flat[:, c * P:(c + 1) * P], ident)
                last.then_inc(s_th, 1)

            def tile(j, n, pair, first=False, more=True):
                arrived, at = weights_of(j)
                if not first:
                    down(j - 2)
                hidden_transposed(j - 1)
                if more:
                    transposed_rows(j + 1, 1 - n, pair + n)
                up(j, n, arrived, at)

            transposed_rows(0, 0, 0)
            transposed_rows(1, 1, 0)
            up(0, 0, *weights_of(0))
            tile(1, 1, 0, first=True)
            tile(2, 0, 1)
            tile(3, 1, 1)
            with pe.Fori(2, TILES // 2 - 1) as pair:
                tile(pair * 2, 0, pair)
                tile(pair * 2 + 1, 1, pair)
            tile(TILES - 2, 0, TILES // 2 - 1)
            tile(TILES - 1, 1, TILES // 2 - 1, more=False)
            down(TILES - 2)
            hidden_transposed(TILES - 1)
            down(TILES - 1)

        @block.vector
        def _(dve):
            v = nc.vector

            def stats(b, src, bn, mv, s_bn, s_mv):
                for t in range(TT):
                    v.bn_stats(bn[:, t, :], src[:, t, :]).then_inc(s_bn, 1)
                for t in range(TT):
                    needed = held(dve, TT * b + t + 1)
                    dve.wait_ge(s_bn, 1)
                    dve.wait_ge(s_bn, needed)
                    v.bn_aggr(mv[:, t, :], bn[:, t, :]).then_inc(s_mv, 1)

            def stats1(b):
                dve.wait_ge(s_xin, 16 * (b + 1))
                stats(b, x_sb, bn1, mv1, s_bn1, s_mv1)

            def normalise1(b):
                dve.wait_ge(s_rs1, b + 1)
                for t in range(TT):
                    last = v.tensor_scalar(x_sb[:, t, :], x_sb[:, t, :], mv1[:, t, 0:1], rstd1[:, t:t + 1],
                                           ALU.subtract, ALU.mult)
                last.then_inc(s_xn, 1)

            stats1(0)
            normalise1(0)
            dve.wait_ge(s_cst, 48)
            v.tensor_copy(base[:, TT, :], cst[:, C_CAP:C_CAP + 8]).then_inc(s_ba, 1)
            v.memset(mx[:, :, :], 0.0).then_inc(s_yn, 8)
            dve.wait_ge(s_silu, 1)
            v.tensor_scalar(sil[:, :, :], sil[:, :, :], 1.0, None, ALU.add).then_inc(s_silu, 1)
            dve.wait_ge(s_silu, 2)
            v.reciprocal(sil[:, :, :], sil[:, :, :]).then_inc(s_silu, 1)
            dve.wait_ge(s_silu, 3)
            v.tensor_tensor(siT[:, :, :], cT_sb[:, :, :], sil[:, :, :], ALU.mult).then_inc(s_silu, 1)
            dve.wait_ge(s_modp, 1)
            cols = pM[:, 0, 0:2 * KD * BATCH].rearrange("p (n b) -> p n b", b=BATCH)
            v.tensor_copy(modT[:, 0:KD, :], cols[:, 0:KD, :]).then_inc(s_mod, 1)
            v.tensor_scalar(modT[:, KD:2 * KD, :], cols[:, KD:2 * KD, :], 1.0, None, ALU.add).then_inc(s_mod, 1)
            n = 2
            for g_psum, r, bias in ((pS[0:BATCH, 0, 0:D], 0, 0), (pS[0:BATCH, 1, D:2 * D], 4, 1)):
                v.tensor_scalar(mtmp[:, 0, :], g_psum, 0.0, 2.0, ALU.is_ge, ALU.mult).then_inc(s_mod, 1)
                dve.wait_ge(s_mod, n + 1)
                v.scalar_tensor_tensor(mtmp[:, 1, :], mtmp[:, 0, :], -1.0, g_psum, ALU.add, ALU.mult).then_inc(s_mod, 1)
                dve.wait_ge(s_mod, n + 2)
                v.tensor_scalar(mtmp[:, 1, :], mtmp[:, 1, :], 0.25, None, ALU.max).then_inc(s_mod, 1)
                dve.wait_ge(s_mod, n + 3)
                v.scalar_tensor_tensor(mrow[r], mtmp[:, 0, :], -1.0, mtmp[:, 1, :],
                                       ALU.add, ALU.mult).then_inc(s_mod, 1)
                dve.wait_ge(s_mod, n + 4)
                v.tensor_tensor(mrow[r + 1], mrow[r], bo_row[:, bias, :], ALU.mult).then_inc(s_mod, 1)
                n += 5
            v.tensor_copy(mrow[3], pS[0:BATCH, 0, D:2 * D]).then_inc(s_mod, 1)
            v.tensor_scalar(mrow[2], pS[0:BATCH, 1, 0:D], 1.0, None, ALU.add).then_inc(s_mod, 1)

            def exponents(b, g, level):
                step = b * GROUPS + g
                pieces = (((0, 2 * TT, DH ** -0.5, C_M0),),
                          ((2 * TT, 2, DH ** -0.5 / 4, C_M1), (2 * TT + 2, 2, cst[:, C_SC2:C_SC2 + 1], C_M2)))[level]
                cols = slice(0, 2 * TT) if level == 0 else slice(2 * TT, 2 * UNITS)
                for e in range(2):
                    dve.wait_ge(s_sc[level], 2 * step + e + 1)
                    for lo, n, scale, mask in pieces:
                        piece = slice(lo * 32, (lo + n) * 32)
                        v.scalar_tensor_tensor(
                            sm[:, e, piece].rearrange("p (n r) -> p n r", r=32),
                            pS[:, e, piece].rearrange("p (n r) -> p n r", r=32), scale,
                            cst[:, mask:mask + 32].unsqueeze(1).broadcast_to([P, n, 32]),
                            ALU.mult, ALU.add).then_inc(s_mk[level], 1)
                    dve.wait_ge(s_mk[level], (level + 1) * (2 * step + e + 1))
                    tiles = sm[:, e, PIECES[level]].rearrange("p (n r) -> p n r", r=32)
                    v.tensor_reduce(mx[:, e, cols], tiles, AX.X, ALU.max).then_inc(s_mx[level], 1)
                    dve.wait_ge(s_mx[level], 2 * step + e + 1)
                    n = tiles.shape[1]
                    v.tensor_tensor(tiles, tiles, mx[:, e, cols].unsqueeze(2).broadcast_to([P, n, 32]),
                                    ALU.subtract).then_inc(s_sb_[level], 1)

            def weights(b, g, level):
                step = b * GROUPS + g
                units = slice(0, TT) if level == 0 else slice(TT, UNITS)
                for e in range(2):
                    dve.wait_ge(s_ex[level], 2 * step + e + 1)
                    tiles = sm[:, e, PIECES[level]].rearrange("p (u c r) -> p u c r", c=2, r=32)
                    v.tensor_reduce(rs[:, units, 4 * g + e:4 * g + e + 3:2], tiles, AX.X, ALU.add).then_inc(s_rs, 1)
                    if some(2 * step):
                        dve.wait_ge(s_y, 2 * step)
                    for quad in range(4):
                        q = slice(quad * 32, (quad + 1) * 32)
                        flat = sm[q, e, :].rearrange("p (n r) -> p n r", r=32)
                        if level == 0:
                            v.transpose(AT[q, e, 0:2 * TT, quad * 32:(quad + 1) * 32],
                                        flat[:, 0:2 * TT, :]).then_inc(s_at, 1)
                            continue
                        v.transpose(AT[q, e, 2 * TT:, quad * 32:(quad + 1) * 32],
                                    flat[:, 2 * TT:2 * TT + 2, :]).then_inc(s_at, 1)
                        if quad < 2:
                            dst = MG[q, e, :, quad * 64:(quad + 1) * 64].rearrange("p c (n r) -> p c n r", r=32)[:, :, :, 16:32]
                        elif quad == 2:
                            dst = MG[q, e, :, 0:P].rearrange("p c (n r s) -> p c n r s", r=32, s=2)[:, :, :, 16:32, 1]
                        else:
                            dst = MG[q, e, :, 64:64 + P].rearrange("p c (n r s) -> p c n r s", r=16, s=4)[:, :, :, :, 3]
                        v.transpose(dst, flat[:, 2 * TT + 2:, :]).then_inc(s_at, 1)

            def sums(b):
                dve.wait_ge(s_rt, b + 1)
                v.tensor_scalar(den[:, :], pM[0:HEADS, 0, :], SUM_EPS, None, ALU.add).then_inc(s_dn, 1)
                n = 5 * b + 1
                for s, lo, cnt in ((2, 0, 8), (4, P, 4), (8, P + 64, 2), (16, P + 96, 1)):
                    dve.wait_ge(s_dn, n)
                    to = den[:, :].rearrange("p (n r s) -> p n r s", r=32, s=s)[:, :, 16:32, s - 1]
                    v.tensor_tensor(to, to, pM[0:HEADS, 1, lo:lo + 16 * cnt].rearrange("p (n r) -> p n r", r=16),
                                    ALU.add).then_inc(s_dn, 1)
                    n += 1
                dve.wait_ge(s_dn, n)
                v.reciprocal(den[:, :], den[:, :]).then_inc(s_rd, 1)

            def divide(b):
                dve.wait_ge(s_ye, 8 * b + 8)
                if some(2 * b):
                    dve.wait_ge(s_op, 2 * b)
                for c in range(8):
                    dve.wait_ge(s_bc, 8 * b + c + 1)
                    v.tensor_tensor(YN[:, c, :], pM[:, c % 2, :], YT[:, c, :], ALU.mult).then_inc(s_yn, 1)

            def residual(b):
                dve.wait_ge(s_xrb, b + 1)
                if some(16 * b):
                    dve.wait_ge(s_x2st, 16 * b)
                for half in range(2):
                    dve.wait_ge(s_op, 2 * b + half + 1)
                    v.tensor_tensor(x2[:, 2 * half:2 * half + 2, :],
                                    pM[:, half, :].rearrange("p (t n) -> p t n", n=D),
                                    rows[:, 0:1, :].broadcast_to([P, 2, D]), ALU.mult).then_inc(s_xg, 1)
                dve.wait_ge(s_xg, 2 * b + 2)
                v.tensor_tensor(x2[:, :, :], x2[:, :, :], xr[:, :, :], ALU.add).then_inc(s_x2, 1)
                dve.wait_ge(s_x2, b + 1)
                stats(b, x2, bn2, mv2, s_bn2, s_mv2)

            def normalise2(b):
                dve.wait_ge(s_rs2, b + 1)
                if some(16 * TOPK * TT * b):
                    dve.wait_ge(s_disp, 16 * TOPK * TT * b)
                for t in range(TT):
                    last = v.tensor_scalar(h2[:, t, :], x2[:, t, :], mv2[:, t, 0:1], rstd2[:, t:t + 1],
                                           ALU.subtract, ALU.mult)
                last.then_inc(s_xn2, 1)

            def choose(b):
                dve.wait_ge(s_lp, b + 1)
                v.tensor_copy(lg[:, :, :], pM[:, 0, 0:TT * EXPERTS].rearrange("p (t e) -> p t e", e=EXPERTS)).then_inc(s_lg, 1)
                needed = held(dve, b + 1)
                dve.wait_ge(s_lg, 1)
                dve.wait_ge(s_lg, needed)
                for t in range(TT):
                    v.max(v8[:, t, :], lg[:, t, :]).then_inc(s_v8, 1)
                for t in range(TT):
                    needed = held(dve, TT * b + t + 1)
                    dve.wait_ge(s_v8, 1)
                    dve.wait_ge(s_v8, needed)
                    v.max_index(i8[:, t, :], v8[:, t, :], lg[:, t, :]).then_inc(s_i8, 1)
                top = v8[:, :, 0:1]
                v.tensor_tensor(ex[:, :, 0:EXPERTS], lg[:, :, :], top.broadcast_to([P, TT, EXPERTS]),
                                ALU.subtract).then_inc(s_dx, 1)
                v.tensor_tensor(ex[:, :, EXPERTS:], v8[:, :, 0:TOPK], top.broadcast_to([P, TT, TOPK]),
                                ALU.subtract).then_inc(s_dx, 1)
                dve.wait_ge(s_i8, TT * b + TT)
                v.tensor_copy(if8[:, :, :], i8[:, :, 0:TOPK]).then_inc(s_if, 1)
                dve.wait_ge(s_if, b + 1)
                for k in range(TOPK):
                    v.tensor_tensor(oh[:, k, :, :],
                                    cst[:, C_E8:C_E8 + 8].unsqueeze(1).broadcast_to([P, TT, EXPERTS]),
                                    if8[:, :, k:k + 1].broadcast_to([P, TT, EXPERTS]), ALU.is_equal).then_inc(s_oh, 1)
                dve.wait_ge(s_oh, TOPK * (b + 1))
                v.tensor_tensor(ohs[:, :, :], oh[:, 0, :, :], oh[:, 1, :, :], ALU.add).then_inc(s_ohs, 1)

            def slots(b):
                dve.wait_ge(s_ex8, b + 1)
                v.tensor_reduce(sume[:, :], ex[:, :, 0:EXPERTS], AX.X, ALU.add).then_inc(s_su, 1)
                dve.wait_ge(s_su, b + 1)
                v.reciprocal(rsum[:, :], sume[:, :]).then_inc(s_rsu, 1)
                dve.wait_ge(s_rsu, b + 1)
                v.tensor_tensor(gate_all[:, bass.ds(b, 1), :].rearrange("p a (t k) -> p (a t) k", k=TOPK),
                                ex[:, :, EXPERTS:], rsum[:, :].unsqueeze(2).broadcast_to([P, TT, TOPK]),
                                ALU.mult).then_inc(s_gt, 1)
                dve.wait_ge(s_px, b + 1)
                v.tensor_copy(base[:, 0, :], base[:, TT, :]).then_inc(s_ba, 1)
                for t in range(TT):
                    dve.wait_ge(s_ba, 5 * b + 2 + t)
                    tot = pM[:, 1, (TT + t) * EXPERTS:(TT + t + 1) * EXPERTS]
                    v.tensor_tensor(base[:, t + 1, :], tot, base[:, t, :], ALU.add).then_inc(s_ba, 1)
                dve.wait_ge(s_ba, 5 * b + 1 + TT)
                v.tensor_tensor(posb[:, :, :], pM[:, 1, 0:TT * EXPERTS].rearrange("p (t e) -> p t e", e=EXPERTS),
                                base[:, 0:TT, :], ALU.add).then_inc(s_pb, 1)
                dve.wait_ge(s_pb, b + 1)
                v.tensor_tensor(posm[:, :, :, :].rearrange("p k t e -> p k (t e)"),
                                oh[:, :, :, :].rearrange("p k t e -> p k (t e)"),
                                posb[:, :, :].rearrange("p t e -> p (t e)").unsqueeze(1)
                                .broadcast_to([P, TOPK, TT * EXPERTS]), ALU.mult).then_inc(s_pm, 1)
                dve.wait_ge(s_pm, b + 1)
                v.tensor_reduce(posf[:, :, :].rearrange("p k t -> p (k t)"),
                                posm[:, :, :, :].rearrange("p k t e -> p (k t) e"), AX.X, ALU.add).then_inc(s_pf, 1)
                dve.wait_ge(s_pf, b + 1)
                v.tensor_copy(slot[:, :, :], posf[:, :, :]).then_inc(s_sl, 1)
                v.tensor_copy(slotf_all[:, bass.ds(b, 1), :],
                              posf[:, :, :].rearrange("p k t -> p (k t)").unsqueeze(1)).then_inc(s_sla, 1)

            def split_inputs(b):
                for k in range(KD):
                    dve.wait_ge(s_hh, KD * b + k + 1)
                    dve.wait_ge(s_pe, job_x(b, k) + 1)
                    v.tensor_tensor(hT_l[:, k, :], hT[:, k, :], f32(hT_h[:, k, :]), ALU.subtract).then_inc(s_hl, 1)

            def split_pooled(b):
                dve.wait_ge(s_hch, b + 1)
                v.tensor_tensor(hC_l[:, :, :], hC[:, :, :], f32(hC_h[:, :, :]), ALU.subtract).then_inc(s_hcl, 1)

            split_inputs(0)
            for g in range(GROUPS):
                dve.wait_ge(s_wqh, g + 1)
                for k in range(KD):
                    part_l, part_h = (of_group(w, g)[:, k, :, :] for w in (wq_l, wq_h))
                    op = v.tensor_tensor(part_l, wq_raw[g][:, k, :, :], f32(part_h), ALU.subtract)
                op.then_inc(s_wql, 1)
            dve.wait_ge(s_b0, 6)

            def keep_sums(b):
                dve.wait_ge(s_rs, 16 * b + 16)
                v.tensor_copy(rs_done[:, :, :], rs[:, :, :]).then_inc(s_rsd, 1)

            def body(b):
                if tail(b):
                    keep_sums(b - 1)
                if head(b):
                    split_pooled(b)
                if late(b):
                    choose(b - 2)
                for g in range(GROUPS):
                    if g == 1 and tail(b):
                        sums(b - 1)
                    if head(b):
                        exponents(b, g, 0)
                    if g == 1 and tail(b):
                        divide(b - 1)
                    if g == 3 and following(b):
                        split_inputs(b + 1)
                    if head(b):
                        weights(b, g, 0)
                    if g == 0 and late(b):
                        slots(b - 2)
                    if g == 1 and following(b):
                        stats1(b + 1)
                    if g == 2:
                        if following(b):
                            normalise1(b + 1)
                        if tail(b):
                            residual(b - 1)
                            normalise2(b - 1)
                    if head(b):
                        exponents(b, g, 1)
                        weights(b, g, 1)

            over_batches(dve, body)

            tab = [0]

            def did(op):
                tab[0] += 1
                op.then_inc(s_tab, 1)
                dve.wait_ge(s_tab, tab[0])

            dve.wait_ge(s_ba, 5 * BATCH + 1)
            dve.wait_ge(s_x2st, 16 * BATCH)
            dve.wait_ge(s_sla, BATCH)
            count, ntile, shift, cum = (tb8[:, i, :] for i in range(4))
            did(v.tensor_copy(endi, base[:, TT, :]))
            did(v.tensor_tensor(count, base[:, TT, :], cst[:, C_CAP:C_CAP + 8], ALU.subtract))
            did(v.tensor_scalar(nti, count, P / 2 - 0.5, 1.0 / P, ALU.add, ALU.mult))
            did(v.tensor_copy(ntile, nti))
            did(v.tensor_tensor_scan(cumf, ones[:, 0:EXPERTS], ntile, 0.0, ALU.mult, ALU.add))
            did(v.tensor_scalar(cumi, cumf, 1.0, None, ALU.add))
            tile_no = cst[:, C_TILE:C_TILE + TILES]
            did(v.tensor_tensor(ind[:, :, :], tile_no.unsqueeze(2).broadcast_to([P, TILES, EXPERTS]),
                                cumf.unsqueeze(1).broadcast_to([P, TILES, EXPERTS]), ALU.is_ge))
            did(v.tensor_scalar(shift, ntile, -float(P), float(CAP), ALU.mult, ALU.add))
            did(v.tensor_tensor(indw[:, :, :], ind[:, :, :],
                                shift.unsqueeze(1).broadcast_to([P, TILES, EXPERTS]), ALU.mult))
            did(v.tensor_reduce(tabf[:, 0, :], indw[:, :, :], AX.X, ALU.add))
            did(v.tensor_reduce(tabf[:, 1, :], ind[:, :, :], AX.X, ALU.add))
            did(v.scalar_tensor_tensor(tabf[:, 2, :], tile_no, float(P), tabf[:, 0, :], ALU.mult, ALU.add))
            did(v.tensor_scalar(tabi[:, 0, :], tabf[:, 2, :], float(EXPERTS * CAP), None, ALU.min))
            did(v.tensor_scalar(tabf[:, 3, :], tabf[:, 1, :], EXPERTS - 1.0, None, ALU.min))
            did(v.tensor_copy(tabi[:, 1, :], tabf[:, 3, :]))
            did(v.tensor_scalar(tabi[:, 2, :], tabf[:, 3, :], 2.0, 2.0, ALU.mult, ALU.add))
            did(v.tensor_scalar(tabi[:, 3, :], tabi[:, 1, :], 1, None, ALU.bitwise_and))
            v.memset(tb8[:, 5, :], 0.0).then_inc(s_m2, 1)

            def result_rows():
                slots = slotf_all[:, :, :].rearrange("p b n -> p (b n)")
                N = BATCH * TOPK * TT
                did(v.tensor_scalar(tb8[:, 4, :], cst[:, C_CAP:C_CAP + 8], float(CAP), None, ALU.add))
                did(v.tensor_tensor(past, slots.unsqueeze(2).broadcast_to([P, N, EXPERTS]),
                                    tb8[:, 4:5, :].broadcast_to([P, N, EXPERTS]), ALU.is_ge))
                did(v.tensor_tensor(pastw, past, shift.unsqueeze(1).broadcast_to([P, N, EXPERTS]), ALU.mult))
                lower = x2[:, 0, 0:N]
                did(v.tensor_reduce(lower, pastw, AX.X, ALU.add))
                did(v.tensor_tensor(slot_all[:, :, :].rearrange("p b n -> p (b n)"), slots, lower, ALU.subtract))

            def take_rows(j, n):
                dve.wait_ge(s_tx, j + 1)
                if some(j - 1):
                    dve.wait_ge(s_m1, j - 1)
                dve.wait_ge(s_xh, j + 1)
                v.tensor_tensor(xT_l[:, n, :, :], pXY[:, 0, 0:D].rearrange("p (k n) -> p k n", k=KD), f32(xT_h[:, n, :, :]),
                                ALU.subtract).then_inc(s_xT, 1)

            def hidden_low(j):
                dve.wait_ge(s_hdh, j + 1)
                v.tensor_tensor(hid_l, pH[:, :, 0:3 * P].rearrange("p a (c n) -> p a c n", c=3), f32(hid_h),
                                ALU.subtract).then_inc(s_hT, 1)

            def gated(j):
                dve.wait_ge(s_gl, j + 1)
                dve.wait_ge(s_m1, j + 1)
                if some(j):
                    dve.wait_ge(s_th, j)
                v.tensor_tensor(hh[:, :, :], p13[1][:, :, 0:FF // 2], gg[:, :, :], ALU.mult).then_inc(s_mu, 1)

            def result(j, n, pair):
                dve.wait_ge(s_m2, j + 2)
                if some(16 * pair):
                    dve.wait_ge(s_yst[n], 16 * pair)
                v.tensor_copy(ysb[:, n, :], pXY[:, 1, 0:D]).then_inc(s_yv, 1)

            v.memset(hh_flat[:, FF:FC * P], 0.0).then_inc(s_pad, 1)
            take_rows(0, 0)
            take_rows(1, 1)
            gated(0)
            hidden_low(0)
            result_rows()

            def tiles(pair):
                for i in range(2):
                    j = pair * 2 + (i + 1)
                    take_rows(j + 1, i)
                    gated(j)
                    result(pair * 2 + i, i, pair)
                    hidden_low(j)

            tiles(0)
            with dve.Fori(1, TILES // 2 - 1) as pair:
                tiles(pair)
            gated(TILES - 1)
            result(TILES - 2, 0, TILES // 2 - 1)
            hidden_low(TILES - 1)
            result(TILES - 1, 1, TILES // 2 - 1)

            def indices(b, n, pair):
                if some(16 * TOPK * TT * pair):
                    dve.wait_ge(s_yg[n], 16 * TOPK * TT * pair)
                v.tensor_copy(gidx[:, n:n + 1, :], slot_all[:, bass.ds(b, 1), :]).then_inc(s_ix, 1)

            def finish(b, n, pair):
                dve.wait_ge(s_xf[n], 32 * (pair + 1))
                v.tensor_tensor(xf[:, n, :, :], xf[:, n, :, :],
                                frow[:, n, 1:2, :].broadcast_to([P, TT, D]), ALU.add).then_inc(s_fd, 1)
                dve.wait_ge(s_yg[n], 16 * TOPK * TT * (pair + 1))
                if some(16 * pair):
                    dve.wait_ge(s_out[n], 16 * pair)
                for t in range(TT):
                    v.tensor_scalar(of[:, n, t, :], yg[:, n, t, :],
                                    gate_all[:, bass.ds(b, 1), TOPK * t:TOPK * t + 1].rearrange("p a n -> p (a n)"),
                                    None, ALU.mult).then_inc(s_fa, 1)
                for t in range(TT):
                    dve.wait_ge(s_fa, TT * b + t + 1)
                    v.scalar_tensor_tensor(of[:, n, t, :], yg[:, n, TT + t, :],
                                           gate_all[:, bass.ds(b, 1), TOPK * t + 1:TOPK * t + 2].rearrange("p a n -> p (a n)"),
                                           of[:, n, t, :], ALU.mult, ALU.add).then_inc(s_fb, 1)
                dve.wait_ge(s_fb, TT * (b + 1))
                v.tensor_tensor(of[:, n, :, :], of[:, n, :, :],
                                frow[:, n, 0:1, :].broadcast_to([P, TT, D]), ALU.mult).then_inc(s_fc, 1)
                dve.wait_ge(s_fc, b + 1)
                v.tensor_tensor(of[:, n, :, :], of[:, n, :, :], xf[:, n, :, :], ALU.add).then_inc(s_f, 1)

            for n in range(2):
                dve.wait_ge(s_yst[n], 8 * TILES)
            for n in range(2):
                indices(n, n, 0)
            for n in range(2):
                finish(n, n, 0)
                indices(n + 2, n, 1)
            with dve.Fori(1, BATCH // 2 - 1) as pair:
                for n in range(2):
                    finish(pair * 2 + n, n, pair)
                    indices(pair * 2 + (n + 2), n, pair + 1)
            for n in range(2):
                finish(BATCH - 2 + n, n, BATCH // 2 - 1)


def constants():
    import numpy as np
    c = np.zeros((P, C_END), np.float32)
    r = np.arange(P)
    c[:, C_ID:C_ID + P] = np.eye(P)
    c[:, C_TRI:C_TRI + P] = r[:, None] < r[None, :]
    row, col = r[:, None] % 32, np.arange(32)[None, :]
    same = row // 16 == col // 16
    c[:, C_M0:C_M0 + 32] = np.where(same & (col <= row), 0.0, -1e30)
    c[:, C_M1:C_M1 + 32] = np.where(same, 0.0, -1e30)
    c[:, C_M2:C_M2 + 32] = np.where(np.where(r[:, None] < 96, same, col < 16), 0.0, -1e30)
    level = np.array([2, 2, 3, 4])[r // 32]
    c[:, C_SC2] = DH ** -0.5 / 4.0 ** level
    c[:, C_E8:C_E8 + 8] = np.arange(8)
    c[:, C_CAP:C_CAP + 8] = np.arange(8) * CAP
    c[:, C_TILE:C_TILE + TILES] = np.arange(TILES)
    sel = np.zeros((HEADS, 8, P), np.float32)
    for h in range(HEADS):
        sel[h, h // 2, (h % 2) * DH:(h % 2 + 1) * DH] = 1.0
    return c, sel


def kernel(**inputs):
    import numpy as np
    import concourse.bacc as bacc
    from concourse.bass_utils import run_bass_kernel_spmd

    def chunks(w):
        k = w.shape[0] // P
        return np.ascontiguousarray(w.reshape(k, P, -1).transpose(1, 0, 2))

    a = {n: np.asarray(v) for n, v in inputs.items()}
    c, sel = constants()
    up = np.concatenate([a["L0_ffn_w1"], a["L0_ffn_v1"]], axis=2)
    arrays = {
        "x": np.ascontiguousarray(a["L0_attn_x"].reshape(TOKENS, D)),
        "cT": chunks(a["L0_c"].T),
        "wmod": chunks(a["L0_wmod"]),
        "wqkv": chunks(a["L0_attn_w_qkv"].T),
        "wout": chunks(a["L0_attn_w_out"].T),
        "b_out": a["L0_attn_b_out"],
        "router": chunks(a["L0_ffn_router_w"]),
        "w13": np.ascontiguousarray(up.reshape(EXPERTS, KD, P, FF2).transpose(0, 2, 1, 3).reshape(EXPERTS, P, KD * FF2)),
        "w2": np.ascontiguousarray(a["L0_ffn_w2"]),
        "ffn_bias": a["L0_ffn_bias"],
        "consts": c,
        "sel": sel,
    }
    nc = bacc.Bacc("TRN2", target_bir_lowering=False, num_devices=1)
    args = [nc.dram_tensor(n, v.shape, F32, kind="ExternalInput").ap() for n, v in arrays.items()]
    out = nc.dram_tensor("out", (TOKENS, D), F32, kind="ExternalOutput").ap()
    build(nc, *args, out)
    r = run_bass_kernel_spmd(nc, [arrays], core_ids=[0])
    return r.results[0]["out"].reshape(BATCH, SEQ, D)
```

```python
from contextlib import ExitStack

import concourse.bass as bass
from concourse import mybir

F32 = mybir.dt.float32
F32R = mybir.dt.float32r
I32 = mybir.dt.int32
U32 = mybir.dt.uint32
ALU = mybir.AluOpType
ACT = mybir.ActivationFunctionType
AX = mybir.AxisListType

P = 128
BATCH, SEQ, D = 8, 512, 256
KD = D // P
TT = SEQ // P
TOKENS = BATCH * SEQ
HEADS, DH = 16, 64
INNER = HEADS * DH
GROUPS = 4
UNITS = TT + 2
EXPERTS, TOPK, FF = 8, 2, 704
FF2 = 2 * FF
FC = 6
FTAIL = FF - 5 * P
CAP = TOKENS + P
SLOTS = EXPERTS * CAP + P
TILES = 72
LN_EPS, SUM_EPS = 1e-5, 1e-8

C_ID, C_TRI = 0, P
C_M0, C_M1, C_M2 = 2 * P, 2 * P + 32, 2 * P + 64
C_SC2 = 2 * P + 96
C_E8 = C_SC2 + 1
C_CAP = C_E8 + 8
C_TILE = C_CAP + 8
C_END = C_TILE + TILES

W13, W2 = KD * FF2, FC * D
SLOT = 2 * W13 + 2 * W2

JOBS = 7 * GROUPS + KD


def some(count):
    return not (isinstance(count, int) and count <= 0)


def held(eng, count):
    return count if isinstance(count, int) else eng.to_reg(count)


def f32(ap):
    return ap.bitcast(F32)


def parts(stationary, moving):
    return ((stationary[0], moving[0]), (stationary[0], moving[1]), (stationary[1], moving[0]))


def job_x(b, k):
    return b * JOBS + k


def job(b, g, i):
    return b * JOBS + (KD + 7 * g + i)


def build(nc, x, cT, wmod, wqkv, wout, b_out, router, w13, w2, ffn_bias, consts, sel, out):
    rows_dram = nc.dram_tensor("mod_rows", [BATCH, 6, D], F32, kind="Internal").ap()
    x2_dram = nc.dram_tensor("x_after_attention", [TOKENS, D], F32, kind="Internal").ap()
    xs_dram = nc.dram_tensor("dispatched_rows", [SLOTS, D], F32, kind="Internal").ap()
    ys_dram = nc.dram_tensor("expert_rows", [TILES * P, D], F32, kind="Internal").ap()

    ctx = ExitStack()
    with ctx:
        def sb(name, shape, dt=F32):
            return ctx.enter_context(nc.sbuf_tensor(name, shape, dt))

        def pb(name, shape):
            return ctx.enter_context(nc.psum_tensor(name, shape, F32))

        def sem(name):
            return ctx.enter_context(nc.semaphore(name))

        cst = sb("cst", [P, C_END])
        sel_p = sb("sel_p", [P, 8, P], F32R)
        ones = sb("ones", [P, P])
        halfneg = sb("halfneg", [P, TT])
        big = sb("big", [P, 2 * SLOT], F32R)
        work = sb("work", [P, 2 * UNITS * 4 * DH + 4 * SEQ])
        WQ = KD * 3 * INNER
        wq_h, wq_l = (big[:, i * WQ:(i + 1) * WQ].rearrange("p (k n) -> p k n", k=KD) for i in range(2))
        assert WQ <= SLOT
        V = work[:, 0:2 * UNITS * 4 * DH].rearrange("p (s u n) -> p s u n", s=2, u=UNITS)
        at_q = 2 * UNITS * 4 * DH
        qT, kT = (work[:, at_q + i * 2 * SEQ:at_q + (i + 1) * 2 * SEQ].rearrange("p (c n) -> p c n", c=2)
                  for i in range(2))
        wout_sb = sb("wout_sb", [P, 8, D])
        bias_row = wout_sb[:, 0:1, :]
        den_h, den_l = (big[:, 2 * WQ + i * SEQ:2 * WQ + (i + 1) * SEQ] for i in range(2))
        wout_h, wout_l = (big[:, 2 * WQ + 2 * SEQ + i * 8 * D:2 * WQ + 2 * SEQ + (i + 1) * 8 * D]
                          .rearrange("p (c n) -> p c n", c=8) for i in range(2))
        rout_sb = sb("rout_sb", [P, KD, EXPERTS])
        cT_sb = sb("cT_sb", [P, KD, BATCH])
        sil = sb("sil", [P, KD, BATCH])
        siT = sb("siT", [P, KD, BATCH])
        modT = sb("modT", [P, 2 * KD, BATCH])
        ident = cst[:, C_ID:C_ID + P]
        x_sb = sb("x_sb", [P, TT, D])
        bn1 = sb("bn1", [P, TT, 6])
        mv1 = sb("mv1", [P, TT, 2])
        rstd1 = sb("rstd1", [P, TT])
        hT = sb("hT", [P, KD, SEQ])
        hP = [sb(f"hP{n}", [P, KD, SEQ >> n]) for n in (1, 2, 3)]
        hT_h, hT_l = sb("hT_h", [P, KD, SEQ], F32R), sb("hT_l", [P, KD, SEQ], F32R)
        hC = sb("hC", [P, KD, 2 * P])
        hC_l = sb("hC_l", [P, KD, 2 * P], F32R)
        hC_h = sb("hC_h", [P, KD, 2 * P], F32R)
        qP = [sb(f"qP{n}", [P, 2, SEQ >> n]) for n in (1, 2, 3)]
        qC = sb("qC", [P, 2, 2 * P])
        kP = [sb(f"kP{n}", [P, 2, SEQ >> n]) for n in (1, 2, 3, 4)]
        sm = sb("sm", [P, 2, UNITS * 2 * 32])
        mx = sb("mx", [P, 2, UNITS * 2])
        rs = sb("rs", [P, UNITS, HEADS])
        rs_done = sb("rs_done", [P, UNITS, HEADS])
        AT = sb("AT", [P, 2, 5 * 2, P])
        MG = sb("MG", [P, 2, 2, P + 64])
        YT = sb("YT", [P, 8, SEQ])
        YN_h, YN_l = (sb("YN_" + n, [P, 8, SEQ // 2], F32R) for n in "hl")
        den = sb("den", [HEADS, SEQ])
        rows = sb("rows", [P, 4, D])
        xr = sb("xr", [P, TT, D])
        x2 = sb("x2", [P, TT, D])
        bn2 = sb("bn2", [P, TT, 6])
        mv2 = sb("mv2", [P, TT, 2])
        rstd2 = sb("rstd2", [P, TT])
        h2 = sb("h2", [P, TT, D])
        mrow = [x2[0:BATCH, r, :] for r in range(4)] + [h2[0:BATCH, r, :] for r in range(2)]
        bo_row = h2[0:BATCH, 2:4, :]
        mtmp = xr[0:BATCH, 0:2, :]
        h2T = xr[:, :, :].rearrange("p t n -> p (t n)").rearrange("p (k n) -> p k n", k=KD)
        lg = sb("lg", [P, TT, EXPERTS])
        v8 = sb("v8", [P, TT, 8])
        i8 = sb("i8", [P, TT, 8], U32)
        if8 = sb("if8", [P, TT, TOPK])
        ex = sb("ex", [P, TT, EXPERTS + TOPK])
        sume = sb("sume", [P, TT])
        rsum = sb("rsum", [P, TT])
        oh = sb("oh", [P, TOPK, TT, EXPERTS])
        ohs = sb("ohs", [P, TT, EXPERTS])
        base = sb("base", [P, TT + 1, EXPERTS])
        posb = sb("posb", [P, TT, EXPERTS])
        posm = sb("posm", [P, TOPK, TT, EXPERTS])
        posf = sb("posf", [P, TOPK, TT])
        slot = sb("slot", [P, TOPK, TT], I32)
        slotf_all = sb("slotf_all", [P, BATCH, TOPK * TT])
        gate_all = sb("gate_all", [P, BATCH, TT * TOPK])
        zrow = sb("zrow", [P, D])
        tb8 = rows[:, 0, 2 * TILES:2 * TILES + 6 * EXPERTS].rearrange("p (i e) -> p i e", e=EXPERTS)
        past, pastw = (buf.rearrange("p (n e) -> p n e", e=EXPERTS)
                       for buf in (h2T[:, 0, 0:512], wout_sb[:, 2:4, :].rearrange("p a n -> p (a n)")))
        ind, indw = (buf[:, :, :].rearrange("p t n -> p (t n)")[:, 0:TILES * EXPERTS]
                     .rearrange("p (t e) -> p t e", e=EXPERTS) for buf in (xr, x_sb))
        tabf = rows[:, :, 0:TILES]
        tabi = rows[:, :, TILES:2 * TILES].bitcast(I32)
        cumf = rows[:, 2, 2 * TILES:2 * TILES + EXPERTS]

        wq_raw = [buf.rearrange("p (k s n) -> p k s n", k=KD, s=3) for buf in (
            work[:, 0:3 * SEQ], wout_sb[:, 0:6, :].rearrange("p a n -> p (a n)"),
            YT[:, 0:3, :].rearrange("p a n -> p (a n)"), YT[:, 3:6, :].rearrange("p a n -> p (a n)"))]
        assert 3 * SEQ <= at_q
        sel_raw = rows[:, :, :].rearrange("p a n -> p (a n)").rearrange("p (c n) -> p c n", c=8)
        xs = YT[:, 0:1, :].rearrange("p a (b n) -> p (a b) n", b=2)
        xT_h, xT_l = (buf[:, :, :].rearrange("p k n -> p (k n)").rearrange("p (n k c) -> p n k c", n=2, k=KD)
                      for buf in (hC_h, hC_l))
        hh_flat = YT[:, 4:6, :].rearrange("p a n -> p (a n)")[:, 0:FC * P]
        gg = YT[:, 2:4, :].rearrange("p a n -> p (a n)")[:, 0:FF].rearrange("p (a n) -> p a n", a=2)
        ints = x2[:, 1, :].bitcast(I32)
        slot_all = ints[:, 0:BATCH * TOPK * TT].rearrange("p (b n) -> p b n", b=BATCH)
        stores_i = ints[:, 64:66]
        endi, nti, cumi = (rows[:, 3, 2 * TILES + i * EXPERTS:2 * TILES + (i + 1) * EXPERTS].bitcast(I32) for i in range(3))
        w13_raw, w2_raw = work[:, 0:W13], work[:, W13:W13 + W2]
        hh = hh_flat[:, 0:FF].rearrange("p (a n) -> p a n", a=2)
        hid_h, hid_l = (buf[:, :, 0:3 * P].rearrange("p a (c n) -> p a c n", c=3) for buf in (hT_h, hT_l))
        ysb = YT[:, 6, :].rearrange("p (b n) -> p b n", b=2)
        y_low = [buf.rearrange("p (t n) -> p t n", n=D) for buf in
                 [work[:, b * TT * D:(b + 1) * TT * D] for b in range(4)]
                 + [wout_sb[:, i * TT:(i + 1) * TT, :].rearrange("p t n -> p (t n)") for i in range(2)]
                 + [AT[:, :, :, :].rearrange("p a b n -> p (a b n)")[:, i * TT * D:(i + 1) * TT * D] for i in range(2)]]
        y_high = [work[:, 4 * TT * D:5 * TT * D].rearrange("p (t n) -> p t n", n=D), x_sb[:, :, :]] + [
            YT[:, i:i + 2, :].rearrange("p a (c n) -> p (a c) n", n=D) for i in (0, 2)]
        AHEAD = len(y_high)
        gates = x2[:, 3, 0:TOPK * BATCH * TT].rearrange("p (k b t) -> p k b t", k=TOPK, b=BATCH)
        xf = [xr[:, :, :], h2[:, :, :]]
        of = YT[:, 4:8, :].rearrange("p (a b) (c n) -> p a (b c) n", a=2, c=2)
        frow = hT[:, :, :].rearrange("p n (r d) -> p n r d", r=2)

        pA = pb("pA", [P, 2, SEQ])
        pS = pb("pS", [P, 2, SEQ])
        pY = pb("pY", [P, 2, SEQ])
        pM = pb("pM", [P, 2, SEQ])
        p13 = [pA, pS]
        pH, pXY = pY, pM

        s_cm = sem("s_cm")
        s_cst = sem("s_cst")
        s_wq = [sem(f"s_wq{g}") for g in range(GROUPS)]
        s_late = sem("s_late")
        s_zeros = sem("s_zeros")
        s_wqh, s_wql = sem("s_wqh"), sem("s_wql")
        s_hh, s_hl, s_hch, s_hcl = (sem("s_" + n) for n in ("hh", "hl", "hch", "hcl"))
        s_wh, s_wl = sem("s_wh"), sem("s_wl")
        s_pad = sem("s_pad")
        s_b0 = sem("s_b0")
        s_silu = sem("s_silu")
        s_modp = sem("s_modp")
        s_mod = sem("s_mod")
        s_modst = sem("s_modst")
        s_xin = sem("s_xin")
        s_bn1, s_mv1, s_ve1, s_rs1, s_xn = (sem("s_" + n) for n in ("bn1", "mv1", "ve1", "rs1", "xn"))
        s_pj = sem("s_pj")
        s_pe = sem("s_pe")
        s_hp = sem("s_hp")
        s_qk = sem("s_qk")
        s_sc, s_mk, s_mx, s_sb_, s_ex = ([sem(f"s_{n}{i}") for i in range(2)] for n in ("sc", "mk", "mx", "sb", "ex"))
        s_rs, s_rsd = sem("s_rs"), sem("s_rsd")
        s_at = sem("s_at")
        s_y = sem("s_y")
        s_ye = sem("s_ye")
        s_woh, s_wol = sem("s_woh"), sem("s_wol")
        s_dh, s_dl, s_yh, s_yl = (sem("s_" + n) for n in ("dh", "dl", "yh", "yl"))
        s_rt, s_dn, s_rd, s_bc, s_yn = (sem("s_" + n) for n in ("rt", "dn", "rd", "bc", "yn"))
        s_rows, s_xres, s_xrb = sem("s_rows"), sem("s_xres"), sem("s_xrb")
        s_brow, s_x2b = sem("s_brow"), sem("s_x2b")
        s_op, s_xg, s_x2, s_x2st = (sem("s_" + n) for n in ("op", "xg", "x2", "x2st"))
        s_bn2, s_mv2, s_ve2, s_rs2, s_xn2, s_hm, s_h2 = (
            sem("s_" + n) for n in ("bn2", "mv2", "ve2", "rs2", "xn2", "hm", "h2"))
        s_t2, s_t2e, s_lp, s_lg, s_v8, s_i8 = (sem("s_" + n) for n in ("t2", "t2e", "lp", "lg", "v8", "i8"))
        s_dx, s_ex8, s_su, s_rsu, s_gt, s_if, s_oh, s_ohs = (
            sem("s_" + n) for n in ("dx", "ex8", "su", "rsu", "gt", "if", "oh", "ohs"))
        s_px, s_ba, s_pb, s_pm, s_pf, s_sl, s_sla, s_disp = (
            sem("s_" + n) for n in ("px", "ba", "pb", "pm", "pf", "sl", "sla", "disp"))
        s_tab = sem("s_tab")
        s_zero = sem("s_zero")
        s_win, s_win2 = sem("s_win"), sem("s_win2")
        s_xh, s_hdh = sem("s_xh"), sem("s_hdh")
        s_tx, s_xT, s_m1, s_gl, s_mu, s_th, s_hT, s_m2, s_yv = (
            sem("s_" + n) for n in ("tx", "xT", "m1", "gl", "mu", "th", "hT", "m2", "yv"))
        s_xs, s_yst, s_xf, s_out = ([sem(f"s_{n}{i}") for i in range(2)] for n in ("xs", "yst", "xf", "out"))
        s_yg = [sem(f"s_yg{i}") for i in range(AHEAD)]
        s_plan = sem("s_plan")
        s_ylow, s_ul = sem("s_ylow"), sem("s_ul")
        s_fb, s_fc, s_f = (sem("s_" + n) for n in ("fb", "fc", "f"))

        block = ctx.enter_context(nc.Block())

        NMOD = 14
        NTAB = 17

        def of_group(w, g):
            return w.rearrange("p k (s n) -> p k s n", s=3)[:, :, :, g * 4 * DH:(g + 1) * 4 * DH]

        def slot_parts(n):
            at = n * SLOT
            return (big[:, at:at + W13], big[:, at + W13:at + 2 * W13],
                    big[:, at + 2 * W13:at + 2 * W13 + W2], big[:, at + 2 * W13 + W2:at + SLOT])

        def load_weights(eng, e, arrived):
            eng.dma_start(w13_raw, w13[bass.ds(e, 1), :, :].rearrange("a p n -> (a p) n")).then_inc(arrived, 16)
            src = w2[bass.ds(e, 1), :, :].rearrange("a f n -> (a f) n")
            eng.dma_start(w2_raw[:, 0:5 * D].rearrange("p (c n) -> p c n", c=5),
                          src[0:5 * P, :].rearrange("(c p) n -> p c n", p=P)).then_inc(arrived, 16)
            eng.dma_start(w2_raw[0:FTAIL, 5 * D:6 * D], src[5 * P:FF, :]).then_inc(arrived, 16)

        PIECES = (slice(0, 2 * TT * 32), slice(2 * TT * 32, 2 * UNITS * 32))

        def x_rows(b):
            return x[bass.ds(b * SEQ, SEQ), :].rearrange("(t p) d -> p t d", p=P)

        def over_batches(eng, body):
            body(0)
            body(1)
            with eng.Fori(2, BATCH - 1) as b:
                body(b)
            body(BATCH - 1)
            body(BATCH)
            body(BATCH + 1)

        def head(b):
            return not (isinstance(b, int) and b >= BATCH)

        def tail(b):
            return not (isinstance(b, int) and not 1 <= b <= BATCH)

        def late(b):
            return not (isinstance(b, int) and b < 2)

        def following(b):
            return not (isinstance(b, int) and b >= BATCH - 1)

        @block.sync
        def _(sp):
            sp.dma_start(cT_sb[:, :, :], cT).then_inc(s_cm, 16)
            sp.dma_start(x_sb[:, :, :], x_rows(0)).then_inc(s_xin, 16)
            sp.dma_start(YT[:, 0:6, :].rearrange("p (k a) n -> p k (a n)", k=KD), wmod).then_inc(s_cm, 16)
            for dst, src in ((cst[:, :], consts),
                             (bo_row[:, 0, :], b_out.partition_broadcast(BATCH)),
                             (bo_row[:, 1, :], ffn_bias.partition_broadcast(BATCH))):
                sp.dma_start(dst, src).then_inc(s_cst, 16)
            for g in range(GROUPS):
                if g == 2:
                    sp.wait_ge(s_modp, 2)
                for k in range(KD):
                    sp.dma_start(wq_raw[g][:, k, :, :], of_group(wqkv, g)[:, k, :, :]).then_inc(s_wq[g], 16)
            sp.wait_ge(s_wql, 2)
            for dst, src in ((sel_raw, sel), (rout_sb[:, :, :], router), (wout_sb[:, :, :], wout)):
                sp.dma_start(dst, src).then_inc(s_late, 16)
            sp.wait_ge(s_b0, 6)
            sp.dma_start(xs_dram[EXPERTS * CAP:SLOTS, :], zrow[:, :]).then_inc(s_zeros, 16)
            sp.wait_ge(s_mod, NMOD)
            sp.dma_start(rows_dram[:, 0:4, :], x2[0:BATCH, :, :]).then_inc(s_modst, 16)
            sp.dma_start(rows_dram[:, 4:6, :], h2[0:BATCH, 0:2, :]).then_inc(s_modst, 16)
            sp.wait_ge(s_modst, 32)

            FILL = TILES // BATCH * P

            def body(b):
                if head(b):
                    sp.dma_start(ys_dram[bass.ds(b * FILL, FILL), :].rearrange("(t p) d -> p t d", p=P),
                                 zrow[:, :].unsqueeze(1).broadcast_to([P, FILL // P, D])).then_inc(s_zeros, 16)
                if following(b):
                    sp.wait_ge(s_pj, job_x(b, KD - 1) + 1)
                    sp.dma_start(x_sb[:, :, :], x_rows(b + 1)).then_inc(s_xin, 16)
                if tail(b):
                    if some(b - 1):
                        sp.wait_ge(s_lp, b - 1)
                    sp.dma_start(xr[:, :, :], x_rows(b - 1)).then_inc(s_xres, 16)
                    if some(b - 1):
                        sp.wait_ge(s_h2, b - 1)
                    if isinstance(b, int) and b == 1:
                        sp.wait_ge(s_woh, 2)
                    sp.dma_start(rows[:, :, :],
                                 rows_dram[bass.ds(b - 1, 1), 0:4, :].rearrange("a r n -> (a r) n")
                                 .partition_broadcast(P)).then_inc(s_rows, 16)
                    if isinstance(b, int) and b == BATCH:
                        sp.wait_ge(s_pad, 1)
                        load_weights(sp, 0, s_win)
                    if isinstance(b, int) and b == 1:
                        sp.wait_ge(s_wol, 3)
                    if some(b - 1):
                        sp.wait_ge(s_x2b, b - 1)
                    sp.dma_start(bias_row,
                                 rows_dram[bass.ds(b - 1, 1), 5:6, :].rearrange("a r n -> (a r) n")
                                 .partition_broadcast(P)).then_inc(s_brow, 16)
                    if isinstance(b, int) and b == BATCH:
                        sp.wait_ge(s_wl, 2)
                        load_weights(sp, 1, s_win)
                    sp.wait_ge(s_x2b, b)
                    sp.dma_start(x2_dram[bass.ds((b - 1) * SEQ, SEQ), :].rearrange("(t p) d -> p t d", p=P),
                                 x2[:, :, :]).then_inc(s_x2st, 16)

            over_batches(sp, body)
            sp.wait_ge(s_tab, 1)
            for e in range(EXPERTS):
                end = sp.value_load(endi[0:1, e:e + 1], min_val=e * CAP, max_val=e * CAP + TOKENS)
                sp.dma_start(xs_dram[bass.ds(end, P), :], zrow[:, :]).then_inc(s_zero, 16)
            sp.wait_ge(s_disp, 16 * BATCH * TOPK * TT)
            sp.wait_ge(s_zero, 16 * EXPERTS)
            sp.wait_ge(s_zeros, 16 * (1 + BATCH))
            sp.wait_ge(s_tab, NTAB)
            sp.wait_ge(s_op, 2 * BATCH)

            def load_rows(j, n):
                row = sp.value_load(tabi[0:1, 0, bass.ds(j, 1)], min_val=0, max_val=EXPERTS * CAP)
                sp.dma_start(xs[:, n, :], xs_dram[bass.ds(row, P), :]).then_inc(s_xs[n], 16)

            load_rows(0, 0)
            load_rows(1, 1)
            with sp.Fori(0, TILES // 2 - 1) as pair:
                for n in range(2):
                    sp.wait_ge(s_tx, pair * 2 + (n + 1))
                    load_rows(pair * 2 + (n + 2), n)
            sp.wait_ge(s_plan, 1)
            sp.wait_ge(s_x2st, 16 * BATCH)
            def load_last(b, n):
                sp.dma_start(xf[n],
                             x2_dram[bass.ds(b * SEQ, SEQ), :].rearrange("(t p) d -> p t d", p=P)).then_inc(s_xf[n], 16)
                sp.dma_start(frow[:, n, 0:1, :],
                             rows_dram[bass.ds(b, 1), 4:5, :].rearrange("a r n -> (a r) n")
                             .partition_broadcast(P)).then_inc(s_xf[n], 16)

            def store_last(b, n):
                sp.wait_ge(s_f, b + 1)
                sp.dma_start(out[bass.ds(b * SEQ, SEQ), :].rearrange("(t p) d -> p t d", p=P),
                             of[:, n, :, :]).then_inc(s_out[n], 16)

            load_last(0, 0)
            load_last(1, 1)
            with sp.Fori(0, BATCH // 2 - 1) as pair:
                for n in range(2):
                    store_last(pair * 2 + n, n)
                    load_last(pair * 2 + (n + 2), n)
            for n in range(2):
                store_last(BATCH - 2 + n, n)
            for n in range(2):
                sp.wait_ge(s_out[n], 8 * BATCH)

        @block.gpsimd
        def _(pool):
            nc.gpsimd.memset(halfneg[:, :], -0.5).then_inc(s_b0, 1)

            def rstd(b, mv, r, s_mv, s_ve, s_rs_):
                needed = held(pool, TT * b + TT)
                pool.wait_ge(s_mv, 1)
                pool.wait_ge(s_mv, needed)
                nc.gpsimd.tensor_scalar(r[:, :], mv[:, :, 1], LN_EPS, None, ALU.add).then_inc(s_ve, 1)
                pool.wait_ge(s_ve, b + 1)
                nc.gpsimd.tensor_tensor(r[:, :], r[:, :], halfneg[:, :], ALU.pow).then_inc(s_rs_, 1)

            rstd(0, mv1, rstd1, s_mv1, s_ve1, s_rs1)
            nc.gpsimd.memset(zrow[:, :], 0.0).then_inc(s_b0, 1)
            nc.gpsimd.memset(AT[:, :, :, :], 0.0).then_inc(s_b0, 1)
            nc.gpsimd.memset(MG[:, :, :, :], 0.0).then_inc(s_b0, 1)
            nc.gpsimd.memset(rs[:, :, :], 0.0).then_inc(s_b0, 1)
            nc.gpsimd.memset(ones[:, :], 1.0).then_inc(s_b0, 1)

            def halve(dst, src, s):
                nc.gpsimd.tensor_tensor(dst[:, :, :], src[:, :, 0::2], src[:, :, 1::2], ALU.add).then_inc(s, 1)

            def halve_part(dst, lo, n, src, block, s):
                pairs = src[:, :, 0:64 * n].rearrange("p k (n r s) -> p k n r s", r=32, s=2)[:, :, :, 16 * block:16 * block + 16, :]
                nc.gpsimd.tensor_tensor(dst[:, :, lo:lo + 16 * n].rearrange("p k (n r) -> p k n r", r=16),
                                        pairs[:, :, :, :, 0], pairs[:, :, :, :, 1], ALU.add).then_inc(s, 1)

            def pool_h(b):
                pool.wait_ge(s_pe, job_x(b, KD - 1) + 1)
                if tail(b):
                    pool.wait_ge(s_pj, job(b - 1, GROUPS - 1, 6) + 1)
                halve(hP[0], hT, s_hp)
                halve_part(hC, 0, 8, hT, 0, s_hp)
                pool.wait_ge(s_hp, 8 * b + 1)
                halve(hP[1], hP[0], s_hp)
                halve_part(hC, P, 4, hP[0], 0, s_hp)
                pool.wait_ge(s_hp, 8 * b + 3)
                halve(hP[2], hP[1], s_hp)
                halve_part(hC, P + 64, 2, hP[1], 0, s_hp)
                pool.wait_ge(s_hp, 8 * b + 5)
                halve_part(hC, P + 96, 1, hP[2], 0, s_hp)
                halve_part(hC, P + 112, 1, hP[2], 0, s_hp)

            def pool_qk(b, g):
                step = b * GROUPS + g
                pool.wait_ge(s_pe, job(b, g, 3) + 1)
                if some(2 * step):
                    pool.wait_ge(s_sc[1], 2 * step)
                done = 12 * step
                halve(qP[0], qT, s_qk)
                halve(kP[0], kT, s_qk)
                halve_part(qC, 0, 8, qT, 1, s_qk)
                pool.wait_ge(s_qk, done + 2)
                halve(qP[1], qP[0], s_qk)
                halve(kP[1], kP[0], s_qk)
                halve_part(qC, P, 4, qP[0], 1, s_qk)
                pool.wait_ge(s_qk, done + 5)
                halve(qP[2], qP[1], s_qk)
                halve(kP[2], kP[1], s_qk)
                halve_part(qC, P + 64, 2, qP[1], 1, s_qk)
                pool.wait_ge(s_qk, done + 8)
                halve(kP[3], kP[2], s_qk)
                halve_part(qC, P + 96, 1, qP[2], 1, s_qk)
                halve_part(qC, P + 112, 1, qP[2], 1, s_qk)

            def residual(b):
                pool.wait_ge(s_xres, 16 * (b + 1))
                pool.wait_ge(s_rows, 16 * (b + 1))
                nc.gpsimd.tensor_tensor(xr[:, :, :], xr[:, :, :],
                                        rows[:, 1:2, :].broadcast_to([P, TT, D]), ALU.add).then_inc(s_xrb, 1)

            def modulate2(b):
                pool.wait_ge(s_xn2, b + 1)
                nc.gpsimd.tensor_tensor(h2[:, :, :], h2[:, :, :],
                                        rows[:, 2:3, :].broadcast_to([P, TT, D]), ALU.mult).then_inc(s_hm, 1)
                pool.wait_ge(s_hm, b + 1)
                nc.gpsimd.tensor_tensor(h2[:, :, :], h2[:, :, :],
                                        rows[:, 3:4, :].broadcast_to([P, TT, D]), ALU.add).then_inc(s_h2, 1)

            def dispatch(b):
                needed = held(pool, b + 1)
                pool.wait_ge(s_sl, 1)
                pool.wait_ge(s_sl, needed)
                pool.wait_ge(s_h2, b + 1)
                for k in range(TOPK):
                    for t in range(TT):
                        nc.gpsimd.indirect_dma_start(
                            xs_dram, bass.IndirectOffsetOnAxis(ap=slot[:, k, t:t + 1], axis=0),
                            h2[:, t, :], None).then_inc(s_disp, 16)

            def high(dst, raw, s):
                nc.gpsimd.tensor_tensor(dst, raw, zrow[:, 0:1].broadcast_to([P, dst.shape[-1]]),
                                        ALU.add).then_inc(s, 1)

            def low(dst, raw, high_, s):
                nc.gpsimd.tensor_tensor(dst, raw, f32(high_), ALU.subtract).then_inc(s, 1)

            def low_weights(e, n):
                w13_h, w13_l, w2_h, w2_l = slot_parts(n)
                pool.wait_ge(s_wh, 2 * e + 2)
                low(w13_l, w13_raw, w13_h, s_wl)
                low(w2_l, w2_raw, w2_h, s_wl)

            def body(b):
                if head(b):
                    if not tail(b):
                        pool_h(0)
                    pool_qk(b, 0)
                if late(b):
                    dispatch(b - 2)
                if tail(b):
                    residual(b - 1)
                if head(b):
                    pool_qk(b, 1)
                    if following(b):
                        rstd(b + 1, mv1, rstd1, s_mv1, s_ve1, s_rs1)
                    pool_qk(b, 2)
                elif tail(b):
                    pool.wait_ge(s_y, 2 * BATCH * GROUPS)
                    pool.wait_ge(s_qk, 12 * BATCH * GROUPS)
                    pool.wait_ge(s_xrb, BATCH)
                    nc.gpsimd.memset(w2_raw[FTAIL:P, 5 * D:6 * D], 0.0).then_inc(s_pad, 1)
                    pool.wait_ge(s_pad, 1)
                if tail(b):
                    rstd(b - 1, mv2, rstd2, s_mv2, s_ve2, s_rs2)
                    if head(b):
                        modulate2(b - 1)
                if head(b):
                    pool_qk(b, 3)
                    if following(b):
                        pool_h(b + 1)

            over_batches(pool, body)
            low_weights(1, 1)

            pool.wait_ge(s_tab, NTAB)

            def weights(e, n):
                w13_h, w13_l, w2_h, w2_l = slot_parts(n)
                last_use = pool.value_load(cumi[0:1, bass.ds(e - 2, 1)], min_val=1, max_val=TILES + 1)
                pool.wait_ge(s_m2, last_use)
                load_weights(pool, e, s_win2)
                pool.wait_ge(s_win2, 48 * e - 48)
                high(w13_h, w13_raw, s_wh)
                high(w2_h, w2_raw, s_wh)
                low_weights(e, n)

            with pool.Fori(1, EXPERTS // 2) as pair:
                weights(pair * 2, 0)
                weights(pair * 2 + 1, 1)
            pool.wait_ge(s_plan, 1)
            pool.wait_ge(s_wl, 2 * EXPERTS)
            stores = pool.value_load(stores_i[0:1, 1:2], min_val=16, max_val=8 * TILES)
            pool.wait_ge(s_yst[0], 16)
            for n in range(2):
                pool.wait_ge(s_yst[n], stores)

            def gather(dst, which, b, arrived):
                for t in range(TT):
                    nc.gpsimd.indirect_dma_start(
                        dst[:, t, :], None, ys_dram,
                        bass.IndirectOffsetOnAxis(ap=slot_all[:, b, which * TT + t:which * TT + t + 1], axis=0)
                    ).then_inc(arrived, 16)

            for b in range(BATCH):
                gather(y_low[b], 0, b, s_ylow)
            pool.wait_ge(s_ylow, 16 * BATCH * TT)
            for b in range(BATCH):
                nc.gpsimd.tensor_tensor(y_low[b], y_low[b], gates[:, 0, b, :].unsqueeze(2).broadcast_to([P, TT, D]),
                                        ALU.mult).then_inc(s_ul, 1)
            for n in range(2):
                pool.wait_ge(s_yst[n], 8 * TILES)
            for b in range(BATCH):
                if b >= AHEAD:
                    pool.wait_ge(s_fb, TT * (b - AHEAD + 1))
                gather(y_high[b % AHEAD], 1, b, s_yg[b % AHEAD])

        @block.scalar
        def _(act):
            act.wait_ge(s_cm, 32)
            nc.scalar.activation(sil[:, :, :], cT_sb[:, :, :], ACT.Exp, scale=-1.0).then_inc(s_silu, 1)

            def evac(dst, src, src_job):
                act.wait_ge(s_pj, src_job + 1)
                nc.scalar.activation(dst, src, ACT.Copy).then_inc(s_pe, 1)

            def copy(dst, src, s):
                nc.scalar.activation(dst, src, ACT.Copy).then_inc(s, 1)

            def evac_x(b):
                for k in range(KD):
                    act.wait_ge(s_pj, job_x(b, k) + 1)
                    if k == 0 and tail(b):
                        act.wait_ge(s_hp, 8 * b)
                    for dst, done in ((hT_h, s_hh), (hT, s_pe)):
                        nc.scalar.activation(dst[:, k, :], pA[:, k, :], ACT.Identity,
                                             bias=modT[:, k, bass.ds(b, 1)],
                                             scale=modT[:, KD + k, bass.ds(b, 1)]).then_inc(done, 1)

            def exps(step, level, e):
                act.wait_ge(s_sb_[level], 2 * step + e + 1)
                piece = PIECES[level]
                nc.scalar.activation(sm[:, e, piece], sm[:, e, piece], ACT.Exp).then_inc(s_ex[level], 1)

            def results(b, g):
                step = b * GROUPS + g
                for c in range(2):
                    act.wait_ge(s_y, 2 * step + c + 1)
                    if isinstance(step, int) and step == 0:
                        act.wait_ge(s_wql, GROUPS)
                    if some(2 * b):
                        act.wait_ge(s_yl, 2 * b)
                    nc.scalar.activation(YT[:, 2 * g + c, :], pY[:, c, :], ACT.Copy).then_inc(s_ye, 1)

            def high_results(b, half):
                act.wait_ge(s_yn, 8 * b + 16)
                if some(2 * b + half):
                    act.wait_ge(s_op, 2 * b + half)
                copy(YN_h[:, :, :], YT[:, :, half * SEQ // 2:(half + 1) * SEQ // 2], s_yh)

            act.wait_ge(s_mod, 2)
            evac_x(0)
            def high_wqkv(g):
                act.wait_ge(s_wq[g], 16 * KD)
                copy(of_group(wq_h, g), wq_raw[g], s_wqh)

            high_wqkv(0)
            high_wqkv(1)

            def heads(b, g):
                step = b * GROUPS + g
                if some(2 * step):
                    act.wait_ge(s_sc[0], 2 * step)
                if some(12 * step):
                    act.wait_ge(s_qk, 12 * step)
                for i in range(4):
                    dst = (qT if i < 2 else kT)[:, i % 2, :]
                    evac(dst, pA[:, (KD + 7 * g + i) % 2, :], job(b, g, i))
                if some(step):
                    exps(step - 1, 1, 0)
                    exps(step - 1, 1, 1)
                if g == 2 and tail(b):
                    high_results(b - 1, 1)
                if isinstance(step, int) and step == 0:
                    act.wait_ge(s_wql, 1)
                if some(2 * step - 2):
                    act.wait_ge(s_y, 2 * step - 2)
                if g == 0:
                    act.wait_ge(s_hp, 8 * b + 8)
                    copy(hC_h[:, :, :], hC[:, :, :], s_hch)
                for i in range(3):
                    evac(V[:, g % 2, 2 * i:2 * i + 2, :].rearrange("p u n -> p (u n)"),
                         pA[:, (KD + 7 * g + 4 + i) % 2, :], job(b, g, 4 + i))
                    if i == 0 and g == 2:
                        results(b, 0)
                    if i == (1 if g == GROUPS - 1 else 0):
                        exps(step, 0, 0)
                        exps(step, 0, 1)

            def body(b):
                for g in range(GROUPS):
                    if head(b):
                        heads(b, g)
                        if g == 0 and isinstance(b, int) and b == 0:
                            high_wqkv(2)
                            high_wqkv(3)
                        if g == GROUPS - 1 and following(b):
                            evac_x(b + 1)
                    elif g == 0 and tail(b):
                        exps(BATCH * GROUPS - 1, 1, 0)
                        exps(BATCH * GROUPS - 1, 1, 1)
                    if g == 0:
                        if late(b):
                            act.wait_ge(s_dx, 2 * (b - 1))
                            nc.scalar.activation(ex[:, :, :], ex[:, :, :], ACT.Exp).then_inc(s_ex8, 1)
                        if tail(b):
                            results(b - 1, GROUPS - 1)
                    elif head(b) and g > 1:
                        results(b, g - 1)
                    if g == 1 and tail(b):
                        high_results(b - 1, 0)
                    if g == 2 and tail(b) and not head(b):
                        high_results(b - 1, 1)
                        act.wait_ge(s_win, 48)
                        high_weights(0)
                    if g == 2 and isinstance(b, int) and b == 0:
                        act.wait_ge(s_late, 48)
                        copy(sel_p[:, :, :], sel_raw, s_woh)
                        copy(wout_h, wout_sb[:, :, :], s_woh)
                    if g == GROUPS - 1 and tail(b):
                        for k in range(KD):
                            act.wait_ge(s_t2, (b - 1) * KD + k + 1)
                            nc.scalar.activation(h2T[:, k, :], pM[:, k, :], ACT.Copy).then_inc(s_t2e, 1)

            def high_weights(n):
                w13_h, _, w2_h, _ = slot_parts(n)
                copy(w13_h, w13_raw, s_wh)
                copy(w2_h, w2_raw, s_wh)

            over_batches(act, body)
            act.wait_ge(s_win, 96)
            high_weights(1)

            def rows_high(j, n):
                act.wait_ge(s_tx, j + 1)
                if some(j - 1):
                    act.wait_ge(s_m1, j - 1)
                copy(xT_h[:, n, :, :], pXY[:, 0, 0:D].rearrange("p (k n) -> p k n", k=KD), s_xh)

            def store_rows(j, n):
                act.wait_ge(s_yv, j + 1)
                act.dma_start(ys_dram[bass.ds(j * P, P), :], ysb[:, n, :]).then_inc(s_yst[n], 16)

            def tile(j, n, more):
                if more:
                    rows_high(j + 1, 1 - n)
                act.wait_ge(s_m1, j + 1)
                if some(j):
                    act.wait_ge(s_mu, j)
                nc.scalar.activation(gg[:, :, :], p13[0][:, :, 0:FF // 2], ACT.Gelu).then_inc(s_gl, 1)
                act.wait_ge(s_th, j + 1)
                act.wait_ge(s_m2, j + 1)
                copy(hid_h, pH[:, :, 0:3 * P].rearrange("p a (c n) -> p a c n", c=3), s_hdh)
                if some(j):
                    store_rows(j - 1, 1 - n)

            act.wait_ge(s_zeros, 16 * (1 + BATCH))
            rows_high(0, 0)
            tile(0, 0, True)
            tile(1, 1, True)
            with act.Fori(1, TILES // 2 - 1) as pair:
                tile(pair * 2, 0, True)
                tile(pair * 2 + 1, 1, True)
            tile(TILES - 2, 0, True)
            tile(TILES - 1, 1, False)
            store_rows(TILES - 1, 1)

        @block.tensor
        def _(pe):
            mm = nc.tensor.matmul

            pe.wait_ge(s_cm, 32)
            pe.wait_ge(s_silu, 4)
            wm = YT[:, 0:6, :].rearrange("p (k a) n -> p k (a n)", k=KD)
            for n in range(2 * KD):
                for k in range(KD):
                    last = mm(pM[:, 0, n * BATCH:(n + 1) * BATCH], wm[:, k, n * P:(n + 1) * P], siT[:, k, :],
                              start=(k == 0), stop=(k == KD - 1))
            last.then_inc(s_modp, 1)
            pe.wait_ge(s_cst, 48)

            def transposed_x(b):
                pe.wait_ge(s_xn, b + 1)
                for k in range(KD):
                    n = job_x(b, k)
                    if some(n - 1):
                        pe.wait_ge(s_pe, n - 1)
                    for t in range(TT):
                        last = nc.tensor.transpose(pA[:, k, t * P:(t + 1) * P],
                                                   x_sb[:, t, k * P:(k + 1) * P], ident)
                    last.then_inc(s_pj, 1)

            def heads_qk(b, g):
                for i in range(4):
                    n = job(b, g, i)
                    pe.wait_ge(s_pe, n - 1)
                    if i == 0 and g == 0:
                        pe.wait_ge(s_hl, KD * b + KD)
                    if i == 0 and isinstance(b, int) and b == 0:
                        pe.wait_ge(s_wql, g + 1)
                    col = (i // 2) * INNER + (2 * g + i % 2) * P
                    for k in range(KD):
                        w = (wq_h[:, k, col:col + P], wq_l[:, k, col:col + P])
                        products_ = parts(w, (hT_h[:, k, :], hT_l[:, k, :]))
                        for m, (still, moving) in enumerate(products_):
                            last = mm(pA[:, (KD + 7 * g + i) % 2, :], still, moving,
                                      start=(k == 0 and m == 0), stop=(k == KD - 1 and m == 2))
                    last.then_inc(s_pj, 1)

            def heads_v(b, g, jobs):
                for i in jobs:
                    n = job(b, g, 4 + i)
                    pe.wait_ge(s_pe, n - 1)
                    if i == 2 and g == 0:
                        pe.wait_ge(s_hcl, b + 1)
                    col = 2 * INNER + g * 4 * DH
                    for u in (2 * i, 2 * i + 1):
                        at = u % TT * P
                        for k in range(KD):
                            rows_u = tuple(buf[:, k, at:at + P] for buf in ((hT_h, hT_l) if u < TT else (hC_h, hC_l)))
                            w = (wq_h[:, k, col:col + 4 * DH], wq_l[:, k, col:col + 4 * DH])
                            for m, (still, moving) in enumerate(parts(rows_u, w)):
                                last = mm(pA[:, (KD + 7 * g + 4 + i) % 2, (u % 2) * 4 * DH:(u % 2 + 1) * 4 * DH],
                                          still, moving, start=(k == 0 and m == 0), stop=(k == KD - 1 and m == 2))
                    last.then_inc(s_pj, 1)

            def block(e, u, c, quad, q, k):
                return mm(pS[quad * 32:(quad + 1) * 32, e, (2 * u + c) * 32:(2 * u + c + 1) * 32],
                          q, k, start=True, stop=True)

            def scores(b, g):
                step = b * GROUPS + g
                if isinstance(step, int) and step == 0:
                    pe.wait_ge(s_mod, NMOD)
                pe.wait_ge(s_pe, job(b, g, 3) + 1)
                if some(4 * step):
                    needed = held(pe, 4 * step)
                    pe.wait_ge(s_mk[1], 1)
                    pe.wait_ge(s_mk[1], needed)
                for e in range(2):
                    lo, hi = e * DH, (e + 1) * DH
                    for u in range(TT):
                        for c in range(2):
                            for quad in range(4):
                                a = u * P + quad * 32
                                last = block(e, u, c, quad, qT[lo:hi, c, a:a + 32], kT[lo:hi, c, a:a + 32])
                    last.then_inc(s_sc[0], 1)

            def pooled_scores(b, g):
                step = b * GROUPS + g
                pe.wait_ge(s_mk[0], 2 * step + 2)
                needed = held(pe, 12 * step + 12)
                pe.wait_ge(s_qk, 1)
                pe.wait_ge(s_qk, needed)
                for e in range(2):
                    lo, hi = e * DH, (e + 1) * DH
                    for c in range(2):
                        for u in (4, 5):
                            for quad in range(4):
                                q = qC[lo:hi, c, (u - 4) * P + quad * 32:(u - 4) * P + (quad + 1) * 32]
                                n, a = (0, quad * 64) if u == 4 else ((1, quad * 64), (1, quad * 64), (2, 0), (3, 0))[quad]
                                if (u, quad) == (5, 3):
                                    k = kP[n][lo:hi, c:c + 1, 0:16].broadcast_to([DH, 2, 16])
                                else:
                                    k = kP[n][lo:hi, c, a:a + 64].rearrange("p (n r) -> p n r", r=32)[:, :, 0:16]
                                last = block(e, u, c, quad, q, k)
                    last.then_inc(s_sc[1], 1)

            def products(b, g):
                step = b * GROUPS + g
                pe.wait_ge(s_at, 24 * step + 24)
                pe.wait_ge(s_pe, job(b, g, 6) + 1)
                if some(2 * step):
                    pe.wait_ge(s_ye, 2 * step)
                for c in range(2):
                    for u in range(UNITS):
                        for e in range(2):
                            val = V[:, g % 2, u, (2 * c + e) * DH:(2 * c + e + 1) * DH]
                            row = pY[e * DH:(e + 1) * DH, c, :]
                            if u < TT:
                                dst, src = row[:, u * P:(u + 1) * P], AT[:, e, 2 * u + c, :]
                            elif u == TT:
                                dst = row.rearrange("p (n r s) -> p n r s", r=32, s=2)[:, :, 16:32, 1]
                                src = AT[:, e, 2 * u + c, :]
                            else:
                                dst, src = row.rearrange("p (n s) -> p n s", s=4)[:, :, 3], MG[:, e, c, 0:P]
                            last = mm(dst, val, src, start=(u == 0), stop=(u == UNITS - 1),
                                      skip_group_check=True)
                    last.then_inc(s_y, 1)

            def sums_transposed(b):
                pe.wait_ge(s_rsd, b + 1)
                if some(b):
                    pe.wait_ge(s_lg, b)
                if some(b):
                    pe.wait_ge(s_pb, b)
                pe.wait_ge(s_ba, 5 * b + 1)
                for u in range(UNITS):
                    last = nc.tensor.transpose(pM[0:HEADS, u // 4, (u % 4) * P:(u % 4 + 1) * P],
                                               rs_done[:, u, :], ident)
                last.then_inc(s_rt, 1)

            def broadcast_sums(b):
                pe.wait_ge(s_rd, b + 1)
                pe.wait_ge(s_dl, b + 1)
                if isinstance(b, int) and b == 0:
                    pe.wait_ge(s_late, 48)
                    pe.wait_ge(s_woh, 2)
                    pe.wait_ge(s_wol, 3)
                for c in range(8):
                    pe.wait_ge(s_yn, 8 * b + c + 7)
                    mm(pM[:, c % 2, :], sel_p[:, c, :], den_h, start=True, stop=False)
                    mm(pM[:, c % 2, :], sel_p[:, c, :], den_l, start=False, stop=True).then_inc(s_bc, 1)

            def projection(b, half):
                pe.wait_ge(s_yl, 2 * b + half + 1)
                for t in range(2):
                    for c in range(8):
                        results_ = (YN_h[:, c, t * P:(t + 1) * P], YN_l[:, c, t * P:(t + 1) * P])
                        for m, (still, moving) in enumerate(parts(results_, (wout_h[:, c, :], wout_l[:, c, :]))):
                            last = mm(pM[:, half, t * D:(t + 1) * D], still, moving,
                                      start=(c == 0 and m == 0), stop=(c == 7 and m == 2))
                last.then_inc(s_op, 1)

            def transposed_h2(b):
                pe.wait_ge(s_h2, b + 1)
                pe.wait_ge(s_xg, 2 * b + 2)
                for k in range(KD):
                    for t in range(TT):
                        last = nc.tensor.transpose(pM[:, k, t * P:(t + 1) * P], h2[:, t, k * P:(k + 1) * P], ident)
                    last.then_inc(s_t2, 1)

            def route(b):
                pe.wait_ge(s_t2e, KD * b + KD)
                for t in range(TT):
                    for k in range(KD):
                        last = mm(pM[:, 0, t * EXPERTS:(t + 1) * EXPERTS], h2T[:, k, t * P:(t + 1) * P],
                                  rout_sb[:, k, :], start=(k == 0), stop=(k == KD - 1))
                last.then_inc(s_lp, 1)

            def count(b):
                pe.wait_ge(s_ohs, b + 1)
                flat = ohs[:, :, :].rearrange("p t e -> p (t e)")
                mm(pM[:, 1, 0:TT * EXPERTS], cst[:, C_TRI:C_TRI + P], flat, start=True, stop=True)
                mm(pM[:, 1, TT * EXPERTS:2 * TT * EXPERTS], ones[:, :], flat,
                   start=True, stop=True).then_inc(s_px, 1)

            transposed_x(0)
            for m in range(2):
                for k in range(KD):
                    last = mm(pS[0:BATCH, m, :], siT[:, k, :], wm[:, k, (m + 1) * SEQ:(m + 2) * SEQ],
                              start=(k == 0), stop=(k == KD - 1))
            last.then_inc(s_modp, 1)

            def body(b):
                for g in range(GROUPS):
                    if head(b):
                        heads_qk(b, g)
                    if g == 0 and late(b):
                        route(b - 2)
                    if g == 1 and tail(b):
                        sums_transposed(b - 1)
                    if g == 2 and tail(b):
                        projection(b - 1, 0)
                    if head(b):
                        heads_v(b, g, (0,))
                        scores(b, g)
                        heads_v(b, g, (1, 2))
                    if g == GROUPS - 1 and following(b):
                        transposed_x(b + 1)
                    if g == 0:
                        if tail(b):
                            products(b - 1, GROUPS - 1)
                        if late(b):
                            count(b - 2)
                    elif head(b):
                        products(b, g - 1)
                    if tail(b):
                        if g == 1:
                            broadcast_sums(b - 1)
                        if g == 2:
                            projection(b - 1, 1)
                        if g == 3:
                            transposed_h2(b - 1)
                    if head(b):
                        pooled_scores(b, g)

            over_batches(pe, body)

            pe.wait_ge(s_tab, NTAB)

            def transposed_rows(j, n, pair):
                pe.wait_ge(s_xs[n], 16 * pair + 16)
                if some(j):
                    pe.wait_ge(s_xT, j)
                for k in range(KD):
                    last = nc.tensor.transpose(pXY[:, 0, k * P:(k + 1) * P], xs[:, n, k * P:(k + 1) * P], ident)
                last.then_inc(s_tx, 1)

            def weights_of(j):
                return (pe.value_load(tabi[0:1, 2, bass.ds(j, 1)], min_val=2, max_val=2 * EXPERTS),
                        pe.value_load(tabi[0:1, 3, bass.ds(j, 1)], min_val=0, max_val=1))

            def up(j, n, arrived, at):
                pe.wait_ge(s_wl, arrived)
                pe.wait_ge(s_xT, j + 1)
                if some(j):
                    pe.wait_ge(s_mu, j)
                if some(j):
                    pe.wait_ge(s_gl, j)
                for half in range(4):
                    for k in range(KD):
                        w = tuple(big[:, bass.ds(at * SLOT + (part * W13 + k * FF2 + half * (FF // 2)), FF // 2)]
                                  for part in range(2))
                        for m, (still, moving) in enumerate(parts((xT_h[:, n, k, :], xT_l[:, n, k, :]), w)):
                            last = mm(p13[half // 2][:, half % 2, 0:FF // 2], still, moving,
                                      start=(k == 0 and m == 0), stop=(k == KD - 1 and m == 2))
                last.then_inc(s_m1, 1)

            def down(j):
                at = pe.value_load(tabi[0:1, 3, bass.ds(j, 1)], min_val=0, max_val=1)
                pe.wait_ge(s_hT, j + 1)
                if some(j):
                    pe.wait_ge(s_yv, j)
                for c in range(FC):
                    w = tuple(big[:, bass.ds(at * SLOT + (2 * W13 + part * W2 + c * D), D)] for part in range(2))
                    rows_c = (hid_h[:, c // 3, c % 3, :], hid_l[:, c // 3, c % 3, :])
                    for m, (still, moving) in enumerate(parts(rows_c, w)):
                        last = mm(pXY[:, 1, 0:D], still, moving,
                                  start=(c == 0 and m == 0), stop=(c == FC - 1 and m == 2))
                last.then_inc(s_m2, 1)

            pe.wait_ge(s_pad, 2)

            def hidden_transposed(j):
                pe.wait_ge(s_mu, j + 1)
                if some(j):
                    pe.wait_ge(s_hT, j)
                for c in range(FC):
                    last = nc.tensor.transpose(pH[:, c // 3, (c % 3) * P:(c % 3 + 1) * P],
                                               hh_flat[:, c * P:(c + 1) * P], ident)
                last.then_inc(s_th, 1)

            def tile(j, n, pair, first=False, more=True):
                arrived, at = weights_of(j)
                if not first:
                    down(j - 2)
                hidden_transposed(j - 1)
                if more:
                    transposed_rows(j + 1, 1 - n, pair + n)
                up(j, n, arrived, at)

            transposed_rows(0, 0, 0)
            transposed_rows(1, 1, 0)
            up(0, 0, *weights_of(0))
            tile(1, 1, 0, first=True)
            tile(2, 0, 1)
            tile(3, 1, 1)
            with pe.Fori(0, (TILES // 2 - 3) // 3) as turn:
                for i in range(2, 5):
                    tile(turn * 6 + 2 * i, 0, turn * 3 + i)
                    tile(turn * 6 + (2 * i + 1), 1, turn * 3 + i)
            tile(TILES - 2, 0, TILES // 2 - 1)
            tile(TILES - 1, 1, TILES // 2 - 1, more=False)
            down(TILES - 2)
            hidden_transposed(TILES - 1)
            down(TILES - 1)

        @block.vector
        def _(dve):
            v = nc.vector

            def stats(b, src, bn, mv, s_bn, s_mv):
                for t in range(TT):
                    v.bn_stats(bn[:, t, :], src[:, t, :]).then_inc(s_bn, 1)
                for t in range(TT):
                    needed = held(dve, TT * b + t + 1)
                    dve.wait_ge(s_bn, 1)
                    dve.wait_ge(s_bn, needed)
                    v.bn_aggr(mv[:, t, :], bn[:, t, :]).then_inc(s_mv, 1)

            def stats1(b):
                dve.wait_ge(s_xin, 16 * (b + 1))
                stats(b, x_sb, bn1, mv1, s_bn1, s_mv1)

            def normalise1(b):
                dve.wait_ge(s_rs1, b + 1)
                for t in range(TT):
                    last = v.tensor_scalar(x_sb[:, t, :], x_sb[:, t, :], mv1[:, t, 0:1], rstd1[:, t:t + 1],
                                           ALU.subtract, ALU.mult)
                last.then_inc(s_xn, 1)

            stats1(0)
            normalise1(0)
            dve.wait_ge(s_cst, 48)
            v.tensor_copy(base[:, TT, :], cst[:, C_CAP:C_CAP + 8]).then_inc(s_ba, 1)
            v.memset(mx[:, :, :], 0.0).then_inc(s_yn, 8)
            dve.wait_ge(s_silu, 1)
            v.tensor_scalar(sil[:, :, :], sil[:, :, :], 1.0, None, ALU.add).then_inc(s_silu, 1)
            dve.wait_ge(s_silu, 2)
            v.reciprocal(sil[:, :, :], sil[:, :, :]).then_inc(s_silu, 1)
            dve.wait_ge(s_silu, 3)
            v.tensor_tensor(siT[:, :, :], cT_sb[:, :, :], sil[:, :, :], ALU.mult).then_inc(s_silu, 1)
            dve.wait_ge(s_modp, 1)
            cols = pM[:, 0, 0:2 * KD * BATCH].rearrange("p (n b) -> p n b", b=BATCH)
            v.tensor_copy(modT[:, 0:KD, :], cols[:, 0:KD, :]).then_inc(s_mod, 1)
            v.tensor_scalar(modT[:, KD:2 * KD, :], cols[:, KD:2 * KD, :], 1.0, None, ALU.add).then_inc(s_mod, 1)

            def exponents(b, g, level):
                step = b * GROUPS + g
                pieces = (((0, 2 * TT, DH ** -0.5, C_M0),),
                          ((2 * TT, 2, DH ** -0.5 / 4, C_M1), (2 * TT + 2, 2, cst[:, C_SC2:C_SC2 + 1], C_M2)))[level]
                cols = slice(0, 2 * TT) if level == 0 else slice(2 * TT, 2 * UNITS)
                for e in range(2):
                    dve.wait_ge(s_sc[level], 2 * step + e + 1)
                    for lo, n, scale, mask in pieces:
                        piece = slice(lo * 32, (lo + n) * 32)
                        v.scalar_tensor_tensor(
                            sm[:, e, piece].rearrange("p (n r) -> p n r", r=32),
                            pS[:, e, piece].rearrange("p (n r) -> p n r", r=32), scale,
                            cst[:, mask:mask + 32].unsqueeze(1).broadcast_to([P, n, 32]),
                            ALU.mult, ALU.add).then_inc(s_mk[level], 1)
                    dve.wait_ge(s_mk[level], (level + 1) * (2 * step + e + 1))
                    tiles = sm[:, e, PIECES[level]].rearrange("p (n r) -> p n r", r=32)
                    v.tensor_reduce(mx[:, e, cols], tiles, AX.X, ALU.max).then_inc(s_mx[level], 1)
                    dve.wait_ge(s_mx[level], 2 * step + e + 1)
                    n = tiles.shape[1]
                    v.tensor_tensor(tiles, tiles, mx[:, e, cols].unsqueeze(2).broadcast_to([P, n, 32]),
                                    ALU.subtract).then_inc(s_sb_[level], 1)

            def weights(b, g, level):
                step = b * GROUPS + g
                units = slice(0, TT) if level == 0 else slice(TT, UNITS)
                for e in range(2):
                    dve.wait_ge(s_ex[level], 2 * step + e + 1)
                    tiles = sm[:, e, PIECES[level]].rearrange("p (u c r) -> p u c r", c=2, r=32)
                    v.tensor_reduce(rs[:, units, 4 * g + e:4 * g + e + 3:2], tiles, AX.X, ALU.add).then_inc(s_rs, 1)
                    if some(2 * step):
                        dve.wait_ge(s_y, 2 * step)
                    for quad in range(4):
                        q = slice(quad * 32, (quad + 1) * 32)
                        flat = sm[q, e, :].rearrange("p (n r) -> p n r", r=32)
                        if level == 0:
                            v.transpose(AT[q, e, 0:2 * TT, quad * 32:(quad + 1) * 32],
                                        flat[:, 0:2 * TT, :]).then_inc(s_at, 1)
                            continue
                        v.transpose(AT[q, e, 2 * TT:, quad * 32:(quad + 1) * 32],
                                    flat[:, 2 * TT:2 * TT + 2, :]).then_inc(s_at, 1)
                        if quad < 2:
                            dst = MG[q, e, :, quad * 64:(quad + 1) * 64].rearrange("p c (n r) -> p c n r", r=32)[:, :, :, 16:32]
                        elif quad == 2:
                            dst = MG[q, e, :, 0:P].rearrange("p c (n r s) -> p c n r s", r=32, s=2)[:, :, :, 16:32, 1]
                        else:
                            dst = MG[q, e, :, 64:64 + P].rearrange("p c (n r s) -> p c n r s", r=16, s=4)[:, :, :, :, 3]
                        v.transpose(dst, flat[:, 2 * TT + 2:, :]).then_inc(s_at, 1)

            def sums(b):
                dve.wait_ge(s_rt, b + 1)
                v.tensor_scalar(den[:, :], pM[0:HEADS, 0, :], SUM_EPS, None, ALU.add).then_inc(s_dn, 1)
                n = 5 * b + 1
                for s, lo, cnt in ((2, 0, 8), (4, P, 4), (8, P + 64, 2), (16, P + 96, 1)):
                    dve.wait_ge(s_dn, n)
                    to = den[:, :].rearrange("p (n r s) -> p n r s", r=32, s=s)[:, :, 16:32, s - 1]
                    v.tensor_tensor(to, to, pM[0:HEADS, 1, lo:lo + 16 * cnt].rearrange("p (n r) -> p n r", r=16),
                                    ALU.add).then_inc(s_dn, 1)
                    n += 1
                dve.wait_ge(s_dn, n)
                v.reciprocal(den[:, :], den[:, :]).then_inc(s_rd, 1)
                dve.wait_ge(s_rd, b + 1)
                v.tensor_copy(den_h[0:HEADS, :], den[:, :]).then_inc(s_dh, 1)
                dve.wait_ge(s_dh, b + 1)
                v.tensor_tensor(den_l[0:HEADS, :], den[:, :], f32(den_h)[0:HEADS, :], ALU.subtract).then_inc(s_dl, 1)

            def divide(b):
                dve.wait_ge(s_ye, 8 * b + 8)
                if some(2 * b):
                    dve.wait_ge(s_op, 2 * b)
                for c in range(8):
                    dve.wait_ge(s_bc, 8 * b + c + 1)
                    v.tensor_tensor(YT[:, c, :], pM[:, c % 2, :], YT[:, c, :], ALU.mult).then_inc(s_yn, 1)

            def low_results(b, half):
                dve.wait_ge(s_yh, 2 * b + half + 1)
                v.tensor_tensor(YN_l[:, :, :], YT[:, :, half * SEQ // 2:(half + 1) * SEQ // 2], f32(YN_h[:, :, :]),
                                ALU.subtract).then_inc(s_yl, 1)

            def residual(b):
                dve.wait_ge(s_xrb, b + 1)
                if some(16 * b):
                    dve.wait_ge(s_x2st, 16 * b)
                for half in range(2):
                    dve.wait_ge(s_op, 2 * b + half + 1)
                    v.tensor_tensor(x2[:, 2 * half:2 * half + 2, :],
                                    pM[:, half, :].rearrange("p (t n) -> p t n", n=D),
                                    rows[:, 0:1, :].broadcast_to([P, 2, D]), ALU.mult).then_inc(s_xg, 1)
                dve.wait_ge(s_xg, 2 * b + 2)
                v.tensor_tensor(x2[:, :, :], x2[:, :, :], xr[:, :, :], ALU.add).then_inc(s_x2, 1)
                dve.wait_ge(s_x2, b + 1)
                stats(b, x2, bn2, mv2, s_bn2, s_mv2)

            def normalise2(b):
                dve.wait_ge(s_rs2, b + 1)
                if some(16 * TOPK * TT * b):
                    dve.wait_ge(s_disp, 16 * TOPK * TT * b)
                for t in range(TT):
                    last = v.tensor_scalar(h2[:, t, :], x2[:, t, :], mv2[:, t, 0:1], rstd2[:, t:t + 1],
                                           ALU.subtract, ALU.mult)
                last.then_inc(s_xn2, 1)

            def modulate_last(b):
                dve.wait_ge(s_xn2, b + 1)
                v.tensor_tensor(h2[:, :, :], h2[:, :, :], rows[:, 2:3, :].broadcast_to([P, TT, D]),
                                ALU.mult).then_inc(s_hm, 1)
                dve.wait_ge(s_hm, b + 1)
                v.tensor_tensor(h2[:, :, :], h2[:, :, :], rows[:, 3:4, :].broadcast_to([P, TT, D]),
                                ALU.add).then_inc(s_h2, 1)

            def first_expert_low():
                w13_h, w13_l, w2_h, w2_l = slot_parts(0)
                dve.wait_ge(s_wh, 2)
                v.tensor_tensor(w13_l, w13_raw, f32(w13_h), ALU.subtract).then_inc(s_wl, 1)
                v.tensor_tensor(w2_l, w2_raw, f32(w2_h), ALU.subtract).then_inc(s_wl, 1)

            def keep_residual(b):
                dve.wait_ge(s_xn2, b + 1)
                dve.wait_ge(s_brow, 16 * (b + 1))
                v.tensor_tensor(x2[:, :, :], x2[:, :, :], bias_row.broadcast_to([P, TT, D]), ALU.add).then_inc(s_x2b, 1)

            def choose(b):
                dve.wait_ge(s_lp, b + 1)
                v.tensor_copy(lg[:, :, :], pM[:, 0, 0:TT * EXPERTS].rearrange("p (t e) -> p t e", e=EXPERTS)).then_inc(s_lg, 1)
                needed = held(dve, b + 1)
                dve.wait_ge(s_lg, 1)
                dve.wait_ge(s_lg, needed)
                for t in range(TT):
                    v.max(v8[:, t, :], lg[:, t, :]).then_inc(s_v8, 1)
                for t in range(TT):
                    needed = held(dve, TT * b + t + 1)
                    dve.wait_ge(s_v8, 1)
                    dve.wait_ge(s_v8, needed)
                    v.max_index(i8[:, t, :], v8[:, t, :], lg[:, t, :]).then_inc(s_i8, 1)
                top = v8[:, :, 0:1]
                v.tensor_tensor(ex[:, :, 0:EXPERTS], lg[:, :, :], top.broadcast_to([P, TT, EXPERTS]),
                                ALU.subtract).then_inc(s_dx, 1)
                v.tensor_tensor(ex[:, :, EXPERTS:], v8[:, :, 0:TOPK], top.broadcast_to([P, TT, TOPK]),
                                ALU.subtract).then_inc(s_dx, 1)
                dve.wait_ge(s_i8, TT * b + TT)
                v.tensor_copy(if8[:, :, :], i8[:, :, 0:TOPK]).then_inc(s_if, 1)
                dve.wait_ge(s_if, b + 1)
                for k in range(TOPK):
                    v.tensor_tensor(oh[:, k, :, :],
                                    cst[:, C_E8:C_E8 + 8].unsqueeze(1).broadcast_to([P, TT, EXPERTS]),
                                    if8[:, :, k:k + 1].broadcast_to([P, TT, EXPERTS]), ALU.is_equal).then_inc(s_oh, 1)
                dve.wait_ge(s_oh, TOPK * (b + 1))
                v.tensor_tensor(ohs[:, :, :], oh[:, 0, :, :], oh[:, 1, :, :], ALU.add).then_inc(s_ohs, 1)

            def slots(b):
                dve.wait_ge(s_ex8, b + 1)
                v.tensor_reduce(sume[:, :], ex[:, :, 0:EXPERTS], AX.X, ALU.add).then_inc(s_su, 1)
                dve.wait_ge(s_su, b + 1)
                v.reciprocal(rsum[:, :], sume[:, :]).then_inc(s_rsu, 1)
                dve.wait_ge(s_rsu, b + 1)
                v.tensor_tensor(gate_all[:, bass.ds(b, 1), :].rearrange("p a (t k) -> p (a t) k", k=TOPK),
                                ex[:, :, EXPERTS:], rsum[:, :].unsqueeze(2).broadcast_to([P, TT, TOPK]),
                                ALU.mult).then_inc(s_gt, 1)
                dve.wait_ge(s_px, b + 1)
                v.tensor_copy(base[:, 0, :], base[:, TT, :]).then_inc(s_ba, 1)
                for t in range(TT):
                    dve.wait_ge(s_ba, 5 * b + 2 + t)
                    tot = pM[:, 1, (TT + t) * EXPERTS:(TT + t + 1) * EXPERTS]
                    v.tensor_tensor(base[:, t + 1, :], tot, base[:, t, :], ALU.add).then_inc(s_ba, 1)
                dve.wait_ge(s_ba, 5 * b + 1 + TT)
                v.tensor_tensor(posb[:, :, :], pM[:, 1, 0:TT * EXPERTS].rearrange("p (t e) -> p t e", e=EXPERTS),
                                base[:, 0:TT, :], ALU.add).then_inc(s_pb, 1)
                dve.wait_ge(s_pb, b + 1)
                v.tensor_tensor(posm[:, :, :, :].rearrange("p k t e -> p k (t e)"),
                                oh[:, :, :, :].rearrange("p k t e -> p k (t e)"),
                                posb[:, :, :].rearrange("p t e -> p (t e)").unsqueeze(1)
                                .broadcast_to([P, TOPK, TT * EXPERTS]), ALU.mult).then_inc(s_pm, 1)
                dve.wait_ge(s_pm, b + 1)
                v.tensor_reduce(posf[:, :, :].rearrange("p k t -> p (k t)"),
                                posm[:, :, :, :].rearrange("p k t e -> p (k t) e"), AX.X, ALU.add).then_inc(s_pf, 1)
                dve.wait_ge(s_pf, b + 1)
                v.tensor_copy(slot[:, :, :], posf[:, :, :]).then_inc(s_sl, 1)
                v.tensor_copy(slotf_all[:, bass.ds(b, 1), :],
                              posf[:, :, :].rearrange("p k t -> p (k t)").unsqueeze(1)).then_inc(s_sla, 1)

            def split_inputs(b):
                for k in range(KD):
                    dve.wait_ge(s_hh, KD * b + k + 1)
                    dve.wait_ge(s_pe, job_x(b, k) + 1)
                    v.tensor_tensor(hT_l[:, k, :], hT[:, k, :], f32(hT_h[:, k, :]), ALU.subtract).then_inc(s_hl, 1)

            def split_pooled(b):
                dve.wait_ge(s_hch, b + 1)
                v.tensor_tensor(hC_l[:, :, :], hC[:, :, :], f32(hC_h[:, :, :]), ALU.subtract).then_inc(s_hcl, 1)

            def low_wqkv(g):
                dve.wait_ge(s_wqh, g + 1)
                for k in range(KD):
                    part_l, part_h = (of_group(w, g)[:, k, :, :] for w in (wq_l, wq_h))
                    op = v.tensor_tensor(part_l, wq_raw[g][:, k, :, :], f32(part_h), ALU.subtract)
                op.then_inc(s_wql, 1)

            split_inputs(0)
            low_wqkv(0)
            dve.wait_ge(s_modp, 2)
            n = 2
            for g_psum, r, bias in ((pS[0:BATCH, 0, 0:D], 0, 0), (pS[0:BATCH, 1, D:2 * D], 4, 1)):
                v.tensor_scalar(mtmp[:, 0, :], g_psum, 0.0, 2.0, ALU.is_ge, ALU.mult).then_inc(s_mod, 1)
                dve.wait_ge(s_mod, n + 1)
                v.scalar_tensor_tensor(mtmp[:, 1, :], mtmp[:, 0, :], -1.0, g_psum, ALU.add, ALU.mult).then_inc(s_mod, 1)
                dve.wait_ge(s_mod, n + 2)
                v.tensor_scalar(mtmp[:, 1, :], mtmp[:, 1, :], 0.25, None, ALU.max).then_inc(s_mod, 1)
                dve.wait_ge(s_mod, n + 3)
                v.scalar_tensor_tensor(mrow[r], mtmp[:, 0, :], -1.0, mtmp[:, 1, :],
                                       ALU.add, ALU.mult).then_inc(s_mod, 1)
                dve.wait_ge(s_mod, n + 4)
                v.tensor_tensor(mrow[r + 1], mrow[r], bo_row[:, bias, :], ALU.mult).then_inc(s_mod, 1)
                n += 5
            v.tensor_copy(mrow[3], pS[0:BATCH, 0, D:2 * D]).then_inc(s_mod, 1)
            v.tensor_scalar(mrow[2], pS[0:BATCH, 1, 0:D], 1.0, None, ALU.add).then_inc(s_mod, 1)
            low_wqkv(1)
            dve.wait_ge(s_b0, 6)

            def keep_sums(b):
                dve.wait_ge(s_rs, 16 * b + 16)
                v.tensor_copy(rs_done[:, :, :], rs[:, :, :]).then_inc(s_rsd, 1)

            def body(b):
                if tail(b):
                    keep_sums(b - 1)
                if head(b):
                    split_pooled(b)
                if late(b):
                    choose(b - 2)
                for g in range(GROUPS):
                    if g == 1 and tail(b):
                        sums(b - 1)
                    if g == 2 and tail(b):
                        low_results(b - 1, 1)
                        if not head(b):
                            first_expert_low()
                    if head(b):
                        exponents(b, g, 0)
                    if g == 1 and tail(b):
                        divide(b - 1)
                    if g == 3 and following(b):
                        split_inputs(b + 1)
                    if head(b):
                        weights(b, g, 0)
                    if g == 1 and tail(b):
                        low_results(b - 1, 0)
                    if g == 3 and tail(b):
                        keep_residual(b - 1)
                    if g == 0 and isinstance(b, int) and b == 0:
                        for group in range(2, GROUPS):
                            low_wqkv(group)
                    if g == 2 and isinstance(b, int) and b == 0:
                        for part in (den_h, den_l):
                            for half in range(2):
                                last = v.tensor_copy(part[:, half * D:(half + 1) * D], zrow[:, :])
                            last.then_inc(s_wol, 1)
                        dve.wait_ge(s_woh, 2)
                        v.tensor_tensor(wout_l, wout_sb[:, :, :], f32(wout_h), ALU.subtract).then_inc(s_wol, 1)
                    if g == 0 and late(b):
                        slots(b - 2)
                    if g == 1 and following(b):
                        stats1(b + 1)
                    if g == 2:
                        if following(b):
                            normalise1(b + 1)
                        if tail(b):
                            residual(b - 1)
                            normalise2(b - 1)
                            if not head(b):
                                modulate_last(b - 1)
                    if head(b):
                        exponents(b, g, 1)
                        weights(b, g, 1)

            over_batches(dve, body)

            tab = [0]

            def did(op):
                tab[0] += 1
                op.then_inc(s_tab, 1)
                dve.wait_ge(s_tab, tab[0])

            dve.wait_ge(s_ba, 5 * BATCH + 1)
            dve.wait_ge(s_x2st, 16 * BATCH)
            dve.wait_ge(s_sla, BATCH)
            count, ntile, shift, cum = (tb8[:, i, :] for i in range(4))
            did(v.tensor_copy(endi, base[:, TT, :]))
            did(v.tensor_tensor(count, base[:, TT, :], cst[:, C_CAP:C_CAP + 8], ALU.subtract))
            did(v.tensor_scalar(nti, count, P / 2 - 0.5, 1.0 / P, ALU.add, ALU.mult))
            did(v.tensor_copy(ntile, nti))
            did(v.tensor_tensor_scan(cumf, ones[:, 0:EXPERTS], ntile, 0.0, ALU.mult, ALU.add))
            did(v.tensor_scalar(cumi, cumf, 1.0, None, ALU.add))
            tile_no = cst[:, C_TILE:C_TILE + TILES]
            did(v.tensor_tensor(ind[:, :, :], tile_no.unsqueeze(2).broadcast_to([P, TILES, EXPERTS]),
                                cumf.unsqueeze(1).broadcast_to([P, TILES, EXPERTS]), ALU.is_ge))
            did(v.tensor_scalar(shift, ntile, -float(P), float(CAP), ALU.mult, ALU.add))
            did(v.tensor_tensor(indw[:, :, :], ind[:, :, :],
                                shift.unsqueeze(1).broadcast_to([P, TILES, EXPERTS]), ALU.mult))
            did(v.tensor_reduce(tabf[:, 0, :], indw[:, :, :], AX.X, ALU.add))
            did(v.tensor_reduce(tabf[:, 1, :], ind[:, :, :], AX.X, ALU.add))
            did(v.scalar_tensor_tensor(tabf[:, 2, :], tile_no, float(P), tabf[:, 0, :], ALU.mult, ALU.add))
            did(v.tensor_scalar(tabi[:, 0, :], tabf[:, 2, :], float(EXPERTS * CAP), None, ALU.min))
            did(v.tensor_scalar(tabf[:, 3, :], tabf[:, 1, :], EXPERTS - 1.0, None, ALU.min))
            did(v.tensor_copy(tabi[:, 1, :], tabf[:, 3, :]))
            did(v.tensor_scalar(tabi[:, 2, :], tabf[:, 3, :], 2.0, 2.0, ALU.mult, ALU.add))
            did(v.tensor_scalar(tabi[:, 3, :], tabi[:, 1, :], 1, None, ALU.bitwise_and))
            v.memset(tb8[:, 5, :], 0.0).then_inc(s_m2, 1)

            def result_rows():
                slots = slotf_all[:, :, :].rearrange("p b n -> p (b n)")
                N = BATCH * TOPK * TT
                did(v.tensor_scalar(tb8[:, 4, :], cst[:, C_CAP:C_CAP + 8], float(CAP), None, ALU.add))
                did(v.tensor_tensor(past, slots.unsqueeze(2).broadcast_to([P, N, EXPERTS]),
                                    tb8[:, 4:5, :].broadcast_to([P, N, EXPERTS]), ALU.is_ge))
                did(v.tensor_tensor(pastw, past, shift.unsqueeze(1).broadcast_to([P, N, EXPERTS]), ALU.mult))
                lower = x2[:, 0, 0:N]
                did(v.tensor_reduce(lower, pastw, AX.X, ALU.add))
                found = x2[:, 0, N:2 * N]
                did(v.tensor_tensor(found, slots, lower, ALU.subtract))
                by_rank = found.rearrange("p (b k t) -> p b k t", k=TOPK, t=TT)
                first, second = by_rank[:, :, 0, :], by_rank[:, :, 1, :]
                gate = gate_all[:, :, :].rearrange("p b (t k) -> p b t k", k=TOPK)
                scratch = x2[:, 2, 0:4 * BATCH * TT].rearrange("p (i b t) -> p i b t", i=4, b=BATCH)
                for which, least in ((0, ALU.min), (1, ALU.max)):
                    did(v.tensor_tensor(slot_all[:, :, which * TT:(which + 1) * TT], first, second, least))
                did(v.tensor_tensor(scratch[:, 0, :, :], first, second, ALU.is_lt))
                did(v.tensor_tensor(scratch[:, 1, :, :], second, first, ALU.is_lt))
                for which in range(2):
                    did(v.tensor_tensor(scratch[:, 2, :, :], scratch[:, which, :, :], gate[:, :, :, 0], ALU.mult))
                    did(v.tensor_tensor(scratch[:, 3, :, :], scratch[:, 1 - which, :, :], gate[:, :, :, 1], ALU.mult))
                    did(v.tensor_tensor(gates[:, which, :, :], scratch[:, 2, :, :], scratch[:, 3, :, :], ALU.add))
                did(v.tensor_scalar(stores_i[:, 0:1], cumf[:, EXPERTS - 2:EXPERTS - 1], 1.5, 0.5, ALU.add, ALU.mult))
                v.tensor_scalar(stores_i[:, 1:2], stores_i[:, 0:1], 16.0, None, ALU.mult).then_inc(s_plan, 1)

            def take_rows(j, n):
                dve.wait_ge(s_tx, j + 1)
                if some(j - 1):
                    dve.wait_ge(s_m1, j - 1)
                dve.wait_ge(s_xh, j + 1)
                v.tensor_tensor(xT_l[:, n, :, :], pXY[:, 0, 0:D].rearrange("p (k n) -> p k n", k=KD), f32(xT_h[:, n, :, :]),
                                ALU.subtract).then_inc(s_xT, 1)

            def hidden_low(j):
                dve.wait_ge(s_hdh, j + 1)
                v.tensor_tensor(hid_l, pH[:, :, 0:3 * P].rearrange("p a (c n) -> p a c n", c=3), f32(hid_h),
                                ALU.subtract).then_inc(s_hT, 1)

            def gated(j):
                dve.wait_ge(s_gl, j + 1)
                dve.wait_ge(s_m1, j + 1)
                if some(j):
                    dve.wait_ge(s_th, j)
                v.tensor_tensor(hh[:, :, :], p13[1][:, :, 0:FF // 2], gg[:, :, :], ALU.mult).then_inc(s_mu, 1)

            def result(j, n, pair):
                dve.wait_ge(s_m2, j + 2)
                if some(16 * pair):
                    dve.wait_ge(s_yst[n], 16 * pair)
                v.tensor_copy(ysb[:, n, :], pXY[:, 1, 0:D]).then_inc(s_yv, 1)

            v.memset(hh_flat[:, FF:FC * P], 0.0).then_inc(s_pad, 1)
            take_rows(0, 0)
            take_rows(1, 1)
            gated(0)
            hidden_low(0)
            result_rows()

            def tiles(pair):
                for i in range(2):
                    j = pair * 2 + (i + 1)
                    take_rows(j + 1, i)
                    gated(j)
                    result(pair * 2 + i, i, pair)
                    hidden_low(j)

            tiles(0)
            with dve.Fori(1, TILES // 2 - 1) as pair:
                tiles(pair)
            gated(TILES - 1)
            result(TILES - 2, 0, TILES // 2 - 1)
            hidden_low(TILES - 1)
            result(TILES - 1, 1, TILES // 2 - 1)

            def finish(b, n):
                dve.wait_ge(s_ul, b + 1)
                dve.wait_ge(s_yg[b % AHEAD], 16 * TT * (b // AHEAD + 1))
                if b >= 2:
                    dve.wait_ge(s_out[n], 16 * (b // 2))
                for t in range(TT):
                    v.scalar_tensor_tensor(of[:, n, t, :], y_high[b % AHEAD][:, t, :], gates[:, 1, b, t:t + 1],
                                           y_low[b][:, t, :], ALU.mult, ALU.add).then_inc(s_fb, 1)
                dve.wait_ge(s_fb, TT * (b + 1))
                dve.wait_ge(s_xf[n], 32 * (b // 2 + 1))
                v.tensor_tensor(of[:, n, :, :], of[:, n, :, :],
                                frow[:, n, 0:1, :].broadcast_to([P, TT, D]), ALU.mult).then_inc(s_fc, 1)
                dve.wait_ge(s_fc, b + 1)
                v.tensor_tensor(of[:, n, :, :], of[:, n, :, :], xf[n], ALU.add).then_inc(s_f, 1)

            for b in range(BATCH):
                finish(b, b % 2)


def constants():
    import numpy as np
    c = np.zeros((P, C_END), np.float32)
    r = np.arange(P)
    c[:, C_ID:C_ID + P] = np.eye(P)
    c[:, C_TRI:C_TRI + P] = r[:, None] < r[None, :]
    row, col = r[:, None] % 32, np.arange(32)[None, :]
    same = row // 16 == col // 16
    c[:, C_M0:C_M0 + 32] = np.where(same & (col <= row), 0.0, -1e30)
    c[:, C_M1:C_M1 + 32] = np.where(same, 0.0, -1e30)
    c[:, C_M2:C_M2 + 32] = np.where(np.where(r[:, None] < 96, same, col < 16), 0.0, -1e30)
    level = np.array([2, 2, 3, 4])[r // 32]
    c[:, C_SC2] = DH ** -0.5 / 4.0 ** level
    c[:, C_E8:C_E8 + 8] = np.arange(8)
    c[:, C_CAP:C_CAP + 8] = np.arange(8) * CAP
    c[:, C_TILE:C_TILE + TILES] = np.arange(TILES)
    sel = np.zeros((P, 8, P), np.float32)
    for h in range(HEADS):
        sel[h, h // 2, (h % 2) * DH:(h % 2 + 1) * DH] = 1.0
    return c, sel


def kernel(**inputs):
    import numpy as np
    import concourse.bacc as bacc
    from concourse.bass_utils import run_bass_kernel_spmd

    def chunks(w):
        k = w.shape[0] // P
        return np.ascontiguousarray(w.reshape(k, P, -1).transpose(1, 0, 2))

    a = {n: np.asarray(v) for n, v in inputs.items()}
    c, sel = constants()
    up = np.concatenate([a["L0_ffn_w1"], a["L0_ffn_v1"]], axis=2)
    arrays = {
        "x": np.ascontiguousarray(a["L0_attn_x"].reshape(TOKENS, D)),
        "cT": chunks(a["L0_c"].T),
        "wmod": chunks(a["L0_wmod"]),
        "wqkv": chunks(a["L0_attn_w_qkv"].T),
        "wout": chunks(a["L0_attn_w_out"].T),
        "b_out": a["L0_attn_b_out"],
        "router": chunks(a["L0_ffn_router_w"]),
        "w13": np.ascontiguousarray(up.reshape(EXPERTS, KD, P, FF2).transpose(0, 2, 1, 3).reshape(EXPERTS, P, KD * FF2)),
        "w2": np.ascontiguousarray(a["L0_ffn_w2"]),
        "ffn_bias": a["L0_ffn_bias"],
        "consts": c,
        "sel": sel,
    }
    nc = bacc.Bacc("TRN2", target_bir_lowering=False, num_devices=1)
    args = [nc.dram_tensor(n, v.shape, F32, kind="ExternalInput").ap() for n, v in arrays.items()]
    out = nc.dram_tensor("out", (TOKENS, D), F32, kind="ExternalOutput").ap()
    build(nc, *args, out)
    r = run_bass_kernel_spmd(nc, [arrays], core_ids=[0])
    return r.results[0]["out"].reshape(BATCH, SEQ, D)
```
